# Optimizing a Trainium2 kernel written in Bass

```python
import numpy as np
import jax
import jax.numpy as jnp

def _softmax(x, axis=-1):
    return jax.nn.softmax(x, axis=axis)

def _gelu(x):
    return jax.nn.gelu(x, approximate=True)

def _silu(x):
    return jax.nn.silu(x)

def _sigmoid(x):
    return jax.nn.sigmoid(x)

def _layernorm(x, axis=-1, eps=1e-05):
    m = jnp.mean(x, axis=axis, keepdims=True)
    v = jnp.var(x, axis=axis, keepdims=True)
    return (x - m) / jnp.sqrt(v + eps)

def _scatter_add(tgt, idx, src, axis=0):
    return tgt.at[idx].add(src)

def _segment_sum(src, seg, n):
    return jax.ops.segment_sum(src, seg, n)
kernel_name = 'mk_macaron_d2_jaxref_r8_1c7373'

def setup_inputs(seed: int=0):
    np.random.seed(seed)
    _w = jnp.asarray

    def _L0_attn_setup():
        import jax, jax.numpy as jnp
        import numpy as np
        DIM = 128
        HEADS = 16
        HEAD_DIM = DIM // HEADS
        DECAY = 0.95
        EPS = 1e-05

        def _decay_mask(S, dtype):
            idx = jnp.arange(S)
            diff = (idx[:, None] - idx[None, :]).astype(jnp.float32)
            mask = jnp.where(diff >= 0, jnp.exp(diff * np.log(DECAY)), 0.0)
            return mask.astype(dtype)
        key = jax.random.key(seed)
        ks = jax.random.split(key, 11)
        B, S, D = (2, 256, DIM)
        s = 1.0 / np.sqrt(D)
        inp = {'x': jax.random.normal(ks[0], (B, S, D), dtype=jnp.float32), 'Wq': jax.random.normal(ks[1], (D, D), dtype=jnp.float32) * s, 'bq': jnp.zeros((D,), jnp.float32), 'Wk': jax.random.normal(ks[2], (D, D), dtype=jnp.float32) * s, 'bk': jnp.zeros((D,), jnp.float32), 'Wv': jax.random.normal(ks[3], (D, D), dtype=jnp.float32) * s, 'bv': jnp.zeros((D,), jnp.float32), 'Wo': jax.random.normal(ks[4], (D, D), dtype=jnp.float32) * s, 'bo': jnp.zeros((D,), jnp.float32), 'gamma': jnp.ones((D,), jnp.float32), 'beta': jnp.zeros((D,), jnp.float32)}
        return inp
    _L0_attn_in = _L0_attn_setup()

    def _L0_ffn_setup():
        import jax, jax.numpy as jnp
        import numpy as np
        TOP_K = 2
        key = jax.random.key(seed)
        ks = jax.random.split(key, 5)
        B, S, H, I, E = (2, 256, 128, 448, 8)
        scale_h = 1.0 / np.sqrt(H)
        scale_i = 1.0 / np.sqrt(I)
        return {'hidden_states': jax.random.normal(ks[0], (B, S, H), dtype=jnp.float32), 'gate_w': jax.random.normal(ks[1], (E, H), dtype=jnp.float32) * scale_h, 'w1': jax.random.normal(ks[2], (E, H, I), dtype=jnp.float32) * scale_h, 'w3': jax.random.normal(ks[3], (E, H, I), dtype=jnp.float32) * scale_h, 'w2': jax.random.normal(ks[4], (E, I, H), dtype=jnp.float32) * scale_i}
    _L0_ffn_in = _L0_ffn_setup()

    def _L1_attn_setup():
        import jax, jax.numpy as jnp
        import numpy as np
        N_HEADS = 16
        key = jax.random.key(seed)
        ks = jax.random.split(key, 9)
        B, S, E = (2, 256, 128)
        s = 1.0 / np.sqrt(E)
        return {'x': jax.random.normal(ks[0], (B, S, E), jnp.float32), 'Wq': jax.random.normal(ks[1], (E, E), jnp.float32) * s, 'bq': jax.random.normal(ks[2], (E,), jnp.float32) * 0.01, 'Wk': jax.random.normal(ks[3], (E, E), jnp.float32) * s, 'bk': jax.random.normal(ks[4], (E,), jnp.float32) * 0.01, 'Wv': jax.random.normal(ks[5], (E, E), jnp.float32) * s, 'bv': jax.random.normal(ks[6], (E,), jnp.float32) * 0.01, 'Wo': jax.random.normal(ks[7], (E, E), jnp.float32) * s, 'bo': jax.random.normal(ks[8], (E,), jnp.float32) * 0.01}
    _L1_attn_in = _L1_attn_setup()

    def _L1_ffn_setup():
        import jax, jax.numpy as jnp
        import numpy as np
        DIM = 128

        def _reference_tuple_inner(x, W_r, W_k, W_v, mu_r, mu_k):
            B, T, C = x.shape
            x_prev = jnp.concatenate([jnp.zeros((B, 1, C), x.dtype), x[:, :-1, :]], axis=1)
            xr = mu_r * x + (1.0 - mu_r) * x_prev
            xk = mu_k * x + (1.0 - mu_k) * x_prev
            r = jax.nn.sigmoid(jnp.einsum('btc,dc->btd', xr, W_r))
            k = jnp.einsum('btc,dc->btd', xk, W_k)
            k_act = jnp.square(jax.nn.relu(k))
            out = r * jnp.einsum('btc,dc->btd', k_act, W_v)
            new_state = x[:, -1, :]
            return (out, new_state)
        key = jax.random.key(seed)
        ks = jax.random.split(key, 6)
        B, T, C = (8, 256, DIM)
        x = jax.random.normal(ks[0], (B, T, C), dtype=jnp.float32)
        s = 1.0 / np.sqrt(C)
        W_r = jax.random.uniform(ks[1], (C, C), jnp.float32, -s, s)
        W_k = jax.random.uniform(ks[2], (C, C), jnp.float32, -s, s)
        W_v = jax.random.uniform(ks[3], (C, C), jnp.float32, -s, s)
        mu_r = jax.random.uniform(ks[4], (C,), jnp.float32)
        mu_k = jax.random.uniform(ks[5], (C,), jnp.float32)
        return {'x': x, 'W_r': W_r, 'W_k': W_k, 'W_v': W_v, 'mu_r': mu_r, 'mu_k': mu_k}
    _L1_ffn_in = _L1_ffn_setup()
    _d = {'L0_attn_x': _L0_attn_in['x'], 'L0_attn_Wq': _L0_attn_in['Wq'], 'L0_attn_bq': _L0_attn_in['bq'], 'L0_attn_Wk': _L0_attn_in['Wk'], 'L0_attn_bk': _L0_attn_in['bk'], 'L0_attn_Wv': _L0_attn_in['Wv'], 'L0_attn_bv': _L0_attn_in['bv'], 'L0_attn_Wo': _L0_attn_in['Wo'], 'L0_attn_bo': _L0_attn_in['bo'], 'L0_attn_gamma': _L0_attn_in['gamma'], 'L0_attn_beta': _L0_attn_in['beta'], 'L0_ffn_gate_w': _L0_ffn_in['gate_w'], 'L0_ffn_w1': _L0_ffn_in['w1'], 'L0_ffn_w3': _L0_ffn_in['w3'], 'L0_ffn_w2': _L0_ffn_in['w2'], 'L1_attn_Wq': _L1_attn_in['Wq'], 'L1_attn_bq': _L1_attn_in['bq'], 'L1_attn_Wk': _L1_attn_in['Wk'], 'L1_attn_bk': _L1_attn_in['bk'], 'L1_attn_Wv': _L1_attn_in['Wv'], 'L1_attn_bv': _L1_attn_in['bv'], 'L1_attn_Wo': _L1_attn_in['Wo'], 'L1_attn_bo': _L1_attn_in['bo'], 'L1_ffn_W_r': _L1_ffn_in['W_r'], 'L1_ffn_W_k': _L1_ffn_in['W_k'], 'L1_ffn_W_v': _L1_ffn_in['W_v'], 'L1_ffn_mu_r': _L1_ffn_in['mu_r'], 'L1_ffn_mu_k': _L1_ffn_in['mu_k']}
    _x0 = _d['L0_attn_x']
    _d['L0_attn_x'] = jax.random.normal(jax.random.fold_in(jax.random.key(seed), 1), (8, 256, 128), dtype=_x0.dtype)
    del _x0
    return _d

def reference(L0_attn_x, L0_attn_Wq, L0_attn_bq, L0_attn_Wk, L0_attn_bk, L0_attn_Wv, L0_attn_bv, L0_attn_Wo, L0_attn_bo, L0_attn_gamma, L0_attn_beta, L0_ffn_gate_w, L0_ffn_w1, L0_ffn_w3, L0_ffn_w2, L1_attn_Wq, L1_attn_bq, L1_attn_Wk, L1_attn_bk, L1_attn_Wv, L1_attn_bv, L1_attn_Wo, L1_attn_bo, L1_ffn_W_r, L1_ffn_W_k, L1_ffn_W_v, L1_ffn_mu_r, L1_ffn_mu_k):

    def _L0_attn_ref(x, Wq, bq, Wk, bk, Wv, bv, Wo, bo, gamma, beta):
        import jax, jax.numpy as jnp
        import numpy as np
        DIM = 128
        HEADS = 16
        HEAD_DIM = DIM // HEADS
        DECAY = 0.95
        EPS = 1e-05

        def _decay_mask(S, dtype):
            idx = jnp.arange(S)
            diff = (idx[:, None] - idx[None, :]).astype(jnp.float32)
            mask = jnp.where(diff >= 0, jnp.exp(diff * np.log(DECAY)), 0.0)
            return mask.astype(dtype)
        B, S, D = x.shape
        H, hd = (HEADS, HEAD_DIM)

        def split_heads(y):
            return y.reshape(B, S, H, hd).transpose(0, 2, 1, 3)
        q = split_heads(x @ Wq + bq)
        k = split_heads(x @ Wk + bk)
        v = split_heads(x @ Wv + bv)
        mask = _decay_mask(S, x.dtype)
        scores = jnp.einsum('bhid,bhjd->bhij', q, k) * mask
        out = jnp.einsum('bhij,bhjd->bhid', scores, v)
        out = out.transpose(0, 2, 1, 3).reshape(B, S, D)
        out = out @ Wo + bo
        y = out.transpose(0, 2, 1)
        yg = y.reshape(B, H, hd, S)
        mu = yg.mean(axis=(2, 3), keepdims=True)
        var = yg.var(axis=(2, 3), keepdims=True)
        yn = (yg - mu) / jnp.sqrt(var + EPS)
        yn = yn.reshape(B, D, S) * gamma[None, :, None] + beta[None, :, None]
        return yn.transpose(0, 2, 1)

    def _L0_ffn_ref(hidden_states, gate_w, w1, w3, w2):
        import jax, jax.numpy as jnp
        import numpy as np
        TOP_K = 2
        orig_shape = hidden_states.shape
        H = orig_shape[-1]
        E = gate_w.shape[0]
        x = hidden_states.reshape(-1, H)
        T = x.shape[0]
        router_logits = x @ gate_w.T
        probs = jax.nn.softmax(router_logits, axis=-1)
        top_vals, top_idx = jax.lax.top_k(probs, TOP_K)
        top_vals = top_vals / jnp.sum(top_vals, axis=-1, keepdims=True)
        comb = jnp.zeros((T, E), dtype=x.dtype).at[jnp.arange(T)[:, None], top_idx].add(top_vals)
        g = jnp.einsum('th,ehi->eti', x, w1)
        u = jnp.einsum('th,ehi->eti', x, w3)
        h = jax.nn.silu(g) * u
        y = jnp.einsum('eti,eih->eth', h, w2)
        out = jnp.einsum('te,eth->th', comb, y)
        return out.reshape(orig_shape)

    def _L1_attn_ref(x, Wq, bq, Wk, bk, Wv, bv, Wo, bo):
        import jax, jax.numpy as jnp
        import numpy as np
        N_HEADS = 16
        B, S, E = x.shape
        H = N_HEADS
        D = E // H
        q = (x @ Wq.T + bq).reshape(B, S, H, D)
        k = (x @ Wk.T + bk).reshape(B, S, H, D)
        v = (x @ Wv.T + bv).reshape(B, S, H, D)
        scores = jnp.einsum('bqnd,bknd->bnqk', q, k) / jnp.sqrt(jnp.float32(D))
        attn = jax.nn.softmax(scores, axis=1)
        out = jnp.einsum('bnqk,bknd->bnqd', attn, v)
        out = out.transpose(0, 2, 1, 3).reshape(B, S, E)
        return out @ Wo.T + bo

    def _L1_ffn_ref(x, W_r, W_k, W_v, mu_r, mu_k):
        import jax, jax.numpy as jnp
        import numpy as np
        DIM = 128

        def _reference_tuple_inner(x, W_r, W_k, W_v, mu_r, mu_k):
            B, T, C = x.shape
            x_prev = jnp.concatenate([jnp.zeros((B, 1, C), x.dtype), x[:, :-1, :]], axis=1)
            xr = mu_r * x + (1.0 - mu_r) * x_prev
            xk = mu_k * x + (1.0 - mu_k) * x_prev
            r = jax.nn.sigmoid(jnp.einsum('btc,dc->btd', xr, W_r))
            k = jnp.einsum('btc,dc->btd', xk, W_k)
            k_act = jnp.square(jax.nn.relu(k))
            out = r * jnp.einsum('btc,dc->btd', k_act, W_v)
            new_state = x[:, -1, :]
            return (out, new_state)
        return _reference_tuple_inner(x, W_r, W_k, W_v, mu_r, mu_k)[0]
    x = L0_attn_x
    x = x + 0.5 * _L0_ffn_ref(_layernorm(x, axis=-1), L0_ffn_gate_w, L0_ffn_w1, L0_ffn_w3, L0_ffn_w2)
    x = x + _L0_attn_ref(_layernorm(x, axis=-1), L0_attn_Wq, L0_attn_bq, L0_attn_Wk, L0_attn_bk, L0_attn_Wv, L0_attn_bv, L0_attn_Wo, L0_attn_bo, L0_attn_gamma, L0_attn_beta)
    x = x + 0.5 * _L0_ffn_ref(_layernorm(x, axis=-1), L0_ffn_gate_w, L0_ffn_w1, L0_ffn_w3, L0_ffn_w2)
    x = x + 0.5 * _L1_ffn_ref(_layernorm(x, axis=-1), L1_ffn_W_r, L1_ffn_W_k, L1_ffn_W_v, L1_ffn_mu_r, L1_ffn_mu_k)
    x = x + _L1_attn_ref(_layernorm(x, axis=-1), L1_attn_Wq, L1_attn_bq, L1_attn_Wk, L1_attn_bk, L1_attn_Wv, L1_attn_bv, L1_attn_Wo, L1_attn_bo)
    x = x + 0.5 * _L1_ffn_ref(_layernorm(x, axis=-1), L1_ffn_W_r, L1_ffn_W_k, L1_ffn_W_v, L1_ffn_mu_r, L1_ffn_mu_k)
    return x

_drawn_inputs = setup_inputs


def setup_inputs(seed=0):
    import zlib

    import numpy as np

    out = dict(_drawn_inputs(seed))
    spreads = {'L0_attn_bq': (0.0, 0.1),
     'L0_attn_bk': (0.0, 0.1),
     'L0_attn_bv': (0.0, 0.1),
     'L0_attn_bo': (0.0, 0.1),
     'L0_attn_gamma': (1.0, 0.2),
     'L0_attn_beta': (0.0, 0.1)}
    factors = {'L1_attn_bq': 7.803,
     'L1_attn_bk': 7.586,
     'L1_attn_bo': 8.0,
     'L1_ffn_W_r': 6.918,
     'L1_ffn_mu_r': 8.0,
     'L1_ffn_mu_k': 2.716}
    for name, (base, spread) in spreads.items():
        noise = np.random.default_rng([zlib.crc32(name.encode()), seed]).standard_normal(out[name].shape)
        drawn = base * np.exp(spread * noise) if base else spread * noise
        out[name] = jnp.asarray(drawn.astype(out[name].dtype))
    for name, factor in factors.items():
        out[name] = (out[name] * factor).astype(out[name].dtype)
    return out
```

```python
from contextlib import ExitStack

import numpy as np

import concourse.bass as bass
from concourse import mybir

F32 = mybir.dt.float32
BF16 = mybir.dt.bfloat16
ALU = mybir.AluOpType
ACT = mybir.ActivationFunctionType
AX_X = mybir.AxisListType.X

P = 128
B, S, D = 8, 256, 128
TILES = B * S // P
TPB = S // P
H = 16
HD = D // H
HG = 4
HR = H // HG
MW = HD * HR
E = 8
I = 448
NCH = 4
IC = I // NCH
DECAY = 0.95
EPS = 1e-5
SCALE = float(HD) ** -0.5

C_IDENT, C_MASK, C_BLOCK, C_QDECAY, C_HEAD, C_KDECAY, C_RANK = 0, 128, 256, 384, 512, 528, 529
C_COLS = 537
V_NAMES = ["L0_attn_bq", "L0_attn_bk", "L0_attn_bo", "L0_attn_gamma", "L0_attn_beta",
           "L1_attn_bq", "L1_attn_bk", "L1_ffn_mu_r", "L1_ffn_mu_k"]
R_NAMES = ["L0_attn_bv", "L0_attn_bk", "L1_attn_bv", "L1_attn_bo"]
W_NAMES = ["L0_attn_Wq", "L0_attn_Wk", "L0_attn_Wv", "L0_attn_Wo"]
WT_NAMES = ["L1_attn_Wq", "L1_attn_Wk", "L1_attn_Wv", "L1_attn_Wo", "L1_ffn_W_r", "L1_ffn_W_k", "L1_ffn_W_v"]


def shape_constants():
    c = np.zeros((P, C_COLS), np.float32)
    p = np.arange(P)
    c[:, C_IDENT:C_IDENT + P] = np.eye(P)
    gap = p[None, :] - p[:, None]
    c[:, C_MASK:C_MASK + P] = np.where(gap >= 0, DECAY ** np.maximum(gap, 0), 0.0)
    c[:, C_BLOCK:C_BLOCK + P] = p[:, None] // HD == p[None, :] // HD
    c[:, C_QDECAY:C_QDECAY + P] = DECAY ** (p[None, :] + 1.0)
    c[:, C_HEAD:C_HEAD + H] = p[:, None] // HD == np.arange(H)[None, :]
    c[:, C_KDECAY] = DECAY ** (P - 1.0 - p)
    c[:, C_RANK:C_RANK + E] = E - np.arange(E)[None, :]
    return c


ds = bass.ds


def build(nc, io, out):
    with ExitStack() as ctx:
        def sb(name, shape, dt=F32):
            return ctx.enter_context(nc.sbuf_tensor(name, shape, dt))

        def sems(stage, names):
            return {n: ctx.enter_context(nc.semaphore(f"{stage}_{n}")) for n in names.split()}

        X = sb("X", [P, TILES, D])
        consts = sb("consts", [P, C_COLS])
        vecs = sb("vecs", [P, len(V_NAMES)])
        omu = sb("omu", [P, 2])
        rows = sb("rows", [1, len(R_NAMES), D])
        ones = sb("ones", [1, P])
        W = sb("W", [P, len(W_NAMES) + len(WT_NAMES), D])
        gateT = sb("gateT", [P, E])
        W1 = sb("W1", [P, E, I])
        W3 = sb("W3", [P, E, I])
        W2 = sb("W2", [IC, E, NCH, D])
        minus_i = sb("minus_i", [P, P], BF16)
        block_avg = sb("block_avg", [P, P])
        bn = sb("bn", [P, TILES, 6])
        mean = sb("mean", [P, TILES])
        nrm = sb("nrm", [P, 6, TILES])
        xn = sb("xn", [P, 2, TPB, D])
        xT = sb("xT", [P, 2, S + 1])
        qT = sb("qT", [P, 2, S])
        kT = sb("kT", [P, 2, S])
        Km = sb("Km", [P, 2, H, S])
        Vm = sb("Vm", [P, 2, TPB, H, MW])
        Vfull = sb("Vfull", [P, 2, D])
        Kd = sb("Kd", [P, 2, D])
        St = sb("St", [P, 2, D])
        qD = sb("qD", [P, 2, P])
        att = sb("att", [P, 2, HR, HG, P])
        amax = sb("amax", [P, P], BF16)
        den = sb("den", [P, 2, P])
        oT = sb("oT", [P, 2, S])
        gbn = sb("gbn", [P, 6])
        gst = sb("gst", [P, 10])
        yT = sb("yT", [P, S])
        XT = sb("XT", [P, TILES, P])
        LG = sb("LG", [P, TILES, E])
        comb = sb("comb", [P, TILES, E])
        rt = sb("rt", [P, 6, TILES, E])
        rs = sb("rs", [P, 8, TILES])
        xs = sb("xs", [P, 2, P])
        sg = sb("sg", [P, 2, I])
        hb = sb("hb", [P, 2, I])
        hT = sb("hT", [IC, 2, NCH, P])
        mixed = sb("mixed", [P, 2, 4, S])
        rgate = sb("rgate", [P, 2, S])
        kact = sb("kact", [P, 2, 2, S])
        rv = sb("rv", [P, 2, S])

        ps = ctx.enter_context(nc.psum_tensor("ps", [P, 8, 512], F32))

        ident = consts[:, C_IDENT:C_IDENT + P]
        decay_mask = consts[:, C_MASK:C_MASK + P]
        block_diag = consts[:, C_BLOCK:C_BLOCK + P]
        q_decay = consts[:, C_QDECAY:C_QDECAY + P]
        head_of = consts[:, C_HEAD:C_HEAD + H]
        k_decay = consts[:, C_KDECAY:C_KDECAY + 1]
        rank = consts[:, C_RANK:C_RANK + E]

        def vec(name):
            n = V_NAMES.index(name)
            return vecs[:, n:n + 1]

        def row(name):
            return rows[0:1, R_NAMES.index(name), :]

        def w(name):
            return W[:, (W_NAMES + WT_NAMES).index(name), :]

        ld = sems("load", "const x small w moe")
        su = sems("setup", "zeros consts stats")
        final = sems("final", "stored")
        nm = sems("norm", "mean var root newton ready")
        norm_names = "xn xnT xT x_done stats "
        MO = {n: sems(n, norm_names + "lg lgT xcopy rt exp comb xs gu sg h hT_ps hT y") for n in ("moe1", "moe2")}
        RW = {n: sems(n, norm_names + "shift mix rk rgate krelu kact v rv") for n in ("rwkv1", "rwkv2")}
        attn_names = norm_names + "qk_ps v_ps q k km vm sc at av oT yps "
        AT = {"attn0": sems("attn0", attn_names + "vfull kd qd st_ps st ymv ym yvar gm_ps gm dev gv_ps gv groot grs ab yn ynT"),
              "attn1": sems("attn1", attn_names + "mx sub ex den rden at_pool")}

        def batches(eng, front, heavy, tail):
            def turn(i):
                front(i * 2 + 2, 0)
                heavy(i * 2 + 1, 1)
                tail(i * 2, 0)
                front(i * 2 + 3, 1)
                heavy(i * 2 + 2, 0)
                tail(i * 2 + 1, 1)
            front(0, 0)
            front(1, 1)
            heavy(0, 0)
            turn(0)
            with eng.Fori(1, B // 2 - 1) as i:
                turn(i)
            heavy(B - 1, 1)
            tail(B - 2, 0)
            tail(B - 1, 1)

        def nothing(b, par):
            pass

        def after(eng, sem, value):
            if not isinstance(value, int) or value > 0:
                eng.wait_ge(sem, value)

        def two_before(eng, sem, b, each=1):
            after(eng, sem, (b - 1) * each)

        def norm_vector(dve, turn, before):
            dve.wait_ge(*before)
            nc.vector.tensor_tensor(nrm[:, 3, :], bn[:, :, 1], bn[:, :, 4], ALU.add).then_inc(nm["mean"], 1)
            nc.vector.tensor_tensor(nrm[:, 4, :], bn[:, :, 1], bn[:, :, 4], ALU.subtract).then_inc(nm["mean"], 1)
            nc.vector.tensor_tensor(nrm[:, 5, :], bn[:, :, 2], bn[:, :, 5], ALU.add).then_inc(nm["mean"], 1)
            dve.wait_ge(nm["mean"], turn * 6 + 3)
            nc.vector.tensor_scalar(mean[:, :], nrm[:, 3, :], 0.5, None, ALU.mult).then_inc(nm["mean"], 1)
            nc.vector.scalar_tensor_tensor(nrm[:, 4, :], nrm[:, 4, :], 0.25, nrm[:, 4, :], ALU.mult,
                                           ALU.mult).then_inc(nm["mean"], 1)
            nc.vector.tensor_scalar(nrm[:, 5, :], nrm[:, 5, :], 1.0 / D, EPS, ALU.mult, ALU.add).then_inc(nm["mean"], 1)
            dve.wait_ge(nm["mean"], turn * 6 + 6)
            nc.vector.tensor_tensor(nrm[:, 0, :], nrm[:, 4, :], nrm[:, 5, :], ALU.add).then_inc(nm["var"], 1)
            dve.wait_ge(nm["root"], turn + 1)
            nc.vector.reciprocal(nrm[:, 2, :], nrm[:, 1, :]).then_inc(nm["newton"], 1)
            dve.wait_ge(nm["newton"], turn * 4 + 1)
            nc.vector.tensor_tensor(nrm[:, 3, :], nrm[:, 2, :], nrm[:, 2, :], ALU.mult).then_inc(nm["newton"], 1)
            dve.wait_ge(nm["newton"], turn * 4 + 2)
            nc.vector.tensor_tensor(nrm[:, 3, :], nrm[:, 3, :], nrm[:, 0, :], ALU.mult).then_inc(nm["newton"], 1)
            dve.wait_ge(nm["newton"], turn * 4 + 3)
            nc.vector.tensor_scalar(nrm[:, 3, :], nrm[:, 3, :], -0.5, 1.5, ALU.mult, ALU.add).then_inc(nm["newton"], 1)
            dve.wait_ge(nm["newton"], turn * 4 + 4)
            nc.vector.tensor_tensor(nrm[:, 2, :], nrm[:, 2, :], nrm[:, 3, :], ALU.mult).then_inc(nm["ready"], 1)
            dve.wait_ge(nm["ready"], turn + 1)

        def norm_scalar(act, turn):
            act.wait_ge(nm["var"], turn + 1)
            nc.scalar.activation(nrm[:, 1, :], nrm[:, 0, :], ACT.Sqrt).then_inc(nm["root"], 1)

        def front_vector(dve, s, b, par):
            two_before(dve, s["xnT"], b)
            for j in range(TPB):
                t = b * TPB + j
                nc.vector.tensor_scalar(xn[:, par, j, :], X[:, t, :], mean[:, ds(t, 1)], nrm[:, 2, ds(t, 1)],
                                        ALU.subtract, ALU.mult).then_inc(s["xn"], 1)

        def front_tensor(pe, s, b, par):
            pe.wait_ge(s["xn"], b * TPB + TPB)
            after(pe, s["xT"], b)
            nc.tensor.transpose(ps[:, 0, 0:P], xn[:, par, 0, :], ident)
            nc.tensor.transpose(ps[:, 0, P:S], xn[:, par, 1, :], ident).then_inc(s["xnT"], 1)

        def front_scalar(act, s, b, par):
            act.wait_ge(s["xnT"], b + 1)
            nc.scalar.copy(xT[:, par, 1:S + 1], ps[:, 0, 0:S]).then_inc(s["xT"], 1)

        def tile_stats(dve, s, t, updates):
            if updates is not None:
                dve.wait_ge(s["x_done"], updates)
            nc.vector.bn_stats(bn[:, t, :], X[:, t, :]).then_inc(s["stats"], 1)

        def update_batch(dve, s, b, src, stats=True):
            tiles = X[:, ds(b * TPB, TPB), :]
            nc.vector.tensor_tensor(tiles, tiles, src.rearrange("p (j d) -> p j d", j=TPB),
                                    ALU.add).then_inc(s["x_done"], 1)
            if stats:
                for j in range(TPB):
                    tile_stats(dve, s, b * TPB + j, b + 1)

        ROUTE_DIFF = 12

        def moe_front_vector(dve, s, turn, before):
            norm_vector(dve, turn, before)

            def tail(b, par):
                dve.wait_ge(s["lg"], b + 1)
                nc.vector.tensor_copy(LG[:, ds(b * TPB, TPB), :],
                                      ps[:, 2 + par, 0:TPB * E].rearrange("p (j e) -> p j e", j=TPB)).then_inc(s["lgT"], 1)
            batches(dve, lambda b, par: front_vector(dve, s, b, par), nothing, tail)

            dve.wait_ge(s["lgT"], B)
            step = [0]

            def link(ins):
                step[0] += 1
                ins.then_inc(s["rt"], 1)
                dve.wait_ge(s["rt"], step[0])

            def wide(n):
                return rs[:, n, :].unsqueeze(2).broadcast_to([P, TILES, E])
            ranks = rank.unsqueeze(1).broadcast_to([P, TILES, E])
            v = nc.vector
            for k, src in ((0, LG[:, :, :]), (1, rt[:, 2])):
                link(v.tensor_reduce(rs[:, k, :], src, AX_X, ALU.max))
                link(v.tensor_tensor(rt[:, 0], src, wide(k), ALU.is_equal))
                link(v.tensor_tensor(rt[:, 1], rt[:, 0], ranks, ALU.mult))
                link(v.tensor_reduce(rs[:, 2, :], rt[:, 1], AX_X, ALU.max))
                link(v.tensor_tensor(rt[:, 3 + k], rt[:, 1], wide(2), ALU.is_equal))
                if k == 0:
                    link(v.scalar_tensor_tensor(rt[:, 2], rt[:, 3], -3.0e38, LG[:, :, :], ALU.mult, ALU.add))
            link(v.tensor_tensor(rs[:, 3, :], rs[:, 1, :], rs[:, 0, :], ALU.subtract))
            assert step[0] == ROUTE_DIFF
            dve.wait_ge(s["exp"], 1)
            link(v.tensor_scalar(rs[:, 5, :], rs[:, 4, :], 1.0, None, ALU.add))
            link(v.reciprocal(rs[:, 6, :], rs[:, 5, :]))
            link(v.tensor_tensor(rs[:, 7, :], rs[:, 6, :], rs[:, 4, :], ALU.mult))
            link(v.tensor_tensor(rt[:, 0], rt[:, 3], wide(6), ALU.mult))
            link(v.tensor_tensor(rt[:, 1], rt[:, 4], wide(7), ALU.mult))
            v.tensor_tensor(comb[:, :, :], rt[:, 0], rt[:, 1], ALU.add).then_inc(s["comb"], 1)
            dve.wait_ge(s["comb"], 1)

        def moe_front_scalar(act, s, turn):
            norm_scalar(act, turn)

            def front(b, par):
                two_before(act, s["lg"], b)
                two_before(act, s["xcopy"], b)
                front_scalar(act, s, b, par)
            batches(act, front, nothing, nothing)
            act.wait_ge(s["rt"], ROUTE_DIFF)
            nc.scalar.activation(rs[:, 4, :], rs[:, 3, :], ACT.Exp).then_inc(s["exp"], 1)

        def moe_front_tensor(pe, s, before):
            pe.wait_ge(*before)

            def heavy(b, par):
                pe.wait_ge(s["xT"], b + 1)
                two_before(pe, s["lgT"], b)
                nc.tensor.matmul(ps[:, 2 + par, 0:E], xT[:, par, 1:P + 1], gateT[:, :], start=True, stop=True)
                nc.tensor.matmul(ps[:, 2 + par, E:2 * E], xT[:, par, P + 1:S + 1], gateT[:, :],
                                 start=True, stop=True).then_inc(s["lg"], 1)
            batches(pe, lambda b, par: front_tensor(pe, s, b, par), heavy, nothing)

        def moe_front_pool(pool, s):
            def heavy(b, par):
                pool.wait_ge(s["xT"], b + 1)
                nc.gpsimd.tensor_copy(XT[:, ds(b * TPB, TPB), :],
                                      xT[:, par, 1:S + 1].rearrange("p (j d) -> p j d", j=TPB)).then_inc(s["xcopy"], 1)
            batches(pool, nothing, heavy, nothing)

        STEPS = 2 * E

        def turns(eng, body, drain):
            body(0, True)
            with eng.Fori(1, TILES // 2) as i:
                body(i, False)
            drain(TILES // 2)

        def moe_pool(pool, s):
            pool.wait_ge(s["xcopy"], B)

            def body(i, first):
                for t in range(2):
                    if not first:
                        pool.wait_ge(s["gu"], i * STEPS + (t - 1) * E)
                    nc.gpsimd.tensor_copy(xs[:, t, :], XT[:, i * 2 + t, :]).then_inc(s["xs"], 1)
            turns(pool, body, lambda i: None)

        def moe_tensor(pe, s):
            pe.wait_ge(s["lgT"], B)

            def gate_up(i, n, first):
                e, par = n % E, n % 2
                if e == 0:
                    pe.wait_ge(s["xs"], i * 2 + n // E + 1)
                if not (first and n < 2):
                    pe.wait_ge(s["h"], i * STEPS + n - 1)
                lhs = xs[:, n // E, :]
                nc.tensor.matmul(ps[:, 2 * par, 0:I], lhs, W1[:, e, :], start=True, stop=True)
                nc.tensor.matmul(ps[:, 2 * par + 1, 0:I], lhs, W3[:, e, :], start=True,
                                 stop=True).then_inc(s["gu"], 1)

            def turn_hidden(i, n, first):
                par = n % 2
                pe.wait_ge(s["h"], i * STEPS + n + 1)
                if not first:
                    pe.wait_ge(s["hT"], i * STEPS + n - 1)
                for c in range(NCH):
                    last = nc.tensor.transpose(ps[0:IC, 4 + par, c * P:(c + 1) * P],
                                               hb[:, par, c * IC:(c + 1) * IC], ident)
                last.then_inc(s["hT_ps"], 1)

            def down(i, n, first):
                par, e, t = n % 2, n % E, n // E % 2
                pe.wait_ge(s["hT"], i * STEPS + n + 1)
                if e == 0 and not first:
                    pe.wait_ge(s["x_done"], i * 2 + n // E - 1)
                for c in range(NCH):
                    last = nc.tensor.matmul(ps[:, 6 + t, 0:D], hT[:, par, c, :], W2[:, e, c, :],
                                            start=(e == 0 and c == 0), stop=(e == E - 1 and c == NCH - 1))
                last.then_inc(s["y"], 1)

            def body(i, first):
                for n in range(STEPS):
                    gate_up(i, n, first)
                    if not (first and n < 1):
                        turn_hidden(i, n - 1, first and n < 3)
                    if not (first and n < 2):
                        down(i, n - 2, first)

            def drain(i):
                turn_hidden(i, -1, False)
                down(i, -2, False)
                down(i, -1, False)
            turns(pe, body, drain)

        def moe_scalar(act, s):
            def silu(i, n, first):
                par = n % 2
                act.wait_ge(s["gu"], i * STEPS + n + 1)
                if not (first and n < 2):
                    act.wait_ge(s["h"], i * STEPS + n - 1)
                nc.scalar.activation(sg[:, par, :], ps[:, 2 * par, 0:I], ACT.Silu).then_inc(s["sg"], 1)

            def evict(i, n, first):
                par = n % 2
                act.wait_ge(s["hT_ps"], i * STEPS + n + 1)
                if not first:
                    act.wait_ge(s["y"], i * STEPS + n - 1)
                nc.scalar.copy(hT[:, par].rearrange("p c t -> p (c t)"), ps[0:IC, 4 + par, :]).then_inc(s["hT"], 1)

            def body(i, first):
                for n in range(STEPS):
                    silu(i, n, first)
                    if not (first and n < 1):
                        evict(i, n - 1, first and n < 3)
            turns(act, body, lambda i: evict(i, -1, False))

        def moe_vector(dve, s):
            def hidden(i, n, first):
                e, par, t = n % E, n % 2, n // E
                dve.wait_ge(s["sg"], i * STEPS + n + 1)
                if not (first and n < 2):
                    dve.wait_ge(s["hT_ps"], i * STEPS + n - 1)
                nc.vector.scalar_tensor_tensor(hb[:, par, :], sg[:, par, :], comb[:, i * 2 + t, e:e + 1],
                                               ps[:, 2 * par + 1, 0:I], ALU.mult, ALU.mult).then_inc(s["h"], 1)

            def update(tile, t):
                dve.wait_ge(s["y"], tile * E + E)
                nc.vector.scalar_tensor_tensor(X[:, tile, :], ps[:, 6 + t, 0:D], 0.5, X[:, tile, :],
                                               ALU.mult, ALU.add).then_inc(s["x_done"], 1)
                tile_stats(dve, s, tile, tile + 1)

            def body(i, first):
                for n in range(STEPS):
                    hidden(i, n, first)
                    if n == 2 and not first:
                        update(i * 2 - 1, 1)
                    if n == E + 2:
                        update(i * 2, 0)
            turns(dve, body, lambda i: update(i * 2 - 1, 1))

        def rwkv_vector(dve, s, turn, before, stats):
            norm_vector(dve, turn, before)

            def heavy(b, par):
                dve.wait_ge(s["xT"], b + 1)
                two_before(dve, s["rk"], b)
                for k in range(2):
                    nc.vector.tensor_scalar(mixed[:, par, 2 + k, :], xT[:, par, 0:S], omu[:, k:k + 1], None,
                                            ALU.mult).then_inc(s["shift"], 1)
                dve.wait_ge(s["shift"], b * 2 + 2)
                for k, mu in ((0, "L1_ffn_mu_r"), (1, "L1_ffn_mu_k")):
                    nc.vector.scalar_tensor_tensor(mixed[:, par, k, :], xT[:, par, 1:S + 1], vec(mu),
                                                   mixed[:, par, 2 + k, :], ALU.mult, ALU.add).then_inc(s["mix"], 1)

            def tail(b, par):
                dve.wait_ge(s["v"], b + 1)
                dve.wait_ge(s["rgate"], b + 1)
                nc.vector.scalar_tensor_tensor(rv[:, par, :], ps[:, 6 + par, 0:S], 0.5, rgate[:, par, :],
                                               ALU.mult, ALU.mult).then_inc(s["rv"], 1)
                dve.wait_ge(s["rv"], b + 1)
                update_batch(dve, s, b, rv[:, par, :], stats)
            batches(dve, lambda b, par: front_vector(dve, s, b, par), heavy, tail)

        def rwkv_scalar(act, s, turn):
            norm_scalar(act, turn)

            def front(b, par):
                two_before(act, s["mix"], b, 2)
                front_scalar(act, s, b, par)

            def heavy(b, par):
                act.wait_ge(s["rk"], b + 1)
                two_before(act, s["rv"], b)
                nc.scalar.activation(rgate[:, par, :], ps[:, 2 + par, 0:S], ACT.Sigmoid).then_inc(s["rgate"], 1)
                two_before(act, s["v"], b)
                nc.scalar.activation(kact[:, par, 0, :], ps[:, 4 + par, 0:S], ACT.Relu).then_inc(s["krelu"], 1)
                act.wait_ge(s["krelu"], b + 1)
                nc.scalar.activation(kact[:, par, 1, :], kact[:, par, 0, :], ACT.Square).then_inc(s["kact"], 1)
            batches(act, front, heavy, nothing)

        def rwkv_tensor(pe, s, before):
            pe.wait_ge(*before)

            def heavy(b, par):
                pe.wait_ge(s["mix"], b * 2 + 2)
                two_before(pe, s["kact"], b)
                for j in range(TPB):
                    nc.tensor.matmul(ps[:, 2 + par, j * P:(j + 1) * P], mixed[:, par, 0, j * P:(j + 1) * P],
                                     w("L1_ffn_W_r"), start=True, stop=True)
                nc.tensor.matmul(ps[:, 4 + par, 0:S], w("L1_ffn_W_k"), mixed[:, par, 1, :], start=True,
                                 stop=True).then_inc(s["rk"], 1)

            def tail(b, par):
                pe.wait_ge(s["kact"], b + 1)
                for j in range(TPB):
                    last = nc.tensor.matmul(ps[:, 6 + par, j * P:(j + 1) * P], kact[:, par, 1, j * P:(j + 1) * P],
                                            w("L1_ffn_W_v"), start=True, stop=True)
                last.then_inc(s["v"], 1)
            batches(pe, lambda b, par: front_tensor(pe, s, b, par), heavy, tail)

        UNITS = {"L0_attn_": TPB, "L1_attn_": TPB * TPB}

        def attn_front_tensor(pe, s, l, b, par):
            after(pe, s["x_done"], b - 2)
            front_tensor(pe, s, b, par)
            pe.wait_ge(s["xT"], b + 1)
            after(pe, s["q"], b)
            after(pe, s["k"], b)
            x = xT[:, par, 1:S + 1]
            nc.tensor.matmul(ps[:, 1, 0:S], w(l + "Wq"), x, start=True, stop=True)
            nc.tensor.matmul(ps[:, 1, S:2 * S], w(l + "Wk"), x, start=True, stop=True).then_inc(s["qk_ps"], 1)
            after(pe, s["vm"], b * TPB)
            if l == "L0_attn_":
                after(pe, s["vfull"], b)
                after(pe, s["kd"], b)
            for j in range(TPB):
                nc.tensor.matmul(ps[:, 2, j * P:(j + 1) * P], xT[:, par, 1 + j * P:1 + (j + 1) * P], w(l + "Wv"),
                                 start=True, stop=False)
                last = nc.tensor.matmul(ps[:, 2, j * P:(j + 1) * P], ones[:, :], row(l + "bv"), start=False, stop=True)
            if l == "L0_attn_":
                nc.tensor.matmul(ps[:, 2, 2 * P:3 * P], xT[:, par, 1:1 + P], w(l + "Wk"), start=True, stop=False)
                last = nc.tensor.matmul(ps[:, 2, 2 * P:3 * P], ones[:, :], row(l + "bk"), start=False, stop=True)
            last.then_inc(s["v_ps"], 1)

        def attn_front_scalar(act, s, l, b, par):
            two_before(act, s["v_ps"], b)
            front_scalar(act, s, b, par)
            act.wait_ge(s["qk_ps"], b + 1)
            two_before(act, s["sc"], b, UNITS[l] * HR)
            if l == "L0_attn_":
                two_before(act, s["qd"], b)
            nc.scalar.activation(qT[:, par, :], ps[:, 1, 0:S], ACT.Identity, bias=vec(l + "bq")).then_inc(s["q"], 1)
            two_before(act, s["km"], b)
            nc.scalar.activation(kT[:, par, :], ps[:, 1, S:2 * S], ACT.Identity, bias=vec(l + "bk")).then_inc(s["k"], 1)

        def attn_front_pool(pool, s, l, b, par):
            pool.wait_ge(s["k"], b + 1)
            two_before(pool, s["sc"], b, UNITS[l] * HR)
            nc.gpsimd.tensor_tensor(Km[:, par], kT[:, par, :].unsqueeze(1).broadcast_to([P, H, S]),
                                    head_of.unsqueeze(2).broadcast_to([P, H, S]), ALU.mult).then_inc(s["km"], 1)

        def attn_front_vector(dve, s, l, b, par):
            front_vector(dve, s, b, par)
            dve.wait_ge(s["v_ps"], b + 1)
            two_before(dve, s["av"], b, UNITS[l])
            for j in range(TPB):
                dst = Vm[:, par, j].rearrange("p (g r) (q d) -> p g (r q) d", r=HR, q=HR)[:, :, 0:HR * HR:HR + 1, :]
                src = ps[:, 2, j * P:(j + 1) * P].rearrange("p (g r d) -> p g r d", g=HG, r=HR)
                nc.vector.tensor_copy(dst, src).then_inc(s["vm"], 1)
            if l == "L0_attn_":
                nc.vector.tensor_copy(Vfull[:, par, :], ps[:, 2, 0:P]).then_inc(s["vfull"], 1)
                nc.vector.tensor_scalar(Kd[:, par, :], ps[:, 2, 2 * P:3 * P], k_decay, None, ALU.mult).then_inc(s["kd"], 1)

        def scores_tensor(pe, s, unit, par, keys, queries, free):
            for r in range(HR):
                after(pe, free, (unit - 1) * HR + r + 1)
                for g in range(HG):
                    last = nc.tensor.matmul(ps[:, 3 + r, g * P:(g + 1) * P],
                                            Km[:, par, g * HR + r, keys * P:(keys + 1) * P],
                                            qT[:, par, queries * P:(queries + 1) * P],
                                            start=(g == 0), stop=(g == HG - 1), skip_group_check=True)
                last.then_inc(s["sc"], 1)

        def weigh_values(pe, s, par, keys, queries, buf, first, ready):
            for r in range(HR):
                pe.wait_ge(ready[r][0], ready[r][1])
                for g in range(HG):
                    last = nc.tensor.matmul(ps[g * MW:(g + 1) * MW, 7, queries * P:(queries + 1) * P],
                                            Vm[:, par, keys, g * HR + r, :], att[:, buf, r, g, :],
                                            start=(first and r == 0), stop=(r == HR - 1),
                                            skip_group_check=True)
            last.then_inc(s["av"], 1)

        L0 = "L0_attn_"

        def attn0_tensor(pe, s, before):
            pe.wait_ge(*before)

            def heavy(b, par):
                pe.wait_ge(s["km"], b + 1)
                pe.wait_ge(s["q"], b + 1)
                scores_tensor(pe, s, b * TPB, par, 0, 0, s["at"])
                after(pe, s["oT"], b)
                pe.wait_ge(s["kd"], b + 1)
                pe.wait_ge(s["vfull"], b + 1)
                nc.tensor.matmul(ps[:, 7, S:S + P], Kd[:, par, :], Vfull[:, par, :], start=True,
                                 stop=True).then_inc(s["st_ps"], 1)
                scores_tensor(pe, s, b * TPB + 1, par, 1, 1, s["at"])
                pe.wait_ge(s["vm"], b * TPB + TPB)
                pe.wait_ge(s["st"], b + 1)
                at = b * TPB * HR
                weigh_values(pe, s, par, 0, 0, 0, True, [(s["at"], at + r + 1) for r in range(HR)])
                pe.wait_ge(s["qd"], b + 1)
                nc.tensor.matmul(ps[:, 7, P:2 * P], St[:, par, :], qD[:, par, :], start=True, stop=False,
                                 skip_group_check=True)
                weigh_values(pe, s, par, 1, 1, 1, False, [(s["at"], at + HR + r + 1) for r in range(HR)])

            def tail(b, par):
                pe.wait_ge(s["oT"], b + 1)
                after(pe, s["x_done"], b)
                pe.wait_ge(s["xT"], min(b + 3, B) if isinstance(b, int) else b + 3)
                nc.tensor.matmul(ps[:, 0, 0:S], w(L0 + "Wo"), oT[:, par, :], start=True, stop=True).then_inc(s["yps"], 1)
                pe.wait_ge(s["ym"], b + 1)
                nc.tensor.matmul(ps[:, 0, S:S + 1], block_avg[:, :], gst[:, 2:3], start=True, stop=True).then_inc(s["gm_ps"], 1)
                pe.wait_ge(s["dev"], b + 1)
                nc.tensor.matmul(ps[:, 0, S:S + 1], block_avg[:, :], gst[:, 4:5], start=True, stop=True).then_inc(s["gv_ps"], 1)
                pe.wait_ge(s["yn"], b + 1)
                nc.tensor.transpose(ps[:, 0, 0:P], yT[:, 0:P], ident)
                nc.tensor.transpose(ps[:, 0, P:S], yT[:, P:S], ident).then_inc(s["ynT"], 1)
            batches(pe, lambda b, par: attn_front_tensor(pe, s, L0, b, par), heavy, tail)

        def attn0_scalar(act, s, turn):
            norm_scalar(act, turn)

            def heavy(b, par):
                act.wait_ge(s["av"], b * TPB + TPB)
                two_before(act, s["yps"], b)
                nc.scalar.copy(oT[:, par, :], ps[:, 7, 0:S]).then_inc(s["oT"], 1)

            def tail(b, par):
                act.wait_ge(s["gv"], b + 1)
                nc.scalar.activation(gst[:, 6:7], gst[:, 5:6], ACT.Sqrt).then_inc(s["groot"], 1)
            batches(act, lambda b, par: attn_front_scalar(act, s, L0, b, par), heavy, tail)

        def attn0_pool(pool, s):
            batches(pool, lambda b, par: attn_front_pool(pool, s, L0, b, par), nothing, nothing)

        def attn0_vector(dve, s, turn, before):
            norm_vector(dve, turn, before)
            v = nc.vector

            def heavy(b, par):
                dve.wait_ge(s["q"], b + 1)
                v.tensor_tensor(qD[:, par, :], qT[:, par, P:S], q_decay, ALU.mult).then_inc(s["qd"], 1)
                for u in range(TPB):
                    after(dve, s["av"], b * TPB)
                    for r in range(HR):
                        dve.wait_ge(s["sc"], (b * TPB + u) * HR + r + 1)
                        v.tensor_tensor(att[:, u, r], ps[:, 3 + r, :].rearrange("p (g q) -> p g q", g=HG),
                                        decay_mask.unsqueeze(1).broadcast_to([P, HG, P]), ALU.mult).then_inc(s["at"], 1)
                    if u == 0:
                        dve.wait_ge(s["st_ps"], b + 1)
                        v.tensor_tensor(St[:, par, :], ps[:, 7, S:S + P], block_diag, ALU.mult).then_inc(s["st"], 1)

            def tail(b, par):
                col = [gst[:, n:n + 1] for n in range(10)]
                dve.wait_ge(s["yps"], b + 1)
                v.bn_stats(gbn[:, :], ps[:, 0, 0:S]).then_inc(s["ymv"], 1)
                dve.wait_ge(s["ymv"], b * 5 + 1)
                v.tensor_tensor(col[0], gbn[:, 1:2], gbn[:, 4:5], ALU.add).then_inc(s["ymv"], 1)
                dve.wait_ge(s["ymv"], b * 5 + 2)
                v.scalar_tensor_tensor(col[2], col[0], 0.5, vec(L0 + "bo"), ALU.mult, ALU.add).then_inc(s["ym"], 1)
                v.tensor_tensor(col[1], gbn[:, 1:2], gbn[:, 4:5], ALU.subtract).then_inc(s["ymv"], 1)
                v.tensor_tensor(col[7], gbn[:, 2:3], gbn[:, 5:6], ALU.add).then_inc(s["ymv"], 1)
                dve.wait_ge(s["ymv"], b * 5 + 4)
                v.scalar_tensor_tensor(col[8], col[1], 0.25, col[1], ALU.mult, ALU.mult).then_inc(s["ymv"], 1)
                dve.wait_ge(s["ymv"], b * 5 + 5)
                v.scalar_tensor_tensor(col[1], col[7], 1.0 / S, col[8], ALU.mult, ALU.add).then_inc(s["yvar"], 1)
                dve.wait_ge(s["gm_ps"], b + 1)
                v.tensor_tensor(col[3], col[2], ps[:, 0, S:S + 1], ALU.subtract).then_inc(s["gm"], 1)
                dve.wait_ge(s["gm"], b + 1)
                dve.wait_ge(s["yvar"], b + 1)
                v.scalar_tensor_tensor(col[4], col[3], col[3], col[1], ALU.mult, ALU.add).then_inc(s["dev"], 1)
                dve.wait_ge(s["gv_ps"], b + 1)
                v.tensor_scalar(col[5], ps[:, 0, S:S + 1], EPS, None, ALU.add).then_inc(s["gv"], 1)
                v.scalar_tensor_tensor(col[9], col[0], -0.5, col[3], ALU.mult, ALU.add).then_inc(s["ab"], 1)
                dve.wait_ge(s["groot"], b + 1)
                v.reciprocal(col[7], col[6]).then_inc(s["grs"], 1)
                dve.wait_ge(s["grs"], b + 1)
                v.tensor_tensor(col[8], col[7], vec(L0 + "gamma"), ALU.mult).then_inc(s["ab"], 1)
                dve.wait_ge(s["ab"], b * 3 + 2)
                v.scalar_tensor_tensor(col[2], col[8], col[9], vec(L0 + "beta"), ALU.mult, ALU.add).then_inc(s["ab"], 1)
                dve.wait_ge(s["ab"], b * 3 + 3)
                v.tensor_scalar(yT[:, :], ps[:, 0, 0:S], col[8], col[2], ALU.mult, ALU.add).then_inc(s["yn"], 1)
                dve.wait_ge(s["ynT"], b + 1)
                update_batch(dve, s, b, ps[:, 0, 0:S])
            batches(dve, lambda b, par: attn_front_vector(dve, s, L0, b, par), heavy, tail)

        L1 = "L1_attn_"
        NU = UNITS[L1]
        DVE_PARTS = HR // 2

        def attn1_tensor(pe, s, before):
            pe.wait_ge(*before)

            def heavy(b, par):
                pe.wait_ge(s["km"], b + 1)
                pe.wait_ge(s["q"], b + 1)

                def values(u):
                    n = b * NU + u
                    if u == 0:
                        after(pe, s["oT"], b)
                        pe.wait_ge(s["vm"], b * TPB + TPB)
                    rest = HR - DVE_PARTS
                    ready = [(s["at"], n * DVE_PARTS + r + 1) if r < DVE_PARTS else
                             (s["at_pool"], n * rest + r - DVE_PARTS + 1) for r in range(HR)]
                    weigh_values(pe, s, par, u % TPB, u // TPB, u % 2, u % TPB == 0, ready)
                for u in range(NU):
                    n = b * NU + u
                    scores_tensor(pe, s, n, par, u % TPB, u // TPB, s["ex"])
                    pe.wait_ge(s["mx"], n + 1)
                    for r in range(HR):
                        nc.tensor.matmul(ps[:, 3 + r, :], minus_i[:, :], amax[:, :].unsqueeze(1).broadcast_to([P, HG, P]),
                                         start=False, stop=True, skip_group_check=True).then_inc(s["sub"], 1)
                    if u:
                        values(u - 1)
                values(NU - 1)

            def tail(b, par):
                pe.wait_ge(s["oT"], b + 1)
                after(pe, s["x_done"], b)
                pe.wait_ge(s["xT"], min(b + 3, B) if isinstance(b, int) else b + 3)
                for j in range(TPB):
                    nc.tensor.matmul(ps[:, 0, j * P:(j + 1) * P], oT[:, par, j * P:(j + 1) * P], w(L1 + "Wo"),
                                     start=True, stop=False)
                    last = nc.tensor.matmul(ps[:, 0, j * P:(j + 1) * P], ones[:, :], row(L1 + "bo"), start=False, stop=True)
                last.then_inc(s["yps"], 1)
            batches(pe, lambda b, par: attn_front_tensor(pe, s, L1, b, par), heavy, tail)

        def attn1_scalar(act, s, turn):
            norm_scalar(act, turn)

            def heavy(b, par):
                for u in range(NU):
                    n = b * NU + u
                    after(act, s["av"], n - 1)
                    for r in range(HR):
                        act.wait_ge(s["sub"], n * HR + r + 1)
                        nc.scalar.activation(att[:, u % 2, r].rearrange("p g q -> p (g q)"), ps[:, 3 + r, :], ACT.Exp,
                                             scale=SCALE).then_inc(s["ex"], 1)
                act.wait_ge(s["av"], b * NU + NU)
                two_before(act, s["yps"], b)
                nc.scalar.copy(oT[:, par, :], ps[:, 7, 0:S]).then_inc(s["oT"], 1)
            batches(act, lambda b, par: attn_front_scalar(act, s, L1, b, par), heavy, nothing)

        def attn1_pool(pool, s):
            def heavy(b, par):
                for u in range(NU):
                    n = b * NU + u
                    pool.wait_ge(s["rden"], n + 1)
                    for r in range(DVE_PARTS, HR):
                        nc.gpsimd.tensor_tensor(att[:, u % 2, r], att[:, u % 2, r],
                                                den[:, 1, :].unsqueeze(1).broadcast_to([P, HG, P]),
                                                ALU.mult).then_inc(s["at_pool"], 1)
            batches(pool, lambda b, par: attn_front_pool(pool, s, L1, b, par), heavy, nothing)

        def attn1_vector(dve, s, turn, before):
            norm_vector(dve, turn, before)
            v = nc.vector

            def heavy(b, par):
                def largest(u):
                    n = b * NU + u
                    dve.wait_ge(s["sc"], n * HR + HR)
                    after(dve, s["sub"], n * HR)
                    v.tensor_reduce(amax[:, :], ps[:, 3:3 + HR, :].rearrange("p r (g q) -> p q (r g)", g=HG), AX_X,
                                    ALU.max).then_inc(s["mx"], 1)

                def normalise(u):
                    n = b * NU + u
                    buf = u % 2
                    dve.wait_ge(s["ex"], n * HR + HR)
                    v.tensor_reduce(den[:, 0, :], att[:, buf].rearrange("p r g q -> p q (r g)"), AX_X,
                                    ALU.add).then_inc(s["den"], 1)
                    dve.wait_ge(s["den"], n + 1)
                    after(dve, s["at_pool"], n * (HR - DVE_PARTS))
                    v.reciprocal(den[:, 1, :], den[:, 0, :]).then_inc(s["rden"], 1)
                    dve.wait_ge(s["rden"], n + 1)
                    for r in range(DVE_PARTS):
                        v.tensor_tensor(att[:, buf, r], att[:, buf, r], den[:, 1, :].unsqueeze(1).broadcast_to([P, HG, P]),
                                        ALU.mult).then_inc(s["at"], 1)
                for u in range(NU):
                    largest(u)
                    if u:
                        normalise(u - 1)
                normalise(NU - 1)

            def tail(b, par):
                dve.wait_ge(s["yps"], b + 1)
                update_batch(dve, s, b, ps[:, 0, 0:S])
            batches(dve, lambda b, par: attn_front_vector(dve, s, L1, b, par), heavy, tail)

        moe1, moe2, rwkv1, rwkv2 = MO["moe1"], MO["moe2"], RW["rwkv1"], RW["rwkv2"]
        attn0, attn1 = AT["attn0"], AT["attn1"]

        block = ctx.enter_context(nc.Block())

        @block.sync
        def _(sp):
            for n in range(4):
                sp.dma_start(X[:, n * 4:(n + 1) * 4, :],
                             io["x"][n * 4 * P:(n + 1) * 4 * P, :].rearrange("(t p) d -> p t d", p=P)).then_inc(ld["x"], 16)
            sp.dma_start(gateT[:, :], io["gateT"]).then_inc(ld["small"], 16)
            sp.dma_start(rows[:, :, :], io["rows"]).then_inc(ld["small"], 16)
            sp.dma_start(W1[:, :, :], io["w1"]).then_inc(ld["moe"], 16)
            sp.dma_start(W3[:, :, :], io["w3"]).then_inc(ld["moe"], 16)
            sp.dma_start(W2[:, :, :, :], io["w2"]).then_inc(ld["moe"], 16)
            sp.dma_start(W[:, :, :], io["weights"]).then_inc(ld["w"], 16)
            for b in range(B):
                sp.wait_ge(rwkv2["x_done"], b + 1)
                sp.dma_start(out[b].rearrange("(t p) d -> p t d", p=P),
                             X[:, b * TPB:(b + 1) * TPB, :]).then_inc(final["stored"], 16)
            sp.wait_ge(final["stored"], 16 * B)

        @block.gpsimd
        def _(pool):
            nc.gpsimd.memset(ones[:, :], 1.0)
            nc.gpsimd.memset(xT[:, :, 0:1], 0.0)
            nc.gpsimd.memset(Vm[:, :, :, :, :], 0.0).then_inc(su["zeros"], 1)
            moe_front_pool(pool, moe1)
            moe_pool(pool, moe1)
            attn0_pool(pool, attn0)
            moe_front_pool(pool, moe2)
            moe_pool(pool, moe2)
            attn1_pool(pool, attn1)

        @block.vector
        def _(dve):
            dve.wait_ge(ld["const"], 32)
            dve.wait_ge(su["zeros"], 1)
            nc.vector.tensor_scalar(omu[:, :], vecs[:, len(V_NAMES) - 2:], -1.0, 1.0, ALU.mult, ALU.add)
            nc.vector.tensor_scalar(minus_i[:, :], ident, -1.0, None, ALU.mult)
            nc.vector.tensor_scalar(block_avg[:, :], block_diag, 1.0 / HD, None, ALU.mult).then_inc(su["consts"], 1)
            dve.wait_ge(su["consts"], 1)
            for t in range(TILES):
                dve.wait_ge(ld["x"], 16 * 4)
                tile_stats(dve, su, t, None)
            moe_front_vector(dve, moe1, 0, (su["stats"], TILES))
            moe_vector(dve, moe1)
            attn0_vector(dve, attn0, 1, (moe1["stats"], TILES))
            moe_front_vector(dve, moe2, 2, (attn0["stats"], TILES))
            moe_vector(dve, moe2)
            rwkv_vector(dve, rwkv1, 3, (moe2["stats"], TILES), True)
            attn1_vector(dve, attn1, 4, (rwkv1["stats"], TILES))
            rwkv_vector(dve, rwkv2, 5, (attn1["stats"], TILES), False)

        @block.scalar
        def _(act):
            act.dma_start(consts[:, :], io["consts"]).then_inc(ld["const"], 16)
            act.dma_start(vecs[:, :], io["vecs"]).then_inc(ld["const"], 16)
            act.wait_ge(ld["const"], 32)
            moe_front_scalar(act, moe1, 0)
            moe_scalar(act, moe1)
            attn0_scalar(act, attn0, 1)
            moe_front_scalar(act, moe2, 2)
            moe_scalar(act, moe2)
            rwkv_scalar(act, rwkv1, 3)
            attn1_scalar(act, attn1, 4)
            rwkv_scalar(act, rwkv2, 5)

        @block.tensor
        def _(pe):
            pe.wait_ge(ld["const"], 32)
            pe.wait_ge(ld["small"], 32)
            pe.wait_ge(su["consts"], 1)
            moe_front_tensor(pe, moe1, (su["stats"], TILES))
            pe.wait_ge(ld["moe"], 48)
            moe_tensor(pe, moe1)
            pe.wait_ge(ld["w"], 16)
            attn0_tensor(pe, attn0, (moe1["stats"], TILES))
            moe_front_tensor(pe, moe2, (attn0["stats"], TILES))
            moe_tensor(pe, moe2)
            rwkv_tensor(pe, rwkv1, (moe2["stats"], TILES))
            attn1_tensor(pe, attn1, (rwkv1["stats"], TILES))
            rwkv_tensor(pe, rwkv2, (attn1["stats"], TILES))


def kernel(**inputs):
    import concourse.bacc as bacc
    from concourse.bass_utils import run_bass_kernel_spmd as run

    a = {n: np.asarray(v) for n, v in inputs.items()}
    arrays = {
        "x": a["L0_attn_x"].reshape(B * S, D),
        "consts": shape_constants(),
        "vecs": np.stack([a[n] for n in V_NAMES], axis=1),
        "rows": np.stack([a[n] for n in R_NAMES])[None],
        "weights": np.stack([a[n] for n in W_NAMES] + [a[n].T for n in WT_NAMES], axis=1),
        "gateT": a["L0_ffn_gate_w"].T,
        "w1": a["L0_ffn_w1"].transpose(1, 0, 2),
        "w3": a["L0_ffn_w3"].transpose(1, 0, 2),
        "w2": a["L0_ffn_w2"].reshape(E, NCH, IC, D).transpose(2, 0, 1, 3),
    }
    arrays = {n: np.ascontiguousarray(v) for n, v in arrays.items()}
    nc = bacc.Bacc("TRN2", target_bir_lowering=False, num_devices=1)
    io = {n: nc.dram_tensor(f"in_{n}", v.shape, mybir.dt.from_np(v.dtype), kind="ExternalInput").ap()
          for n, v in arrays.items()}
    out = nc.dram_tensor("out_0", (B, S, D), F32, kind="ExternalOutput").ap()
    build(nc, io, out)
    r = run(nc, [{f"in_{n}": v for n, v in arrays.items()}], core_ids=[0])
    return r.results[0]["out_0"]
```

```python
from contextlib import ExitStack

import numpy as np

import concourse.bass as bass
from concourse import mybir

F32 = mybir.dt.float32
BF16 = mybir.dt.bfloat16
I32 = mybir.dt.int32
U32 = mybir.dt.uint32
ALU = mybir.AluOpType
ACT = mybir.ActivationFunctionType
AX_X = mybir.AxisListType.X

P = 128
B, S, D = 8, 256, 128
TILES = B * S // P
TPB = S // P
H = 16
HD = D // H
QH = P // 2
HG = 4
HR = H // HG
MW = HD * HR
E = 8
TOPK = 2
PAD = TILES // 2
PAIRS = TOPK * TILES
SLOT_TILES = (PAIRS * P + E * (P - 1)) // P
I = 448
NCH = 4
IC = I // NCH
DECAY = 0.95
EPS = 1e-5
SCALE = float(HD) ** -0.5

C_IDENT, C_MASK, C_BLOCK, C_QDECAY, C_HEAD, C_KDECAY, C_RANK = 0, 128, 256, 384, 512, 528, 529
C_BEFORE = C_RANK + E
C_LANE = C_BEFORE + P
C_TILE_ROWS = C_LANE + P
C_LOWER = C_TILE_ROWS + TILES
C_PAIR = C_LOWER + E * E
C_SPARE = C_PAIR + PAIRS
C_COLS = C_SPARE + SLOT_TILES
V_NAMES = ["L0_attn_bq", "L0_attn_bk", "L0_attn_bo", "L0_attn_gamma", "L0_attn_beta",
           "L1_attn_bq", "L1_attn_bk", "L1_ffn_mu_r", "L1_ffn_mu_k"]
R_NAMES = ["L0_attn_bv", "L0_attn_bk", "L1_attn_bv", "L1_attn_bo"]
W_NAMES = ["L0_attn_Wq", "L0_attn_Wk", "L0_attn_Wv", "L0_attn_Wo"]
WT_NAMES = ["L1_attn_Wq", "L1_attn_Wk", "L1_attn_Wv", "L1_attn_Wo", "L1_ffn_W_r", "L1_ffn_W_k", "L1_ffn_W_v"]


def shape_constants():
    c = np.zeros((P, C_COLS), np.float32)
    p = np.arange(P)
    c[:, C_IDENT:C_IDENT + P] = np.eye(P)
    gap = p[None, :] - p[:, None]
    c[:, C_MASK:C_MASK + P] = np.where(gap >= 0, DECAY ** np.maximum(gap, 0), 0.0)
    c[:, C_BLOCK:C_BLOCK + P] = p[:, None] // HD == p[None, :] // HD
    c[:, C_QDECAY:C_QDECAY + P] = DECAY ** (p[None, :] + 1.0)
    c[:, C_HEAD:C_HEAD + H] = p[:, None] // HD == np.arange(H)[None, :]
    c[:, C_KDECAY] = DECAY ** (P - 1.0 - p)
    c[:, C_RANK:C_RANK + E] = E - np.arange(E)[None, :]
    c[:, C_BEFORE:C_BEFORE + P] = p[:, None] < p[None, :]
    c[:, C_LANE:C_LANE + P] = p[None, :]
    c[:, C_TILE_ROWS:C_TILE_ROWS + TILES] = P * np.arange(TILES)[None, :]
    c[:, C_LOWER:C_LOWER + E * E] = (np.arange(E)[None, :] < np.arange(E)[:, None]).reshape(1, E * E)
    c[:, C_PAIR:C_PAIR + PAIRS] = 1 + P * np.arange(PAIRS)[None, :] + p[:, None]
    c[:, C_SPARE:C_SPARE + SLOT_TILES] = 1 + P * (PAIRS + np.arange(SLOT_TILES)[None, :]) + p[:, None]
    return c


LANE_PIECE = 8
KEEP = 4
ROUNDER = 1.5 * 2.0 ** 23

ds = bass.ds


def build(nc, io, out):
    with ExitStack() as ctx:
        def sb(name, shape, dt=F32):
            return ctx.enter_context(nc.sbuf_tensor(name, shape, dt))

        def sems(stage, names):
            return {n: ctx.enter_context(nc.semaphore(f"{stage}_{n}")) for n in names.split()}

        X = sb("X", [P, TILES, D])
        consts = sb("consts", [P, C_COLS])
        vecs = sb("vecs", [P, len(V_NAMES)])
        omu = sb("omu", [P, 2])
        rows = sb("rows", [P, len(R_NAMES), D])
        ones = sb("ones", [1, P])
        W = sb("W", [P, len(W_NAMES) + len(WT_NAMES), D])
        gateT = sb("gateT", [P, E])
        W1 = sb("W1", [P, E, I])
        W3 = sb("W3", [P, E, I])
        W2 = sb("W2", [IC, E, NCH, D])
        minus_i = sb("minus_i", [P, P], BF16)
        block_avg = sb("block_avg", [P, P])
        bn = sb("bn", [P, TILES, 6])
        mean = sb("mean", [P, TILES])
        nrm = sb("nrm", [P, 6, TILES])
        xn = sb("xn", [P, 2, TPB, D])
        xT = sb("xT", [P, 2, S + 1])
        qT = sb("qT", [P, 2, S])
        kT = sb("kT", [P, 2, S])
        Qm = sb("Qm", [P, 2, HR, HG, S])
        Vm = sb("Vm", [P, 2, TPB, H, MW])
        Vfull = sb("Vfull", [P, 2, D])
        Kd = sb("Kd", [P, 2, D])
        St = sb("St", [P, 2, D])
        qD = sb("qD", [P, 2, P])
        att = sb("att", [P, 4, HR, HG, P])
        amax = sb("amax", [P, 2, QH], BF16)
        sc16 = sb("sc16", [P, 2, 2, 512], BF16)
        hmax = sb("hmax", [P, 2, 512], BF16)
        den = sb("den", [P, 2, P])
        rden = sb("rden", [P, 2, P])
        bk_decay = sb("bk_decay", [P, D])
        oT = sb("oT", [P, 2, S])
        gbn = sb("gbn", [P, 6])
        gst = sb("gst", [P, 10])
        yT = sb("yT", [P, S])
        LG = sb("LG", [P, TILES, E])
        rt = sb("rt", [P, 6, TILES, E])
        rs = sb("rs", [P, 8, TILES])
        all_ones = sb("all_ones", [P, P])
        run = sb("run", [P, 2, PAD + TILES, E])
        seat = sb("seat", [P, TILES, E])
        fill = sb("fill", [P, E, TILES])
        tri = sb("tri", [P, E, E])
        need = sb("need", [P, E])
        begin = sb("begin", [P, E])
        place = sb("place", [P, 4, PAIRS])
        own = sb("own", [1, 2, SLOT_TILES, E])
        expert_f = sb("expert_f", [1, SLOT_TILES])
        expert = sb("expert", [1, SLOT_TILES], I32)
        slot = sb("slot", [P, 6, SLOT_TILES])
        source = sb("source", [P, SLOT_TILES], U32)
        target = sb("target", [P, SLOT_TILES], U32)
        source_now = sb("source_now", [P, 2, 1], U32)
        target_now = sb("target_now", [P, 2, 1], U32)
        pool_turn = sb("pool_turn", [1, 2])
        xg = sb("xg", [P, 2, D])
        xs = sb("xs", [P, 2, P])
        sg = sb("sg", [P, 2, I])
        hb = sb("hb", [P, 2, I])
        hT = sb("hT", [IC, 2, NCH, P])
        ys = sb("ys", [P, 2, D])
        lane_of = att.rearrange("p n r g q -> p (n r g) q")[:, 0:PAIRS, :]
        claim = att.rearrange("p n r g q -> p (n r g q)")[:, PAIRS * P:PAIRS * (P + 2 * SLOT_TILES)].rearrange(
            "p (n k a) -> p n k a", k=2, a=SLOT_TILES)
        yback = Qm.rearrange("p n r g s -> p (n r g s)")[:, 0:PAIRS * D].rearrange("p (k t d) -> p k t d", k=TOPK, d=D)
        spare = Qm.rearrange("p n r g s -> p (n r g s)")[:, PAIRS * D:]
        mixed = spare[:, 0:8 * S].rearrange("p (n k s) -> p n k s", n=2, s=S)
        rgate = spare[:, 8 * S:10 * S].rearrange("p (n s) -> p n s", n=2)
        kact = spare[:, 10 * S:14 * S].rearrange("p (n k s) -> p n k s", n=2, s=S)
        rv = spare[:, 14 * S:16 * S].rearrange("p (n s) -> p n s", n=2)

        ps = ctx.enter_context(nc.psum_tensor("ps", [P, 8, 512], F32))

        ident = consts[:, C_IDENT:C_IDENT + P]
        decay_mask = consts[:, C_MASK:C_MASK + P]
        block_diag = consts[:, C_BLOCK:C_BLOCK + P]
        q_decay = consts[:, C_QDECAY:C_QDECAY + P]
        head_of = consts[:, C_HEAD:C_HEAD + H]
        k_decay = consts[:, C_KDECAY:C_KDECAY + 1]
        rank = consts[:, C_RANK:C_RANK + E]
        before_me = consts[:, C_BEFORE:C_BEFORE + P]
        lane = consts[:, C_LANE:C_LANE + P]
        tile_rows = consts[:, C_TILE_ROWS:C_TILE_ROWS + TILES]
        lower = consts[:, C_LOWER:C_LOWER + E * E].rearrange("p (a b) -> p a b", a=E)
        pair_no = consts[:, C_PAIR:C_PAIR + PAIRS]
        spare_row = consts[:, C_SPARE:C_SPARE + SLOT_TILES]

        def vec(name):
            n = V_NAMES.index(name)
            return vecs[:, n:n + 1]

        def row(name):
            return rows[:, R_NAMES.index(name), :]

        def w(name):
            return W[:, (W_NAMES + WT_NAMES).index(name), :]

        ld = sems("load", "const x small w moe")
        su = sems("setup", "zeros consts stats")
        final = sems("final", "stored")
        nm = sems("norm", "mean var root newton ready")
        norm_names = "xn xnT xT x_done stats "
        MO = {n: sems(n, norm_names + "lg lgT sum") for n in ("moe1", "moe2")}
        me = sems("moe", "rt exp both count claim lanes slots expert source target "
                  "source_now target_now xg_ps xs gu sg h hT_ps hT y ys")
        kept_done, gathered, scattered = ([ctx.enter_context(nc.semaphore(f"{n}{par}")) for par in range(2)]
                                          for n in ("kept_done", "gathered", "scattered"))
        turned = [ctx.enter_context(nc.semaphore(f"turned{k}")) for k in range(2)]
        fetched = [ctx.enter_context(nc.semaphore(f"fetched{n}")) for n in range(TILES // KEEP)]
        RW = {n: sems(n, norm_names + "shift mix rk rgate krelu kact v rv") for n in ("rwkv1", "rwkv2")}
        attn_names = norm_names + "qk_ps v_ps q k qm vm sc at av oT yps "
        AT = {"attn0": sems("attn0", attn_names + "vfull kd qd st_ps st ymv ym yvar gm_ps gm dev gv_ps gv groot grs ab yn ynT"),
              "attn1": sems("attn1", attn_names + "sc16 hmax mx sub ex den rden at_pool")}

        def batches(eng, front, heavy, tail):
            def turn(i):
                front(i * 2 + 2, 0)
                heavy(i * 2 + 1, 1)
                tail(i * 2, 0)
                front(i * 2 + 3, 1)
                heavy(i * 2 + 2, 0)
                tail(i * 2 + 1, 1)
            front(0, 0)
            front(1, 1)
            heavy(0, 0)
            turn(0)
            with eng.Fori(1, B // 2 - 1) as i:
                turn(i)
            heavy(B - 1, 1)
            tail(B - 2, 0)
            tail(B - 1, 1)

        def nothing(b, par):
            pass

        def after(eng, sem, value):
            if not isinstance(value, int) or value > 0:
                eng.wait_ge(sem, value)

        def two_before(eng, sem, b, each=1):
            after(eng, sem, (b - 1) * each)

        def norm_vector(dve, turn, before):
            dve.wait_ge(*before)
            nc.vector.tensor_tensor(nrm[:, 3, :], bn[:, :, 1], bn[:, :, 4], ALU.add).then_inc(nm["mean"], 1)
            nc.vector.tensor_tensor(nrm[:, 4, :], bn[:, :, 1], bn[:, :, 4], ALU.subtract).then_inc(nm["mean"], 1)
            nc.vector.tensor_tensor(nrm[:, 5, :], bn[:, :, 2], bn[:, :, 5], ALU.add).then_inc(nm["mean"], 1)
            dve.wait_ge(nm["mean"], turn * 6 + 3)
            nc.vector.tensor_scalar(mean[:, :], nrm[:, 3, :], 0.5, None, ALU.mult).then_inc(nm["mean"], 1)
            nc.vector.scalar_tensor_tensor(nrm[:, 4, :], nrm[:, 4, :], 0.25, nrm[:, 4, :], ALU.mult,
                                           ALU.mult).then_inc(nm["mean"], 1)
            nc.vector.tensor_scalar(nrm[:, 5, :], nrm[:, 5, :], 1.0 / D, EPS, ALU.mult, ALU.add).then_inc(nm["mean"], 1)
            dve.wait_ge(nm["mean"], turn * 6 + 6)
            nc.vector.tensor_tensor(nrm[:, 0, :], nrm[:, 4, :], nrm[:, 5, :], ALU.add).then_inc(nm["var"], 1)
            dve.wait_ge(nm["root"], turn + 1)
            nc.vector.reciprocal(nrm[:, 2, :], nrm[:, 1, :]).then_inc(nm["newton"], 1)
            dve.wait_ge(nm["newton"], turn * 4 + 1)
            nc.vector.tensor_tensor(nrm[:, 3, :], nrm[:, 2, :], nrm[:, 2, :], ALU.mult).then_inc(nm["newton"], 1)
            dve.wait_ge(nm["newton"], turn * 4 + 2)
            nc.vector.tensor_tensor(nrm[:, 3, :], nrm[:, 3, :], nrm[:, 0, :], ALU.mult).then_inc(nm["newton"], 1)
            dve.wait_ge(nm["newton"], turn * 4 + 3)
            nc.vector.tensor_scalar(nrm[:, 3, :], nrm[:, 3, :], -0.5, 1.5, ALU.mult, ALU.add).then_inc(nm["newton"], 1)
            dve.wait_ge(nm["newton"], turn * 4 + 4)
            nc.vector.tensor_tensor(nrm[:, 2, :], nrm[:, 2, :], nrm[:, 3, :], ALU.mult).then_inc(nm["ready"], 1)
            dve.wait_ge(nm["ready"], turn + 1)

        def norm_scalar(act, turn):
            act.wait_ge(nm["var"], turn + 1)
            nc.scalar.activation(nrm[:, 1, :], nrm[:, 0, :], ACT.Sqrt).then_inc(nm["root"], 1)

        def front_vector(dve, s, b, par, m=None):
            two_before(dve, s["xnT"], b)
            if m is not None:
                after(dve, kept_done[par], m * 16 * B // 2 + (b - par) * 8)
            for j in range(TPB):
                t = b * TPB + j
                nc.vector.tensor_scalar(xn[:, par, j, :], X[:, t, :], mean[:, ds(t, 1)], nrm[:, 2, ds(t, 1)],
                                        ALU.subtract, ALU.mult).then_inc(s["xn"], 1)

        def front_tensor(pe, s, b, par, bank=0):
            pe.wait_ge(s["xn"], b * TPB + TPB)
            after(pe, s["xT"], b)
            nc.tensor.transpose(ps[:, bank, 0:P], xn[:, par, 0, :], ident)
            nc.tensor.transpose(ps[:, bank, P:S], xn[:, par, 1, :], ident).then_inc(s["xnT"], 1)

        def front_scalar(act, s, b, par, bank=0):
            act.wait_ge(s["xnT"], b + 1)
            nc.scalar.copy(xT[:, par, 1:S + 1], ps[:, bank, 0:S]).then_inc(s["xT"], 1)

        def tile_stats(dve, s, t, updates):
            if updates is not None:
                dve.wait_ge(s["x_done"], updates)
            nc.vector.bn_stats(bn[:, t, :], X[:, t, :]).then_inc(s["stats"], 1)

        def update_batch(dve, s, b, src, stats=True):
            tiles = X[:, ds(b * TPB, TPB), :]
            nc.vector.tensor_tensor(tiles, tiles, src.rearrange("p (j d) -> p j d", j=TPB),
                                    ALU.add).then_inc(s["x_done"], 1)
            if stats:
                for j in range(TPB):
                    tile_stats(dve, s, b * TPB + j, b + 1)

        ROUTE_STEPS = 44
        ROUTE_DIFF = 12

        def moe_front_vector(dve, s, m, turn, before):
            norm_vector(dve, turn, before)

            def tail(b, par):
                dve.wait_ge(s["lg"], b + 1)
                nc.vector.tensor_copy(LG[:, ds(b * TPB, TPB), :],
                                      ps[:, 2 + par, 0:TPB * E].rearrange("p (j e) -> p j e", j=TPB)).then_inc(s["lgT"], 1)
            batches(dve, lambda b, par: front_vector(dve, s, b, par, m), nothing, tail)

            dve.wait_ge(s["lgT"], B)
            step = [0]

            def link(ins):
                step[0] += 1
                ins.then_inc(me["rt"], 1)
                dve.wait_ge(me["rt"], m * ROUTE_STEPS + step[0])

            def wide(n):
                return rs[:, n, :].unsqueeze(2).broadcast_to([P, TILES, E])
            ranks = rank.unsqueeze(1).broadcast_to([P, TILES, E])
            v = nc.vector
            for k, src in ((0, LG[:, :, :]), (1, rt[:, 2])):
                link(v.tensor_reduce(rs[:, k, :], src, AX_X, ALU.max))
                link(v.tensor_tensor(rt[:, 0], src, wide(k), ALU.is_equal))
                link(v.tensor_tensor(rt[:, 1], rt[:, 0], ranks, ALU.mult))
                link(v.tensor_reduce(rs[:, 2, :], rt[:, 1], AX_X, ALU.max))
                link(v.tensor_tensor(rt[:, 3 + k], rt[:, 1], wide(2), ALU.is_equal))
                if k == 0:
                    link(v.scalar_tensor_tensor(rt[:, 2], rt[:, 3], -3.0e38, LG[:, :, :], ALU.mult, ALU.add))
            link(v.tensor_tensor(rs[:, 3, :], rs[:, 1, :], rs[:, 0, :], ALU.subtract))
            assert step[0] == ROUTE_DIFF
            v.tensor_tensor(rt[:, 5], rt[:, 3], rt[:, 4], ALU.add).then_inc(me["both"], 1)
            dve.wait_ge(me["exp"], m + 1)
            link(v.tensor_scalar(rs[:, 5, :], rs[:, 4, :], 1.0, None, ALU.add))
            link(v.reciprocal(rs[:, 6, :], rs[:, 5, :]))
            link(v.tensor_tensor(rs[:, 7, :], rs[:, 6, :], rs[:, 4, :], ALU.mult))
            dve.wait_ge(me["count"], m + 1)
            link(v.tensor_copy(run[:, 0, PAD:, :], ps[:, 1, 0:TILES * E].rearrange("p (t e) -> p t e", e=E)))
            side, shift = 0, 1
            while shift < TILES:
                link(v.tensor_tensor(run[:, 1 - side, PAD:, :], run[:, side, PAD:, :],
                                     run[:, side, PAD - shift:PAD + TILES - shift, :], ALU.add))
                side, shift = 1 - side, shift * 2
            total = run[:, side, PAD + TILES - 1, :]
            link(v.tensor_tensor(fill[:, :, :], total.unsqueeze(2).broadcast_to([P, E, TILES]),
                                 tile_rows.unsqueeze(1).broadcast_to([P, E, TILES]), ALU.is_gt))
            link(v.tensor_reduce(need[:, :], fill[:, :, :], AX_X, ALU.add))
            link(v.tensor_tensor(tri[:, :, :], need[:, :].unsqueeze(1).broadcast_to([P, E, E]), lower, ALU.mult))
            link(v.tensor_reduce(begin[:, :], tri[:, :, :], AX_X, ALU.add))
            link(v.tensor_tensor(seat[:, :, :], ps[:, 0, 0:TILES * E].rearrange("p (t e) -> p t e", e=E),
                                 run[:, side, PAD - 1:PAD + TILES - 1, :], ALU.add))
            link(v.scalar_tensor_tensor(seat[:, :, :], begin[:, :].unsqueeze(1).broadcast_to([P, TILES, E]), float(P),
                                        seat[:, :, :], ALU.mult, ALU.add))
            for k in range(TOPK):
                link(v.tensor_tensor(rt[:, k], rt[:, 3 + k], seat[:, :, :], ALU.mult))
            link(v.tensor_reduce(place[:, 0, :], rt[:, 0:TOPK].rearrange("p k t e -> p (k t) e"), AX_X, ALU.add))
            link(v.tensor_scalar(place[:, 1, :], place[:, 0, :], 1.0 / P, -0.5 + 0.5 / P, ALU.mult, ALU.add))
            link(v.tensor_scalar(place[:, 1, :], place[:, 1, :], ROUNDER, None, ALU.add))
            link(v.tensor_scalar(place[:, 2, :], place[:, 1, :], ROUNDER, None, ALU.subtract))
            link(v.scalar_tensor_tensor(place[:, 3, :], place[:, 2, :], -float(P), place[:, 0, :], ALU.mult, ALU.add))
            tiles_of = [P, PAIRS, SLOT_TILES]
            link(v.tensor_tensor(claim[:, :, 0, :], place[:, 2, :].unsqueeze(2).broadcast_to(tiles_of),
                                 lane[:, 0:SLOT_TILES].unsqueeze(1).broadcast_to(tiles_of), ALU.is_equal))
            link(v.tensor_tensor(claim[:, :, 1, :], rs[:, 6:8, :].rearrange("p k t -> p (k t)").unsqueeze(2).broadcast_to(tiles_of),
                                 claim[:, :, 0, :], ALU.mult))
            v.tensor_tensor(claim[:, :, 0, :], pair_no.unsqueeze(2).broadcast_to(tiles_of),
                            claim[:, :, 0, :], ALU.mult).then_inc(me["claim"], 1)
            for n in range(0, PAIRS, LANE_PIECE):
                v.tensor_tensor(lane_of[:, n:n + LANE_PIECE, :],
                                place[:, 3, n:n + LANE_PIECE].unsqueeze(2).broadcast_to([P, LANE_PIECE, P]),
                                lane.unsqueeze(1).broadcast_to([P, LANE_PIECE, P]), ALU.is_equal).then_inc(me["lanes"], 1)
            own_of = [1, SLOT_TILES, E - 1]
            link(v.tensor_tensor(own[:, 0, :, 0:E - 1], begin[0:1, 1:].unsqueeze(1).broadcast_to(own_of),
                                 lane[0:1, 0:SLOT_TILES].unsqueeze(2).broadcast_to(own_of), ALU.is_le))
            link(v.tensor_reduce(expert_f[:, :], own[:, 0, :, 0:E - 1], AX_X, ALU.add))
            v.tensor_copy(expert[:, :], expert_f[:, :]).then_inc(me["expert"], 1)
            dve.wait_ge(me["slots"], m + 1)
            link(v.tensor_copy(slot[:, 0:2, :], ps[:, 2, 0:2 * SLOT_TILES].rearrange("p (k n) -> p k n", k=2)))
            link(v.tensor_scalar(slot[:, 2, :], slot[:, 0, :], TILES * P + 0.5, -float(TILES * P), ALU.is_gt, ALU.mult))
            link(v.tensor_tensor(slot[:, 3, :], slot[:, 0, :], slot[:, 2, :], ALU.add))
            link(v.tensor_scalar(slot[:, 3, :], slot[:, 3, :], -1.0, 0.0, ALU.add, ALU.max))
            v.tensor_copy(source[:, :], slot[:, 3, :]).then_inc(me["source"], 1)
            link(v.tensor_scalar(slot[:, 4, :], slot[:, 0, :], 0.5, None, ALU.is_lt))
            link(v.tensor_tensor(slot[:, 4, :], slot[:, 4, :], spare_row, ALU.mult))
            link(v.scalar_tensor_tensor(slot[:, 5, :], slot[:, 0, :], -1.0, slot[:, 4, :], ALU.add, ALU.add))
            v.tensor_copy(target[:, :], slot[:, 5, :]).then_inc(me["target"], 1)
            assert step[0] == ROUTE_STEPS

        def moe_front_scalar(act, s, m, turn):
            norm_scalar(act, turn)

            def front(b, par):
                two_before(act, s["lg"], b)
                front_scalar(act, s, b, par)
            batches(act, front, nothing, nothing)
            act.wait_ge(me["rt"], m * ROUTE_STEPS + ROUTE_DIFF)
            nc.scalar.activation(rs[:, 4, :], rs[:, 3, :], ACT.Exp).then_inc(me["exp"], 1)

        def moe_front_tensor(pe, s, before):
            pe.wait_ge(*before)

            def heavy(b, par):
                pe.wait_ge(s["xT"], b + 1)
                two_before(pe, s["lgT"], b)
                nc.tensor.matmul(ps[:, 2 + par, 0:E], xT[:, par, 1:P + 1], gateT[:, :], start=True, stop=True)
                nc.tensor.matmul(ps[:, 2 + par, E:2 * E], xT[:, par, P + 1:S + 1], gateT[:, :],
                                 start=True, stop=True).then_inc(s["lg"], 1)
            batches(pe, lambda b, par: front_tensor(pe, s, b, par), heavy, nothing)

        def dispatch_tensor(pe, s, m):
            pe.wait_ge(me["both"], m + 1)
            pe.wait_ge(s["xT"], B)
            taken = rt[:, 5].rearrange("p t e -> p (t e)")
            nc.tensor.matmul(ps[:, 0, 0:TILES * E], before_me, taken, start=True, stop=True)
            nc.tensor.matmul(ps[:, 1, 0:TILES * E], all_ones[:, :], taken, start=True, stop=True).then_inc(me["count"], 1)
            pe.wait_ge(s["lgT"], B)
            pe.wait_ge(me["claim"], m + 1)
            for n in range(PAIRS):
                if n % LANE_PIECE == 0:
                    pe.wait_ge(me["lanes"], (m * PAIRS + n) // LANE_PIECE + 1)
                last = nc.tensor.matmul(ps[:, 2, 0:2 * SLOT_TILES], lane_of[:, n, :],
                                        claim[:, n].rearrange("p k n -> p (k n)"), start=(n == 0), stop=(n == PAIRS - 1))
            last.then_inc(me["slots"], 1)

        def keep_tokens(sp, s, kept):
            for b in range(B):
                sp.wait_ge(s["xn"], (b + 1) * TPB)
                sp.dma_start(kept[b * S:(b + 1) * S, :].rearrange("(t p) d -> p t d", p=P),
                             xn[:, b % 2]).then_inc(kept_done[b % 2], 16)

        def slot_tiles(eng, step, drain, peel=1, spare=0):
            end = (SLOT_TILES - spare) // 2
            for n in range(2 * peel):
                step(n, n % 2)
            with eng.Fori(peel, end) as i:
                step(i * 2, 0)
                step(i * 2 + 1, 1)
            for n in range(end * 2, SLOT_TILES):
                step(n, n % 2)
            drain()

        def there(n, back):
            return not isinstance(n, int) or n >= back

        def moved(n, par, m):
            return m * 16 * ((SLOT_TILES + 1 - par) // 2) + (n - par + 2) * 8

        def after_moved(eng, sem, n, par, m):
            if not isinstance(n, int) or n >= 0:
                eng.wait_ge(sem[par], moved(n, par, m))

        AHEAD = 3
        BEHIND = 5

        def moe_pool(pool, s, m, kept, back):
            for par in range(2):
                pool.wait_ge(kept_done[par], (m + 1) * 16 * B // 2)
            pool.wait_ge(me["source"], m + 1)
            pool.wait_ge(me["target"], m + 1)

            def wait_taken(k, n):
                after(pool, turned[k], m * SLOT_TILES + n)
                nc.gpsimd.tensor_tensor(pool_turn[:, k:k + 1], ones[:, 0:1], ones[:, 0:1], ALU.add).then_inc(turned[k], 1)

            def gather(n, par):
                after(pool, me["xg_ps"], m * SLOT_TILES + n - 1)
                pool.wait_ge(me["source_now"], m * SLOT_TILES + n + 1)
                wait_taken(0, n)
                nc.gpsimd.indirect_dma_start(xg[:, par, :], None, kept,
                                             bass.IndirectOffsetOnAxis(ap=source_now[:, par, :], axis=0)).then_inc(gathered[par], 16)

            def scatter(n, par):
                pool.wait_ge(me["target_now"], m * SLOT_TILES + n + 1)
                pool.wait_ge(me["ys"], m * SLOT_TILES + n + 1)
                wait_taken(1, n)
                nc.gpsimd.indirect_dma_start(back, bass.IndirectOffsetOnAxis(ap=target_now[:, par, :], axis=0),
                                             ys[:, par, :], None).then_inc(scattered[par], 16)

            def step(n, par):
                gather(n, par)
                if there(n, BEHIND):
                    scatter(n - BEHIND, 1 - par)

            def drain():
                for n in range(SLOT_TILES - BEHIND, SLOT_TILES):
                    scatter(n, n % 2)
            slot_tiles(pool, step, drain, peel=3)

        def moe_tensor(pe, m):
            pe.wait_ge(me["expert"], m + 1)
            pe.wait_ge(me["source"], m + 1)

            def expert_of(n):
                return pe.value_load(expert[0:1, ds(n, 1)], min_val=0, max_val=E - 1)

            def turn_tokens(n, par):
                pe.wait_ge(gathered[par], moved(n, par, m))
                after(pe, me["xs"], m * SLOT_TILES + n)
                nc.tensor.transpose(ps[:, 7, 0:P], xg[:, par, :], ident).then_inc(me["xg_ps"], 1)

            def gate_up(n, par):
                e = expert_of(n)
                pe.wait_ge(me["xs"], m * SLOT_TILES + n + 1)
                after(pe, me["h"], m * SLOT_TILES + n - 1)
                nc.tensor.matmul(ps[:, 2 * par, 0:I], xs[:, par, :], W1[:, e, :], start=True, stop=True)
                nc.tensor.matmul(ps[:, 2 * par + 1, 0:I], xs[:, par, :], W3[:, e, :], start=True,
                                 stop=True).then_inc(me["gu"], 1)

            def turn_hidden(n, par):
                pe.wait_ge(me["h"], m * SLOT_TILES + n + 1)
                after(pe, me["hT"], m * SLOT_TILES + n - 1)
                for c in range(NCH):
                    last = nc.tensor.transpose(ps[0:IC, 4 + par, c * P:(c + 1) * P],
                                               hb[:, par, c * IC:(c + 1) * IC], ident)
                last.then_inc(me["hT_ps"], 1)

            def down(n, par):
                e = expert_of(n)
                pe.wait_ge(me["hT"], m * SLOT_TILES + n + 1)
                after(pe, me["ys"], m * SLOT_TILES + n)
                for c in range(NCH):
                    last = nc.tensor.matmul(ps[:, 6, 0:D], hT[:, par, c, :], W2[:, e, c, :],
                                            start=(c == 0), stop=(c == NCH - 1))
                last.then_inc(me["y"], 1)

            def step(n, par):
                if isinstance(n, int) and n == 0:
                    turn_tokens(0, 0)
                gate_up(n, par)
                if not isinstance(n, int) or n + 1 < SLOT_TILES:
                    turn_tokens(n + 1, 1 - par)
                if there(n, 1):
                    turn_hidden(n - 1, 1 - par)
                if there(n, 2):
                    down(n - 2, par)

            def drain():
                n = SLOT_TILES
                turn_hidden(n - 1, (n - 1) % 2)
                down(n - 2, n % 2)
                down(n - 1, (n - 1) % 2)
            slot_tiles(pe, step, drain, peel=2)

        def moe_scalar(act, m):
            def silu(n, par):
                act.wait_ge(me["gu"], m * SLOT_TILES + n + 1)
                after(act, me["h"], m * SLOT_TILES + n - 1)
                nc.scalar.activation(sg[:, par, :], ps[:, 2 * par, 0:I], ACT.Silu).then_inc(me["sg"], 1)

            def evict_hidden(n, par):
                act.wait_ge(me["hT_ps"], m * SLOT_TILES + n + 1)
                after(act, me["y"], m * SLOT_TILES + n - 1)
                nc.scalar.copy(hT[:, par].rearrange("p c t -> p (c t)"), ps[0:IC, 4 + par, :]).then_inc(me["hT"], 1)

            def evict_output(n, par):
                act.wait_ge(me["y"], m * SLOT_TILES + n + 1)
                after_moved(act, scattered, n - 2, par, m)
                nc.scalar.mul(ys[:, par, :], ps[:, 6, 0:D], 0.5).then_inc(me["ys"], 1)

            def step(n, par):
                silu(n, par)
                if there(n, 1):
                    evict_hidden(n - 1, 1 - par)
                if there(n, 2):
                    evict_output(n - 2, par)

            def drain():
                n = SLOT_TILES
                evict_hidden(n - 1, (n - 1) % 2)
                evict_output(n - 2, n % 2)
                evict_output(n - 1, (n - 1) % 2)
            slot_tiles(act, step, drain, peel=2)

        def moe_vector(dve, s, m):
            def evict_tokens(n, par):
                dve.wait_ge(me["xg_ps"], m * SLOT_TILES + n + 1)
                nc.vector.tensor_copy(xs[:, par, :], ps[:, 7, 0:P]).then_inc(me["xs"], 1)

            def hidden(n, par):
                dve.wait_ge(me["sg"], m * SLOT_TILES + n + 1)
                after(dve, me["hT_ps"], m * SLOT_TILES + n - 1)
                nc.vector.scalar_tensor_tensor(hb[:, par, :], sg[:, par, :], slot[:, 1, ds(n, 1)],
                                               ps[:, 2 * par + 1, 0:I], ALU.mult, ALU.mult).then_inc(me["h"], 1)

            def index_source(n, par):
                after_moved(dve, gathered, n - 2, par, m)
                nc.vector.tensor_copy(source_now[:, par, :], source[:, ds(n, 1)]).then_inc(me["source_now"], 1)

            def index_target(n, par):
                after_moved(dve, scattered, n - 2, par, m)
                nc.vector.tensor_copy(target_now[:, par, :], target[:, ds(n, 1)]).then_inc(me["target_now"], 1)

            def step(n, par):
                if isinstance(n, int) and n == 0:
                    for k in range(AHEAD):
                        index_source(k, k % 2)
                    evict_tokens(0, 0)
                if not isinstance(n, int) or n + 1 < SLOT_TILES:
                    evict_tokens(n + 1, 1 - par)
                hidden(n, par)
                if not isinstance(n, int) or n + AHEAD < SLOT_TILES:
                    index_source(n + AHEAD, 1 - par)
                if there(n, 2):
                    index_target(n - 2, par)

            def drain():
                for n in range(SLOT_TILES - 2, SLOT_TILES):
                    index_target(n, n % 2)
            slot_tiles(dve, step, drain, peel=2, spare=AHEAD)

            for n in range(0, TILES, KEEP):
                dve.wait_ge(fetched[n // KEEP], 16 * TOPK * (m + 1))
                both = yback[:, :, n:n + KEEP, :]
                nc.vector.tensor_tensor(both[:, 0], both[:, 0], both[:, 1], ALU.add).then_inc(s["sum"], 1)
                dve.wait_ge(s["sum"], n // KEEP + 1)
                nc.vector.tensor_tensor(X[:, n:n + KEEP, :], X[:, n:n + KEEP, :], both[:, 0], ALU.add).then_inc(s["x_done"], 1)
                for t in range(n, n + KEEP):
                    tile_stats(dve, s, t, n // KEEP + 1)

        def fetch_outputs(sp, s, m, back):
            for n in (SLOT_TILES - 2, SLOT_TILES - 1):
                sp.wait_ge(scattered[n % 2], moved(n, n % 2, m))
            by_token = back[0:PAIRS * P, :].rearrange("(k t p) d -> p k t d", k=TOPK, p=P)
            for n in range(0, TILES, KEEP):
                for k in range(TOPK):
                    sp.dma_start(yback[:, k, n:n + KEEP, :], by_token[:, k, n:n + KEEP, :]).then_inc(fetched[n // KEEP], 16)

        def rwkv_vector(dve, s, turn, before, stats):
            norm_vector(dve, turn, before)

            def heavy(b, par):
                dve.wait_ge(s["xT"], b + 1)
                two_before(dve, s["rk"], b)
                for k in range(2):
                    nc.vector.tensor_scalar(mixed[:, par, 2 + k, :], xT[:, par, 0:S], omu[:, k:k + 1], None,
                                            ALU.mult).then_inc(s["shift"], 1)
                dve.wait_ge(s["shift"], b * 2 + 2)
                for k, mu in ((0, "L1_ffn_mu_r"), (1, "L1_ffn_mu_k")):
                    nc.vector.scalar_tensor_tensor(mixed[:, par, k, :], xT[:, par, 1:S + 1], vec(mu),
                                                   mixed[:, par, 2 + k, :], ALU.mult, ALU.add).then_inc(s["mix"], 1)

            def tail(b, par):
                dve.wait_ge(s["v"], b + 1)
                dve.wait_ge(s["rgate"], b + 1)
                nc.vector.scalar_tensor_tensor(rv[:, par, :], ps[:, 6 + par, 0:S], 0.5, rgate[:, par, :],
                                               ALU.mult, ALU.mult).then_inc(s["rv"], 1)
                dve.wait_ge(s["rv"], b + 1)
                update_batch(dve, s, b, rv[:, par, :], stats)
            batches(dve, lambda b, par: front_vector(dve, s, b, par), heavy, tail)

        def rwkv_scalar(act, s, turn):
            norm_scalar(act, turn)

            def front(b, par):
                two_before(act, s["mix"], b, 2)
                front_scalar(act, s, b, par)

            def heavy(b, par):
                act.wait_ge(s["rk"], b + 1)
                two_before(act, s["rv"], b)
                nc.scalar.activation(rgate[:, par, :], ps[:, 2 + par, 0:S], ACT.Sigmoid).then_inc(s["rgate"], 1)
                two_before(act, s["v"], b)
                nc.scalar.activation(kact[:, par, 0, :], ps[:, 4 + par, 0:S], ACT.Relu).then_inc(s["krelu"], 1)
                act.wait_ge(s["krelu"], b + 1)
                nc.scalar.activation(kact[:, par, 1, :], kact[:, par, 0, :], ACT.Square).then_inc(s["kact"], 1)
            batches(act, front, heavy, nothing)

        def rwkv_tensor(pe, s, before):
            pe.wait_ge(*before)

            def heavy(b, par):
                pe.wait_ge(s["mix"], b * 2 + 2)
                two_before(pe, s["kact"], b)
                for j in range(TPB):
                    nc.tensor.matmul(ps[:, 2 + par, j * P:(j + 1) * P], mixed[:, par, 0, j * P:(j + 1) * P],
                                     w("L1_ffn_W_r"), start=True, stop=True)
                nc.tensor.matmul(ps[:, 4 + par, 0:S], w("L1_ffn_W_k"), mixed[:, par, 1, :], start=True,
                                 stop=True).then_inc(s["rk"], 1)

            def tail(b, par):
                pe.wait_ge(s["kact"], b + 1)
                for j in range(TPB):
                    last = nc.tensor.matmul(ps[:, 6 + par, j * P:(j + 1) * P], kact[:, par, 1, j * P:(j + 1) * P],
                                            w("L1_ffn_W_v"), start=True, stop=True)
                last.then_inc(s["v"], 1)
            batches(pe, lambda b, par: front_tensor(pe, s, b, par), heavy, tail)

        UNITS = {"L0_attn_": TPB, "L1_attn_": TPB * TPB}
        NBUF = 4

        def overlapped(eng, prologue, body, epilogue):
            prologue()
            for b in range(3):
                body(b, b % 2, False)
            with eng.Fori(1, B // 2 - 1) as i:
                body(i * 2 + 1, 1, False)
                body(i * 2 + 2, 0, False)
            body(B - 1, 1, True)
            epilogue()

        def has(b, back):
            return not isinstance(b, int) or b >= back

        def attn_tokens_tensor(pe, s, l, b, par):
            after(pe, s["vm"], b * TPB)
            if l == L0:
                after(pe, s["vfull"], b)
                after(pe, s["kd"], b)
            front_tensor(pe, s, b, par, 2)

        def attn_qk_tensor(pe, s, l, b, par):
            pe.wait_ge(s["xT"], b + 1)
            after(pe, s["q"], b)
            after(pe, s["k"], b)
            x = xT[:, par, 1:S + 1]
            nc.tensor.matmul(ps[:, 1, 0:S], w(l + "Wq"), x, start=True, stop=True)
            nc.tensor.matmul(ps[:, 1, S:2 * S], w(l + "Wk"), x, start=True, stop=True).then_inc(s["qk_ps"], 1)

        def attn_v_tensor(pe, s, l, b, par):
            pe.wait_ge(s["xT"], b + 1)
            for j in range(TPB):
                last = nc.tensor.matmul(ps[:, 2, j * P:(j + 1) * P], xT[:, par, 1 + j * P:1 + (j + 1) * P], w(l + "Wv"),
                                        start=True, stop=True)
            if l == L0:
                last = nc.tensor.matmul(ps[:, 2, 2 * P:3 * P], xT[:, par, 1:1 + P], w(l + "Wk"), start=True, stop=True)
            last.then_inc(s["v_ps"], 1)

        def attn_tokens_scalar(act, s, b, par):
            two_before(act, s["v_ps"], b)
            front_scalar(act, s, b, par, 2)

        def attn_qk_scalar(act, s, l, b, par):
            act.wait_ge(s["qk_ps"], b + 1)
            two_before(act, s["qm"], b, HR)
            if l == L0:
                two_before(act, s["qd"], b)
            nc.scalar.activation(qT[:, par, :], ps[:, 1, 0:S], ACT.Identity, bias=vec(l + "bq")).then_inc(s["q"], 1)
            two_before(act, s["sc"], b, UNITS[l] * HR)
            nc.scalar.activation(kT[:, par, :], ps[:, 1, S:2 * S], ACT.Identity, bias=vec(l + "bk")).then_inc(s["k"], 1)

        def attn_out_scalar(act, s, l, b, par):
            act.wait_ge(s["av"], b * UNITS[l] + UNITS[l])
            two_before(act, s["yps"], b)
            nc.scalar.copy(oT[:, par, :], ps[:, 7, 0:S]).then_inc(s["oT"], 1)

        def queries_by_head(pool, s, l, b, par, parts):
            pool.wait_ge(s["q"], b + 1)
            two_before(pool, s["sc"], b, UNITS[l] * HR)
            for r in parts:
                heads = head_of.rearrange("p (g r) -> p r g", r=HR)[:, r, :]
                nc.gpsimd.tensor_tensor(Qm[:, par, r], qT[:, par, :].unsqueeze(1).broadcast_to([P, HG, S]),
                                        heads.unsqueeze(2).broadcast_to([P, HG, S]), ALU.mult).then_inc(s["qm"], 1)

        def values_vector(dve, s, l, b, par):
            dve.wait_ge(s["v_ps"], b + 1)
            two_before(dve, s["av"], b, UNITS[l])
            bias = row(l + "bv")
            for j in range(TPB):
                dst = Vm[:, par, j].rearrange("p (g r) (q d) -> p g (r q) d", r=HR, q=HR)[:, :, 0:HR * HR:HR + 1, :]
                src = ps[:, 2, j * P:(j + 1) * P].rearrange("p (g r d) -> p g r d", g=HG, r=HR)
                nc.vector.tensor_tensor(dst, src, bias.rearrange("p (g r d) -> p g r d", g=HG, r=HR),
                                        ALU.add).then_inc(s["vm"], 1)
            if l == L0:
                nc.vector.tensor_tensor(Vfull[:, par, :], ps[:, 2, 0:P], bias, ALU.add).then_inc(s["vfull"], 1)
                nc.vector.scalar_tensor_tensor(Kd[:, par, :], ps[:, 2, 2 * P:3 * P], k_decay, bk_decay[:, :],
                                               ALU.mult, ALU.add).then_inc(s["kd"], 1)

        def weigh_values(pe, s, par, keys, queries, buf, first, ready):
            for r in range(HR):
                pe.wait_ge(ready[r][0], ready[r][1])
                for g in range(HG):
                    last = nc.tensor.matmul(ps[g * MW:(g + 1) * MW, 7, queries * P:(queries + 1) * P],
                                            Vm[:, par, keys, g * HR + r, :], att[:, buf, r, g, :],
                                            start=(first and r == 0), stop=(r == HR - 1),
                                            skip_group_check=True)
            last.then_inc(s["av"], 1)

        L0 = "L0_attn_"

        def attn0_tensor(pe, s, before):
            def state(b, par):
                after(pe, s["oT"], b)
                pe.wait_ge(s["kd"], b + 1)
                pe.wait_ge(s["vfull"], b + 1)
                nc.tensor.matmul(ps[:, 7, S:S + P], Kd[:, par, :], Vfull[:, par, :], start=True,
                                 stop=True).then_inc(s["st_ps"], 1)

            def values(b, par, u):
                n = b * TPB + u
                pe.wait_ge(s["vm"], b * TPB + TPB)
                pe.wait_ge(s["st"], b + 1)
                if u == 1:
                    pe.wait_ge(s["qd"], b + 1)
                    nc.tensor.matmul(ps[:, 7, P:2 * P], St[:, par, :], qD[:, par, :], start=True, stop=False,
                                     skip_group_check=True)
                weigh_values(pe, s, par, u, u, 2 * par + u, u == 0, [(s["at"], n * HR + r + 1) for r in range(HR)])

            def output(b, par):
                pe.wait_ge(s["oT"], b + 1)
                after(pe, s["x_done"], b)
                nc.tensor.matmul(ps[:, 0, 0:S], w(L0 + "Wo"), oT[:, par, :], start=True, stop=True).then_inc(s["yps"], 1)

            def head_mean(b):
                pe.wait_ge(s["ym"], b + 1)
                nc.tensor.matmul(ps[:, 0, S:S + 1], block_avg[:, :], gst[:, 2:3], start=True, stop=True).then_inc(s["gm_ps"], 1)

            def head_variance(b):
                pe.wait_ge(s["dev"], b + 1)
                nc.tensor.matmul(ps[:, 0, S:S + 1], block_avg[:, :], gst[:, 4:5], start=True, stop=True).then_inc(s["gv_ps"], 1)

            def turn_output(b):
                pe.wait_ge(s["yn"], b + 1)
                nc.tensor.transpose(ps[:, 0, 0:P], yT[:, 0:P], ident)
                nc.tensor.transpose(ps[:, 0, P:S], yT[:, P:S], ident).then_inc(s["ynT"], 1)

            def prologue():
                pe.wait_ge(*before)
                attn_tokens_tensor(pe, s, L0, 0, 0)
                attn_qk_tensor(pe, s, L0, 0, 0)
                attn_v_tensor(pe, s, L0, 0, 0)

            def body(b, par, last):
                def scores(u, r):
                    pe.wait_ge(s["qm"], b * HR + r + 1)
                    pe.wait_ge(s["k"], b + 1)
                    after(pe, s["at"], (b * TPB + u - 1) * HR + r + 1)
                    nc.tensor.matmul(ps[:, 3 + r, :], kT[:, par, u * P:(u + 1) * P],
                                     Qm[:, par, r, :, u * P:(u + 1) * P], start=True, stop=True).then_inc(s["sc"], 1)
                scores(0, 0)
                if has(b, 1):
                    values(b - 1, 1 - par, 1)
                scores(0, 1)
                if not last:
                    attn_tokens_tensor(pe, s, L0, b + 1, 1 - par)
                if has(b, 2):
                    turn_output(b - 2)
                scores(0, 2)
                state(b, par)
                scores(0, 3)
                if has(b, 1):
                    output(b - 1, 1 - par)
                if not last:
                    attn_qk_tensor(pe, s, L0, b + 1, 1 - par)
                scores(1, 0)
                if not last:
                    attn_v_tensor(pe, s, L0, b + 1, 1 - par)
                scores(1, 1)
                if has(b, 1):
                    head_mean(b - 1)
                scores(1, 2)
                scores(1, 3)
                values(b, par, 0)
                if has(b, 1):
                    head_variance(b - 1)

            def epilogue():
                values(B - 1, 1, 1)
                turn_output(B - 2)
                output(B - 1, 1)
                head_mean(B - 1)
                head_variance(B - 1)
                turn_output(B - 1)
            overlapped(pe, prologue, body, epilogue)

        def attn0_scalar(act, s, turn):
            norm_scalar(act, turn)

            def root(b):
                act.wait_ge(s["gv"], b + 1)
                nc.scalar.activation(gst[:, 6:7], gst[:, 5:6], ACT.Sqrt).then_inc(s["groot"], 1)

            def prologue():
                attn_tokens_scalar(act, s, 0, 0)
                attn_qk_scalar(act, s, L0, 0, 0)

            def body(b, par, last):
                if has(b, 1):
                    attn_out_scalar(act, s, L0, b - 1, 1 - par)
                if not last:
                    attn_tokens_scalar(act, s, b + 1, 1 - par)
                    attn_qk_scalar(act, s, L0, b + 1, 1 - par)
                if has(b, 1):
                    root(b - 1)

            def epilogue():
                attn_out_scalar(act, s, L0, B - 1, 1)
                root(B - 1)
            overlapped(act, prologue, body, epilogue)

        def attn0_pool(pool, s):
            def body(b, par, last):
                if not last:
                    queries_by_head(pool, s, L0, b + 1, 1 - par, range(HR))
            overlapped(pool, lambda: queries_by_head(pool, s, L0, 0, 0, range(HR)), body, lambda: None)

        def attn0_vector(dve, s, turn, before):
            norm_vector(dve, turn, before)
            v = nc.vector
            col = [gst[:, n:n + 1] for n in range(10)]

            def weights(b, par, u, r):
                n = b * TPB + u
                dve.wait_ge(s["sc"], n * HR + r + 1)
                after(dve, s["av"], n - NBUF + 1)
                v.tensor_tensor(att[:, 2 * par + u, r], ps[:, 3 + r, :].rearrange("p (g q) -> p g q", g=HG),
                                decay_mask.unsqueeze(1).broadcast_to([P, HG, P]), ALU.mult).then_inc(s["at"], 1)

            def channel_stats(b):
                dve.wait_ge(s["yps"], b + 1)
                v.bn_stats(gbn[:, :], ps[:, 0, 0:S]).then_inc(s["ymv"], 1)
                dve.wait_ge(s["ymv"], b * 5 + 1)
                v.tensor_tensor(col[0], gbn[:, 1:2], gbn[:, 4:5], ALU.add).then_inc(s["ymv"], 1)
                dve.wait_ge(s["ymv"], b * 5 + 2)
                v.scalar_tensor_tensor(col[2], col[0], 0.5, vec(L0 + "bo"), ALU.mult, ALU.add).then_inc(s["ym"], 1)
                v.tensor_tensor(col[1], gbn[:, 1:2], gbn[:, 4:5], ALU.subtract).then_inc(s["ymv"], 1)
                v.tensor_tensor(col[7], gbn[:, 2:3], gbn[:, 5:6], ALU.add).then_inc(s["ymv"], 1)
                dve.wait_ge(s["ymv"], b * 5 + 4)
                v.scalar_tensor_tensor(col[8], col[1], 0.25, col[1], ALU.mult, ALU.mult).then_inc(s["ymv"], 1)
                dve.wait_ge(s["ymv"], b * 5 + 5)
                v.scalar_tensor_tensor(col[1], col[7], 1.0 / S, col[8], ALU.mult, ALU.add).then_inc(s["yvar"], 1)

            def deviation(b):
                dve.wait_ge(s["gm_ps"], b + 1)
                v.tensor_tensor(col[3], col[2], ps[:, 0, S:S + 1], ALU.subtract).then_inc(s["gm"], 1)
                dve.wait_ge(s["gm"], b + 1)
                dve.wait_ge(s["yvar"], b + 1)
                v.scalar_tensor_tensor(col[4], col[3], col[3], col[1], ALU.mult, ALU.add).then_inc(s["dev"], 1)

            def scale_output(b):
                dve.wait_ge(s["gv_ps"], b + 1)
                v.tensor_scalar(col[5], ps[:, 0, S:S + 1], EPS, None, ALU.add).then_inc(s["gv"], 1)
                v.scalar_tensor_tensor(col[9], col[0], -0.5, col[3], ALU.mult, ALU.add).then_inc(s["ab"], 1)
                dve.wait_ge(s["groot"], b + 1)
                v.reciprocal(col[7], col[6]).then_inc(s["grs"], 1)
                dve.wait_ge(s["grs"], b + 1)
                v.tensor_tensor(col[8], col[7], vec(L0 + "gamma"), ALU.mult).then_inc(s["ab"], 1)
                dve.wait_ge(s["ab"], b * 3 + 2)
                v.scalar_tensor_tensor(col[2], col[8], col[9], vec(L0 + "beta"), ALU.mult, ALU.add).then_inc(s["ab"], 1)
                dve.wait_ge(s["ab"], b * 3 + 3)
                v.tensor_scalar(yT[:, :], ps[:, 0, 0:S], col[8], col[2], ALU.mult, ALU.add).then_inc(s["yn"], 1)

            def update(b):
                dve.wait_ge(s["ynT"], b + 1)
                update_batch(dve, s, b, ps[:, 0, 0:S])

            def prologue():
                front_vector(dve, s, 0, 0)
                values_vector(dve, s, L0, 0, 0)

            def body(b, par, last):
                if not last:
                    front_vector(dve, s, b + 1, 1 - par)
                weights(b, par, 0, 0)
                dve.wait_ge(s["q"], b + 1)
                two_before(dve, s["av"], b, TPB)
                v.tensor_tensor(qD[:, par, :], qT[:, par, P:S], q_decay, ALU.mult).then_inc(s["qd"], 1)
                weights(b, par, 0, 1)
                if has(b, 2):
                    update(b - 2)
                weights(b, par, 0, 2)
                dve.wait_ge(s["st_ps"], b + 1)
                v.tensor_tensor(St[:, par, :], ps[:, 7, S:S + P], block_diag, ALU.mult).then_inc(s["st"], 1)
                weights(b, par, 0, 3)
                weights(b, par, 1, 0)
                if has(b, 1):
                    channel_stats(b - 1)
                weights(b, par, 1, 1)
                if not last:
                    values_vector(dve, s, L0, b + 1, 1 - par)
                weights(b, par, 1, 2)
                if has(b, 1):
                    deviation(b - 1)
                weights(b, par, 1, 3)
                if has(b, 1):
                    scale_output(b - 1)

            def epilogue():
                update(B - 2)
                channel_stats(B - 1)
                deviation(B - 1)
                scale_output(B - 1)
                update(B - 1)
            overlapped(dve, prologue, body, epilogue)

        L1 = "L1_attn_"
        NU = UNITS[L1]
        DVE_PARTS = 1
        POOL_PARTS = HR - DVE_PARTS

        def attn1_tensor(pe, s, before):
            def values(b, par, u):
                n = b * NU + u
                if u == 0:
                    after(pe, s["oT"], b)
                    pe.wait_ge(s["vm"], b * TPB + TPB)
                ready = [(s["at"], n * DVE_PARTS + r + 1) if r < DVE_PARTS else
                         (s["at_pool"], n * POOL_PARTS + r - DVE_PARTS + 1) for r in range(HR)]
                weigh_values(pe, s, par, u % TPB, u // TPB, u, u % TPB == 0, ready)

            def output(b, par):
                pe.wait_ge(s["oT"], b + 1)
                after(pe, s["x_done"], b)
                for j in range(TPB):
                    nc.tensor.matmul(ps[:, 0, j * P:(j + 1) * P], oT[:, par, j * P:(j + 1) * P], w(L1 + "Wo"),
                                     start=True, stop=False)
                    last = nc.tensor.matmul(ps[:, 0, j * P:(j + 1) * P], ones[:, :], row(L1 + "bo")[0:1, :],
                                            start=False, stop=True)
                last.then_inc(s["yps"], 1)

            def prologue():
                pe.wait_ge(*before)
                attn_tokens_tensor(pe, s, L1, 0, 0)
                attn_qk_tensor(pe, s, L1, 0, 0)
                attn_v_tensor(pe, s, L1, 0, 0)

            def scores(b, par, u, half):
                n = b * NU + u
                keys, q0 = u % TPB * P, u // TPB * P + half * QH
                for k in range(2):
                    pe.wait_ge(s["qm"], b * HR + 2 * k + 2)
                    pe.wait_ge(s["k"], b + 1)
                    after(pe, s["ex"], (n - 1) * HR + 2 * half + k + 1)
                    nc.tensor.matmul(ps[:, 3 + 2 * half + k, :], kT[:, par, keys:keys + P],
                                     Qm[:, par, 2 * k:2 * k + 2, :, q0:q0 + QH].rearrange("p r g q -> p (r g) q"),
                                     start=True, stop=True, skip_group_check=True).then_inc(s["sc"], 1)

            def subtract(n, half):
                pe.wait_ge(s["mx"], n * 2 + half + 1)
                for k in range(2):
                    nc.tensor.matmul(ps[:, 3 + 2 * half + k, :], minus_i[:, :],
                                     amax[:, half, :].unsqueeze(1).broadcast_to([P, 2 * HG, QH]),
                                     start=False, stop=True, skip_group_check=True).then_inc(s["sub"], 1)

            def body(b, par, last):
                for u in range(NU):
                    n = b * NU + u
                    scores(b, par, u, 0)
                    if has(b, 1) or u:
                        subtract(n - 1, 1)
                    if u == 0 and not last:
                        attn_tokens_tensor(pe, s, L1, b + 1, 1 - par)
                    if u == 1 and not last:
                        attn_v_tensor(pe, s, L1, b + 1, 1 - par)
                    if u == 3 and has(b, 1):
                        output(b - 1, 1 - par)
                    scores(b, par, u, 1)
                    subtract(n, 0)
                    if u >= 2:
                        values(b, par, u - 2)
                    elif has(b, 1):
                        values(b - 1, 1 - par, u + 2)
                    if u == 0 and not last:
                        attn_qk_tensor(pe, s, L1, b + 1, 1 - par)

            def epilogue():
                subtract(B * NU - 1, 1)
                values(B - 1, 1, 2)
                values(B - 1, 1, 3)
                output(B - 1, 1)
            overlapped(pe, prologue, body, epilogue)

        def attn1_scalar(act, s, turn):
            norm_scalar(act, turn)

            def prologue():
                attn_tokens_scalar(act, s, 0, 0)
                attn_qk_scalar(act, s, L1, 0, 0)

            def round_scores(n, half):
                after(act, s["mx"], n * 2 + half - 1)
                for k in range(2):
                    act.wait_ge(s["sc"], n * HR + 2 * half + k + 1)
                    nc.scalar.copy(sc16[:, half, k, :], ps[:, 3 + 2 * half + k, :]).then_inc(s["sc16"], 1)

            def exponentials(n, u, half):
                after(act, s["av"], n - NBUF + 1)
                for k in range(2):
                    act.wait_ge(s["sub"], n * HR + 2 * half + k + 1)
                    nc.scalar.activation(att[:, u, 2 * k:2 * k + 2, :, half * QH:(half + 1) * QH].rearrange("p r g q -> p (r g) q"),
                                         ps[:, 3 + 2 * half + k, :].rearrange("p (h q) -> p h q", q=QH), ACT.Exp,
                                         scale=SCALE).then_inc(s["ex"], 1)

            def body(b, par, last):
                for u in range(NU):
                    n = b * NU + u
                    round_scores(n, 0)
                    if has(b, 1) or u:
                        exponentials(n - 1, (u - 1) % NBUF, 1)
                    if u == 0 and not last:
                        attn_tokens_scalar(act, s, b + 1, 1 - par)
                    if u == 2 and has(b, 1):
                        attn_out_scalar(act, s, L1, b - 1, 1 - par)
                    round_scores(n, 1)
                    exponentials(n, u, 0)
                    if u == 0 and not last:
                        attn_qk_scalar(act, s, L1, b + 1, 1 - par)

            def epilogue():
                exponentials(B * NU - 1, NBUF - 1, 1)
                attn_out_scalar(act, s, L1, B - 1, 1)
            overlapped(act, prologue, body, epilogue)

        def attn1_pool(pool, s):
            def normalise(b, u):
                pool.wait_ge(s["rden"], b * NU + u + 1)
                for r in range(DVE_PARTS, HR):
                    nc.gpsimd.tensor_tensor(att[:, u, r], att[:, u, r], rden[:, u % 2, :].unsqueeze(1).broadcast_to([P, HG, P]),
                                            ALU.mult).then_inc(s["at_pool"], 1)

            def body(b, par, last):
                for u in range(NU):
                    if not last:
                        queries_by_head(pool, s, L1, b + 1, 1 - par, ((), (0, 1), (2,), (3,))[u])
                    if u:
                        normalise(b, u - 1)
                    elif has(b, 1):
                        normalise(b - 1, NU - 1)
            overlapped(pool, lambda: queries_by_head(pool, s, L1, 0, 0, range(HR)), body, lambda: normalise(B - 1, NU - 1))

        def attn1_vector(dve, s, turn, before):
            norm_vector(dve, turn, before)
            v = nc.vector

            def largest(n, half):
                m = n * 2 + half
                dve.wait_ge(s["sc16"], m * 2 + 2)
                v.tensor_tensor(hmax[:, half, 0:512], sc16[:, half, 0, :], sc16[:, half, 1, :], ALU.max).then_inc(s["hmax"], 1)
                for k, width in ((1, 256), (2, 128)):
                    dve.wait_ge(s["hmax"], m * 3 + k)
                    v.tensor_tensor(hmax[:, half, 0:width], hmax[:, half, 0:width], hmax[:, half, width:2 * width],
                                    ALU.max).then_inc(s["hmax"], 1)
                dve.wait_ge(s["hmax"], m * 3 + 3)
                after(dve, s["sub"], (m - 1) * 2)
                v.tensor_tensor(amax[:, half, :], hmax[:, half, 0:QH], hmax[:, half, QH:2 * QH], ALU.max).then_inc(s["mx"], 1)

            def sum_heads(n, u, half):
                dve.wait_ge(s["ex"], n * HR + 2 * half + 2)
                v.tensor_reduce(den[:, u % 2, half * QH:(half + 1) * QH],
                                att[:, u, :, :, half * QH:(half + 1) * QH].rearrange("p r g q -> p q (r g)"), AX_X,
                                ALU.add).then_inc(s["den"], 1)

            def invert(n, u):
                dve.wait_ge(s["den"], n * 2 + 2)
                after(dve, s["at_pool"], (n - 1) * POOL_PARTS)
                v.reciprocal(rden[:, u % 2, :], den[:, u % 2, :]).then_inc(s["rden"], 1)

            def normalise(n, u):
                dve.wait_ge(s["rden"], n + 1)
                for r in range(DVE_PARTS):
                    v.tensor_tensor(att[:, u, r], att[:, u, r], rden[:, u % 2, :].unsqueeze(1).broadcast_to([P, HG, P]),
                                    ALU.mult).then_inc(s["at"], 1)

            def update(b):
                dve.wait_ge(s["yps"], b + 1)
                update_batch(dve, s, b, ps[:, 0, 0:S])

            def prologue():
                front_vector(dve, s, 0, 0)
                values_vector(dve, s, L1, 0, 0)

            def body(b, par, last):
                if not last:
                    front_vector(dve, s, b + 1, 1 - par)
                for u in range(NU):
                    n = b * NU + u
                    largest(n, 0)
                    if has(b, 1) or u >= 1:
                        sum_heads(n - 1, (u - 1) % NU, 0)
                    if has(b, 1) or u >= 2:
                        normalise(n - 2, (u - 2) % NU)
                    if u == 2 and not last:
                        values_vector(dve, s, L1, b + 1, 1 - par)
                    largest(n, 1)
                    if has(b, 1) or u >= 1:
                        sum_heads(n - 1, (u - 1) % NU, 1)
                        invert(n - 1, (u - 1) % NU)
                    if u == 3 and has(b, 1):
                        update(b - 1)

            def epilogue():
                n = B * NU - 1
                sum_heads(n, NU - 1, 0)
                normalise(n - 1, NU - 2)
                sum_heads(n, NU - 1, 1)
                invert(n, NU - 1)
                normalise(n, NU - 1)
                update(B - 1)
            overlapped(dve, prologue, body, epilogue)

        moe1, moe2, rwkv1, rwkv2 = MO["moe1"], MO["moe2"], RW["rwkv1"], RW["rwkv2"]
        attn0, attn1 = AT["attn0"], AT["attn1"]

        kept = [nc.dram_tensor(f"kept{n}", (TILES * P, D), F32, kind="Internal").ap() for n in range(2)]
        back = [nc.dram_tensor(f"back{n}", ((PAIRS + SLOT_TILES) * P, D), F32, kind="Internal").ap() for n in range(2)]

        block = ctx.enter_context(nc.Block())

        @block.sync
        def _(sp):
            for n in range(4):
                sp.dma_start(X[:, n * 4:(n + 1) * 4, :],
                             io["x"][n * 4 * P:(n + 1) * 4 * P, :].rearrange("(t p) d -> p t d", p=P)).then_inc(ld["x"], 16)
            sp.dma_start(gateT[:, :], io["gateT"]).then_inc(ld["small"], 16)
            sp.dma_start(rows[:, :, :], io["rows"].broadcast_to([P, len(R_NAMES), D])).then_inc(ld["small"], 16)
            sp.dma_start(W1[:, :, :], io["w1"]).then_inc(ld["moe"], 16)
            sp.dma_start(W3[:, :, :], io["w3"]).then_inc(ld["moe"], 16)
            sp.dma_start(W2[:, :, :, :], io["w2"]).then_inc(ld["moe"], 16)
            sp.dma_start(W[:, :, :], io["weights"]).then_inc(ld["w"], 16)
            for n, moe in enumerate((moe1, moe2)):
                keep_tokens(sp, moe, kept[n])
                fetch_outputs(sp, moe, n, back[n])
            for b in range(B):
                sp.wait_ge(rwkv2["x_done"], b + 1)
                sp.dma_start(out[b].rearrange("(t p) d -> p t d", p=P),
                             X[:, b * TPB:(b + 1) * TPB, :]).then_inc(final["stored"], 16)
            sp.wait_ge(final["stored"], 16 * B)

        @block.gpsimd
        def _(pool):
            nc.gpsimd.memset(ones[:, :], 1.0)
            nc.gpsimd.memset(all_ones[:, :], 1.0)
            nc.gpsimd.memset(run[:, :, 0:PAD, :], 0.0)
            nc.gpsimd.memset(xT[:, :, 0:1], 0.0)
            nc.gpsimd.memset(Vm[:, :, :, :, :], 0.0).then_inc(su["zeros"], 1)
            moe_pool(pool, moe1, 0, kept[0], back[0])
            attn0_pool(pool, attn0)
            moe_pool(pool, moe2, 1, kept[1], back[1])
            attn1_pool(pool, attn1)

        @block.vector
        def _(dve):
            dve.wait_ge(ld["const"], 32)
            dve.wait_ge(su["zeros"], 1)
            nc.vector.tensor_scalar(omu[:, :], vecs[:, len(V_NAMES) - 2:], -1.0, 1.0, ALU.mult, ALU.add)
            nc.vector.tensor_scalar(minus_i[:, :], ident, -1.0, None, ALU.mult)
            nc.vector.tensor_scalar(block_avg[:, :], block_diag, 1.0 / HD, None, ALU.mult)
            dve.wait_ge(ld["small"], 32)
            nc.vector.tensor_scalar(bk_decay[:, :], row(L0 + "bk"), k_decay, None, ALU.mult).then_inc(su["consts"], 1)
            dve.wait_ge(su["consts"], 1)
            for t in range(TILES):
                dve.wait_ge(ld["x"], 16 * 4)
                tile_stats(dve, su, t, None)
            moe_front_vector(dve, moe1, 0, 0, (su["stats"], TILES))
            moe_vector(dve, moe1, 0)
            attn0_vector(dve, attn0, 1, (moe1["stats"], TILES))
            moe_front_vector(dve, moe2, 1, 2, (attn0["stats"], TILES))
            moe_vector(dve, moe2, 1)
            rwkv_vector(dve, rwkv1, 3, (moe2["stats"], TILES), True)
            attn1_vector(dve, attn1, 4, (rwkv1["stats"], TILES))
            rwkv_vector(dve, rwkv2, 5, (attn1["stats"], TILES), False)

        @block.scalar
        def _(act):
            act.dma_start(consts[:, :], io["consts"]).then_inc(ld["const"], 16)
            act.dma_start(vecs[:, :], io["vecs"]).then_inc(ld["const"], 16)
            act.wait_ge(ld["const"], 32)
            moe_front_scalar(act, moe1, 0, 0)
            moe_scalar(act, 0)
            attn0_scalar(act, attn0, 1)
            moe_front_scalar(act, moe2, 1, 2)
            moe_scalar(act, 1)
            rwkv_scalar(act, rwkv1, 3)
            attn1_scalar(act, attn1, 4)
            rwkv_scalar(act, rwkv2, 5)

        @block.tensor
        def _(pe):
            pe.wait_ge(ld["const"], 32)
            pe.wait_ge(ld["small"], 32)
            pe.wait_ge(su["consts"], 1)
            moe_front_tensor(pe, moe1, (su["stats"], TILES))
            dispatch_tensor(pe, moe1, 0)
            pe.wait_ge(ld["moe"], 48)
            moe_tensor(pe, 0)
            pe.wait_ge(ld["w"], 16)
            attn0_tensor(pe, attn0, (moe1["stats"], TILES))
            moe_front_tensor(pe, moe2, (attn0["stats"], TILES))
            dispatch_tensor(pe, moe2, 1)
            moe_tensor(pe, 1)
            rwkv_tensor(pe, rwkv1, (moe2["stats"], TILES))
            attn1_tensor(pe, attn1, (rwkv1["stats"], TILES))
            rwkv_tensor(pe, rwkv2, (attn1["stats"], TILES))


def kernel(**inputs):
    import concourse.bacc as bacc
    from concourse.bass_utils import run_bass_kernel_spmd as run

    a = {n: np.asarray(v) for n, v in inputs.items()}
    arrays = {
        "x": a["L0_attn_x"].reshape(B * S, D),
        "consts": shape_constants(),
        "vecs": np.stack([a[n] for n in V_NAMES], axis=1),
        "rows": np.stack([a[n] for n in R_NAMES])[None],
        "weights": np.stack([a[n] for n in W_NAMES] + [a[n].T for n in WT_NAMES], axis=1),
        "gateT": a["L0_ffn_gate_w"].T,
        "w1": a["L0_ffn_w1"].transpose(1, 0, 2),
        "w3": a["L0_ffn_w3"].transpose(1, 0, 2),
        "w2": a["L0_ffn_w2"].reshape(E, NCH, IC, D).transpose(2, 0, 1, 3),
    }
    arrays = {n: np.ascontiguousarray(v) for n, v in arrays.items()}
    nc = bacc.Bacc("TRN2", target_bir_lowering=False, num_devices=1)
    io = {n: nc.dram_tensor(f"in_{n}", v.shape, mybir.dt.from_np(v.dtype), kind="ExternalInput").ap()
          for n, v in arrays.items()}
    out = nc.dram_tensor("out_0", (B, S, D), F32, kind="ExternalOutput").ap()
    build(nc, io, out)
    r = run(nc, [{f"in_{n}": v for n, v in arrays.items()}], core_ids=[0])
    return r.results[0]["out_0"]
```

```python
from contextlib import ExitStack

import numpy as np

import concourse.bass as bass
from concourse import mybir

F32 = mybir.dt.float32
BF16 = mybir.dt.bfloat16
F16 = mybir.dt.float16
I32 = mybir.dt.int32
U32 = mybir.dt.uint32
ALU = mybir.AluOpType
ACT = mybir.ActivationFunctionType
AX_X = mybir.AxisListType.X

P = 128
B, S, D = 8, 256, 128
TILES = B * S // P
TPB = S // P
H = 16
HD = D // H
QH = P // 2
HG = 4
HR = H // HG
MW = HD * HR
E = 8
TOPK = 2
PAD = TILES // 2
PAIRS = TOPK * TILES
SLOT_TILES = (PAIRS * P + E * (P - 1)) // P
I = 448
NCH = 4
IC = I // NCH
DECAY = 0.95
EPS = 1e-5
SCALE = float(HD) ** -0.5

C_IDENT, C_MASK, C_BLOCK, C_QDECAY, C_HEAD, C_KDECAY, C_RANK = 0, 128, 256, 384, 512, 528, 529
C_BEFORE = C_RANK + E
C_LANE = C_BEFORE + P
C_TILE_ROWS = C_LANE + P
C_LOWER = C_TILE_ROWS + TILES
C_PAIR = C_LOWER + E * E
C_SPARE = C_PAIR + 2 * PAIRS
C_COLS = C_SPARE + SLOT_TILES
V_NAMES = ["L0_attn_bq", "L0_attn_bk", "L0_attn_bo", "L0_attn_gamma", "L0_attn_beta",
           "L1_attn_bq", "L1_attn_bk", "L1_ffn_mu_r", "L1_ffn_mu_k"]
R_NAMES = ["L0_attn_bv", "L0_attn_bk", "L1_attn_bv", "L1_attn_bo"]
W_NAMES = ["L0_attn_Wq", "L0_attn_Wk", "L0_attn_Wv", "L0_attn_Wo"]
WT_NAMES = ["L1_attn_Wq", "L1_attn_Wk", "L1_attn_Wv", "L1_attn_Wo", "L1_ffn_W_r", "L1_ffn_W_k", "L1_ffn_W_v"]


def shape_constants():
    c = np.zeros((P, C_COLS), np.float32)
    p = np.arange(P)
    c[:, C_IDENT:C_IDENT + P] = np.eye(P)
    gap = p[None, :] - p[:, None]
    c[:, C_MASK:C_MASK + P] = np.where(gap >= 0, DECAY ** np.maximum(gap, 0), 0.0)
    c[:, C_BLOCK:C_BLOCK + P] = p[:, None] // HD == p[None, :] // HD
    c[:, C_QDECAY:C_QDECAY + P] = DECAY ** (p[None, :] + 1.0)
    c[:, C_HEAD:C_HEAD + HR] = p[:, None] % MW // HD == np.arange(HR)[None, :]
    c[:, C_KDECAY] = DECAY ** (P - 1.0 - p)
    c[:, C_RANK:C_RANK + E] = E - np.arange(E)[None, :]
    c[:, C_BEFORE:C_BEFORE + P] = p[:, None] < p[None, :]
    c[:, C_LANE:C_LANE + P] = p[None, :]
    c[:, C_TILE_ROWS:C_TILE_ROWS + TILES] = P * np.arange(TILES)[None, :]
    c[:, C_LOWER:C_LOWER + E * E] = (np.arange(E)[None, :] < np.arange(E)[:, None]).reshape(1, E * E)
    c[:, C_PAIR:C_PAIR + 2 * PAIRS:2] = 1 + np.arange(PAIRS)[None, :]
    c[:, C_PAIR + 1:C_PAIR + 2 * PAIRS:2] = p[:, None]
    c[:, C_SPARE:C_SPARE + SLOT_TILES] = P + P * (PAIRS + np.arange(SLOT_TILES)[None, :]) + p[:, None]
    return c


LANE_PIECE = 8
KEEP = 4
ROUNDER = 1.5 * 2.0 ** 23


def copying_matrices():
    c = np.zeros((P, 2, HG, 2, P), np.float16)
    j = np.arange(MW)
    for which, blocks in enumerate((((0, 1), (2, 3)), ((0, 2), (1, 3)))):
        for g in range(HG):
            for part in range(2):
                for block in blocks[part]:
                    c[g * MW + j, which, g, part, block * MW + j] = 1.0
    return c


ds = bass.ds


def build(nc, io, out):
    with ExitStack() as ctx:
        def sb(name, shape, dt=F32):
            return ctx.enter_context(nc.sbuf_tensor(name, shape, dt))

        def sems(stage, names):
            return {n: ctx.enter_context(nc.semaphore(f"{stage}_{n}")) for n in names.split()}

        X = sb("X", [P, TILES, D])
        consts = sb("consts", [P, C_COLS])
        vecs = sb("vecs", [P, len(V_NAMES)])
        omu = sb("omu", [P, 2])
        rows = sb("rows", [P, len(R_NAMES), D])
        ones = sb("ones", [1, P])
        W = sb("W", [P, len(W_NAMES) + len(WT_NAMES), D])
        gateT = sb("gateT", [P, E])
        W1 = sb("W1", [P, E, I])
        W3 = sb("W3", [P, E, I])
        W2 = sb("W2", [IC, E, NCH, D])
        minus_i = sb("minus_i", [P, P], BF16)
        block_avg = sb("block_avg", [P, P])
        bn = sb("bn", [P, TILES, 6])
        mean = sb("mean", [P, TILES])
        nrm = sb("nrm", [P, 6, TILES])
        xn = sb("xn", [P, 2, TPB, D])
        xT = sb("xT", [P, 2, S + 1])
        qk = sb("qk", [P, 2, 2, S])
        qk_part = sb("qk_part", [P, 2, 2, 2, S], F16)
        copying = sb("copying", [P, 2, HG, 2, P], F16)
        K4 = sb("K4", [P, 2, HG, S], F16)
        q4 = sb("q4", [P, 2, HG, S], F16)
        Q4 = sb("Q4", [P, 2, HR, HG, S], F16)
        Vm = sb("Vm", [P, 2, TPB, H, MW])
        Vfull = sb("Vfull", [P, 2, D])
        Kd = sb("Kd", [P, 2, D])
        St = sb("St", [P, 2, D])
        qD = sb("qD", [P, 2, P])
        att = sb("att", [P, 4, HR, HG, P])
        amax = sb("amax", [P, 2, QH], BF16)
        den = sb("den", [P, 2, P])
        rden = sb("rden", [P, 2, P])
        bk_decay = sb("bk_decay", [P, D])
        oT = sb("oT", [P, 2, S])
        gbn = sb("gbn", [P, 6])
        gst = sb("gst", [P, 10])
        yT = sb("yT", [P, S])
        LG = sb("LG", [P, TILES, E])
        rt = sb("rt", [P, 6, TILES, E])
        rs = sb("rs", [P, 8, TILES])
        all_ones = sb("all_ones", [P, P])
        run = sb("run", [P, 2, PAD + TILES, E])
        seat = sb("seat", [P, TILES, E])
        fill = sb("fill", [P, E, TILES])
        tri = sb("tri", [P, E, E])
        need = sb("need", [P, E])
        begin = sb("begin", [P, E])
        place = sb("place", [P, 4, PAIRS])
        pair_parts = sb("pair_parts", [P, PAIRS, 2], BF16)
        lane16 = sb("lane16", [P, P], BF16)
        seat16 = sb("seat16", [P, 2, PAIRS], BF16)
        in_tile = sb("in_tile", [P, PAIRS, SLOT_TILES], BF16)
        claim = sb("claim", [P, PAIRS, 2, SLOT_TILES], BF16)
        lane_of = sb("lane_of", [P, PAIRS, P], BF16)
        own = sb("own", [1, 2, SLOT_TILES, E])
        expert_f = sb("expert_f", [1, SLOT_TILES])
        expert = sb("expert", [1, SLOT_TILES], I32)
        slot = sb("slot", [P, 6, SLOT_TILES])
        source = sb("source", [P, SLOT_TILES], U32)
        target = sb("target", [P, SLOT_TILES], U32)
        source_now = sb("source_now", [P, 2, 1], U32)
        target_now = sb("target_now", [P, 2, 1], U32)
        pool_turn = sb("pool_turn", [1, 2])
        xg = sb("xg", [P, 2, D])
        xs = sb("xs", [P, 2, P])
        ys = sb("ys", [P, 2, D])
        roomy = att.rearrange("p n r g q -> p (n r g q)")
        sg = roomy[:, PAIRS * D:PAIRS * D + 2 * I].rearrange("p (n i) -> p n i", n=2)
        hb = roomy[:, PAIRS * D + 2 * I:PAIRS * D + 4 * I].rearrange("p (n i) -> p n i", n=2)
        hT = roomy[0:IC, PAIRS * D + 4 * I:PAIRS * D + 4 * I + 2 * NCH * P].rearrange("p (n c t) -> p n c t", n=2, c=NCH)
        yback = roomy[:, 0:PAIRS * D].rearrange("p (k t d) -> p k t d", k=TOPK, d=D)
        mixed = roomy[:, 0:8 * S].rearrange("p (n k s) -> p n k s", n=2, s=S)
        rgate = roomy[:, 8 * S:10 * S].rearrange("p (n s) -> p n s", n=2)
        kact = roomy[:, 10 * S:14 * S].rearrange("p (n k s) -> p n k s", n=2, s=S)
        rv = roomy[:, 14 * S:16 * S].rearrange("p (n s) -> p n s", n=2)

        ps = ctx.enter_context(nc.psum_tensor("ps", [P, 8, 512], F32))

        ident = consts[:, C_IDENT:C_IDENT + P]
        decay_mask = consts[:, C_MASK:C_MASK + P]
        block_diag = consts[:, C_BLOCK:C_BLOCK + P]
        q_decay = consts[:, C_QDECAY:C_QDECAY + P]
        head_of = consts[:, C_HEAD:C_HEAD + HR]
        k_decay = consts[:, C_KDECAY:C_KDECAY + 1]
        rank = consts[:, C_RANK:C_RANK + E]
        before_me = consts[:, C_BEFORE:C_BEFORE + P]
        lane = consts[:, C_LANE:C_LANE + P]
        tile_rows = consts[:, C_TILE_ROWS:C_TILE_ROWS + TILES]
        lower = consts[:, C_LOWER:C_LOWER + E * E].rearrange("p (a b) -> p a b", a=E)
        spare_row = consts[:, C_SPARE:C_SPARE + SLOT_TILES]

        def vec(name):
            n = V_NAMES.index(name)
            return vecs[:, n:n + 1]

        def row(name):
            return rows[:, R_NAMES.index(name), :]

        def w(name):
            return W[:, (W_NAMES + WT_NAMES).index(name), :]

        ld = sems("load", "const small w moe copying")
        su = sems("setup", "zeros consts stats")
        x_piece = [ctx.enter_context(nc.semaphore(f"x_piece{n}")) for n in range(TILES // KEEP)]
        final = sems("final", "stored")
        nm = sems("norm", "mean var root newton ready")
        norm_names = "xn xnT xT x_done stats "
        MO = {n: sems(n, norm_names + "lg lgT") for n in ("moe1", "moe2")}
        me = sems("moe", "rt exp both count seated in_tile claim claim_act lanes slots expert source target "
                  "source_now target_now xg_ps xs gu sg h hT_ps hT y ys")
        gathered, scattered = ([ctx.enter_context(nc.semaphore(f"{n}{par}")) for par in range(2)]
                               for n in ("gathered", "scattered"))
        kept_done = ctx.enter_context(nc.semaphore("kept_done"))
        turned = [ctx.enter_context(nc.semaphore(f"turned{k}")) for k in range(2)]
        fetched = [ctx.enter_context(nc.semaphore(f"fetched{n}")) for n in range(TILES // KEEP)]
        RW = {n: sems(n, norm_names + "shift mix rk rgate krelu kact v rv") for n in ("rwkv1", "rwkv2")}
        attn_names = norm_names + "qk_ps v_ps q lo copied qm k4 vm sc at av oT yps "
        AT = {"attn0": sems("attn0", attn_names + "vfull kd qd st_ps st ymv ym yvar gm_ps gm dev gv_ps gv groot grs ab yn ynT"),
              "attn1": sems("attn1", attn_names + "mx sub ex den rden")}

        def batches(eng, front, heavy, tail, tail_first=False, straight=False):
            def turn(i):
                for n in range(2):
                    front(i * 2 + n + 2, n)
                    if tail_first:
                        tail(i * 2 + n, n)
                    heavy(i * 2 + n + 1, 1 - n)
                    if not tail_first:
                        tail(i * 2 + n, n)
            front(0, 0)
            front(1, 1)
            heavy(0, 0)
            turn(0)
            if straight:
                for i in range(1, B // 2 - 1):
                    turn(i)
            else:
                with eng.Fori(1, B // 2 - 1) as i:
                    turn(i)
            heavy(B - 1, 1)
            tail(B - 2, 0)
            tail(B - 1, 1)

        def nothing(b, par):
            pass

        def after(eng, sem, value):
            if not isinstance(value, int) or value > 0:
                eng.wait_ge(sem, value)

        def two_before(eng, sem, b, each=1):
            after(eng, sem, (b - 1) * each)

        def norm_vector(dve, turn, before):
            dve.wait_ge(*before)
            nc.vector.tensor_tensor(nrm[:, 3, :], bn[:, :, 1], bn[:, :, 4], ALU.add).then_inc(nm["mean"], 1)
            nc.vector.tensor_tensor(nrm[:, 4, :], bn[:, :, 1], bn[:, :, 4], ALU.subtract).then_inc(nm["mean"], 1)
            nc.vector.tensor_tensor(nrm[:, 5, :], bn[:, :, 2], bn[:, :, 5], ALU.add).then_inc(nm["mean"], 1)
            dve.wait_ge(nm["mean"], turn * 6 + 3)
            nc.vector.tensor_scalar(mean[:, :], nrm[:, 3, :], 0.5, None, ALU.mult).then_inc(nm["mean"], 1)
            nc.vector.scalar_tensor_tensor(nrm[:, 4, :], nrm[:, 4, :], 0.25, nrm[:, 4, :], ALU.mult,
                                           ALU.mult).then_inc(nm["mean"], 1)
            nc.vector.tensor_scalar(nrm[:, 5, :], nrm[:, 5, :], 1.0 / D, EPS, ALU.mult, ALU.add).then_inc(nm["mean"], 1)
            dve.wait_ge(nm["mean"], turn * 6 + 6)
            nc.vector.tensor_tensor(nrm[:, 0, :], nrm[:, 4, :], nrm[:, 5, :], ALU.add).then_inc(nm["var"], 1)
            dve.wait_ge(nm["root"], turn + 1)
            nc.vector.reciprocal(nrm[:, 2, :], nrm[:, 1, :]).then_inc(nm["newton"], 1)
            dve.wait_ge(nm["newton"], turn * 4 + 1)
            nc.vector.tensor_tensor(nrm[:, 3, :], nrm[:, 2, :], nrm[:, 2, :], ALU.mult).then_inc(nm["newton"], 1)
            dve.wait_ge(nm["newton"], turn * 4 + 2)
            nc.vector.tensor_tensor(nrm[:, 3, :], nrm[:, 3, :], nrm[:, 0, :], ALU.mult).then_inc(nm["newton"], 1)
            dve.wait_ge(nm["newton"], turn * 4 + 3)
            nc.vector.tensor_scalar(nrm[:, 3, :], nrm[:, 3, :], -0.5, 1.5, ALU.mult, ALU.add).then_inc(nm["newton"], 1)
            dve.wait_ge(nm["newton"], turn * 4 + 4)
            nc.vector.tensor_tensor(nrm[:, 2, :], nrm[:, 2, :], nrm[:, 3, :], ALU.mult).then_inc(nm["ready"], 1)
            dve.wait_ge(nm["ready"], turn + 1)

        def norm_scalar(act, turn):
            act.wait_ge(nm["var"], turn + 1)
            nc.scalar.activation(nrm[:, 1, :], nrm[:, 0, :], ACT.Sqrt).then_inc(nm["root"], 1)

        def front_vector(dve, s, b, par, tokens=None):
            if tokens is None:
                tokens = xn[:, par]
                two_before(dve, s["xnT"], b)
            for j in range(TPB):
                t = b * TPB + j
                nc.vector.tensor_scalar(tokens[:, j, :], X[:, t, :], mean[:, ds(t, 1)], nrm[:, 2, ds(t, 1)],
                                        ALU.subtract, ALU.mult).then_inc(s["xn"], 1)

        def front_tensor(pe, s, b, par, bank=None, tokens=None):
            if tokens is None:
                tokens = xn[:, par]
            pe.wait_ge(s["xn"], b * TPB + TPB)
            if bank is None:
                bank = par
                two_before(pe, s["xT"], b)
            else:
                after(pe, s["xT"], b)
            nc.tensor.transpose(ps[:, bank, 0:P], tokens[:, 0, :], ident)
            nc.tensor.transpose(ps[:, bank, P:S], tokens[:, 1, :], ident).then_inc(s["xnT"], 1)

        def front_scalar(act, s, b, par, bank=None):
            bank = par if bank is None else bank
            act.wait_ge(s["xnT"], b + 1)
            nc.scalar.copy(xT[:, par, 1:S + 1], ps[:, bank, 0:S]).then_inc(s["xT"], 1)

        def tile_stats(dve, s, t, updates):
            if updates is not None:
                dve.wait_ge(s["x_done"], updates)
            nc.vector.bn_stats(bn[:, t, :], X[:, t, :]).then_inc(s["stats"], 1)

        def update_batch(dve, s, b, src, stats=True):
            tiles = X[:, ds(b * TPB, TPB), :]
            nc.vector.tensor_tensor(tiles, tiles, src.rearrange("p (j d) -> p j d", j=TPB),
                                    ALU.add).then_inc(s["x_done"], 1)
            if stats:
                for j in range(TPB):
                    tile_stats(dve, s, b * TPB + j, b + 1)

        ROUTE_STEPS = 42
        ROUTE_DIFF = 12

        def tokens_of(b):
            return roomy[:, b * S:(b + 1) * S].rearrange("p (j d) -> p j d", j=TPB)

        def moe_front_vector(dve, s, m, turn, before):
            norm_vector(dve, turn, before)

            batches(dve, lambda b, par: front_vector(dve, s, b, par, tokens_of(b)), nothing, nothing, straight=True)
            dve.wait_ge(s["lg"], B)
            nc.vector.tensor_copy(LG[:, :, :], ps[:, 3, 0:TILES * E].rearrange("p (t e) -> p t e", e=E)).then_inc(s["lgT"], 1)

            dve.wait_ge(s["lgT"], 1)
            step = [0]

            def link(ins):
                step[0] += 1
                ins.then_inc(me["rt"], 1)
                dve.wait_ge(me["rt"], m * ROUTE_STEPS + step[0])

            def wide(n):
                return rs[:, n, :].unsqueeze(2).broadcast_to([P, TILES, E])
            ranks = rank.unsqueeze(1).broadcast_to([P, TILES, E])
            v = nc.vector
            for k, src in ((0, LG[:, :, :]), (1, rt[:, 2])):
                link(v.tensor_reduce(rs[:, k, :], src, AX_X, ALU.max))
                link(v.tensor_tensor(rt[:, 0], src, wide(k), ALU.is_equal))
                link(v.tensor_tensor(rt[:, 1], rt[:, 0], ranks, ALU.mult))
                link(v.tensor_reduce(rs[:, 2, :], rt[:, 1], AX_X, ALU.max))
                link(v.tensor_tensor(rt[:, 3 + k], rt[:, 1], wide(2), ALU.is_equal))
                if k == 0:
                    link(v.scalar_tensor_tensor(rt[:, 2], rt[:, 3], -3.0e38, LG[:, :, :], ALU.mult, ALU.add))
            link(v.tensor_tensor(rs[:, 3, :], rs[:, 1, :], rs[:, 0, :], ALU.subtract))
            assert step[0] == ROUTE_DIFF
            v.tensor_tensor(rt[:, 5], rt[:, 3], rt[:, 4], ALU.add).then_inc(me["both"], 1)
            dve.wait_ge(me["exp"], m + 1)
            link(v.tensor_scalar(rs[:, 5, :], rs[:, 4, :], 1.0, None, ALU.add))
            link(v.reciprocal(rs[:, 6, :], rs[:, 5, :]))
            link(v.tensor_tensor(rs[:, 7, :], rs[:, 6, :], rs[:, 4, :], ALU.mult))
            dve.wait_ge(me["count"], m + 1)
            link(v.tensor_copy(run[:, 0, PAD:, :], ps[:, 1, 0:TILES * E].rearrange("p (t e) -> p t e", e=E)))
            side, shift = 0, 1
            while shift < TILES:
                link(v.tensor_tensor(run[:, 1 - side, PAD:, :], run[:, side, PAD:, :],
                                     run[:, side, PAD - shift:PAD + TILES - shift, :], ALU.add))
                side, shift = 1 - side, shift * 2
            total = run[:, side, PAD + TILES - 1, :]
            link(v.tensor_tensor(fill[:, :, :], total.unsqueeze(2).broadcast_to([P, E, TILES]),
                                 tile_rows.unsqueeze(1).broadcast_to([P, E, TILES]), ALU.is_gt))
            link(v.tensor_reduce(need[:, :], fill[:, :, :], AX_X, ALU.add))
            link(v.tensor_tensor(tri[:, :, :], need[:, :].unsqueeze(1).broadcast_to([P, E, E]), lower, ALU.mult))
            link(v.tensor_reduce(begin[:, :], tri[:, :, :], AX_X, ALU.add))
            link(v.tensor_tensor(seat[:, :, :], ps[:, 0, 0:TILES * E].rearrange("p (t e) -> p t e", e=E),
                                 run[:, side, PAD - 1:PAD + TILES - 1, :], ALU.add))
            link(v.scalar_tensor_tensor(seat[:, :, :], begin[:, :].unsqueeze(1).broadcast_to([P, TILES, E]), float(P),
                                        seat[:, :, :], ALU.mult, ALU.add))
            for k in range(TOPK):
                link(v.tensor_tensor(rt[:, k], rt[:, 3 + k], seat[:, :, :], ALU.mult))
            link(v.tensor_reduce(place[:, 0, :], rt[:, 0:TOPK].rearrange("p k t e -> p (k t) e"), AX_X, ALU.add))
            link(v.tensor_scalar(place[:, 1, :], place[:, 0, :], 1.0 / P, -0.5 + 0.5 / P, ALU.mult, ALU.add))
            link(v.tensor_scalar(place[:, 1, :], place[:, 1, :], ROUNDER, None, ALU.add))
            link(v.tensor_scalar(place[:, 2, :], place[:, 1, :], ROUNDER, None, ALU.subtract))
            v.tensor_copy(seat16[:, 0, :], place[:, 2, :]).then_inc(me["seated"], 1)
            v.scalar_tensor_tensor(seat16[:, 1, :], place[:, 2, :], -float(P), place[:, 0, :],
                                   ALU.mult, ALU.add).then_inc(me["seated"], 1)
            dve.wait_ge(me["seated"], m * 2 + 2)
            tiles_of = [P, PAIRS, SLOT_TILES]
            v.tensor_tensor(in_tile[:, :, :], seat16[:, 0, :].unsqueeze(2).broadcast_to(tiles_of),
                            lane16[:, 0:SLOT_TILES].unsqueeze(1).broadcast_to(tiles_of), ALU.is_equal).then_inc(me["in_tile"], 1)
            for n in range(0, PAIRS, LANE_PIECE):
                v.tensor_tensor(lane_of[:, n:n + LANE_PIECE, :],
                                seat16[:, 1, n:n + LANE_PIECE].unsqueeze(2).broadcast_to([P, LANE_PIECE, P]),
                                lane16[:, :].unsqueeze(1).broadcast_to([P, LANE_PIECE, P]), ALU.is_equal).then_inc(me["lanes"], 1)
            own_of = [1, SLOT_TILES, E - 1]
            link(v.tensor_tensor(own[:, 0, :, 0:E - 1], begin[0:1, 1:].unsqueeze(1).broadcast_to(own_of),
                                 lane[0:1, 0:SLOT_TILES].unsqueeze(2).broadcast_to(own_of), ALU.is_le))
            link(v.tensor_reduce(expert_f[:, :], own[:, 0, :, 0:E - 1], AX_X, ALU.add))
            v.tensor_copy(expert[:, :], expert_f[:, :]).then_inc(me["expert"], 1)
            dve.wait_ge(me["slots"], m + 1)
            link(v.tensor_copy(slot[:, 1, :], ps[:, 2, SLOT_TILES:2 * SLOT_TILES]))
            link(v.scalar_tensor_tensor(slot[:, 0, :], ps[:, 2, 0:SLOT_TILES], float(P), slot[:, 1, :], ALU.mult, ALU.add))
            link(v.tensor_scalar(slot[:, 2, :], slot[:, 0, :], (TILES + 1) * P - 0.5, -float(TILES * P), ALU.is_gt, ALU.mult))
            link(v.tensor_tensor(slot[:, 3, :], slot[:, 0, :], slot[:, 2, :], ALU.add))
            link(v.tensor_scalar(slot[:, 3, :], slot[:, 3, :], -float(P), 0.0, ALU.add, ALU.max))
            v.tensor_copy(source[:, :], slot[:, 3, :]).then_inc(me["source"], 1)
            dve.wait_ge(me["source"], m + 1)
            for n in range(2):
                index_source(dve, m, n, n)
            link(v.tensor_scalar(slot[:, 4, :], slot[:, 0, :], 0.5, None, ALU.is_lt))
            link(v.tensor_tensor(slot[:, 4, :], slot[:, 4, :], spare_row, ALU.mult))
            link(v.scalar_tensor_tensor(slot[:, 5, :], slot[:, 0, :], -float(P), slot[:, 4, :], ALU.add, ALU.add))
            v.tensor_copy(target[:, :], slot[:, 5, :]).then_inc(me["target"], 1)
            assert step[0] == ROUTE_STEPS

        def moe_front_scalar(act, s, m, turn):
            norm_scalar(act, turn)

            def front(b, par):
                two_before(act, s["lg"], b)
                front_scalar(act, s, b, par)
            batches(act, front, nothing, nothing, straight=True)
            act.wait_ge(me["rt"], m * ROUTE_STEPS + ROUTE_DIFF)
            nc.scalar.activation(rs[:, 4, :], rs[:, 3, :], ACT.Exp).then_inc(me["exp"], 1)

        def moe_front_tensor(pe, s, before):
            pe.wait_ge(*before)

            def heavy(b, par):
                pe.wait_ge(s["xT"], b + 1)
                for j in range(TPB):
                    last = nc.tensor.matmul(ps[:, 3, (b * TPB + j) * E:(b * TPB + j + 1) * E], xT[:, par, 1 + j * P:1 + (j + 1) * P],
                                            gateT[:, :], start=True, stop=True)
                last.then_inc(s["lg"], 1)
            batches(pe, lambda b, par: front_tensor(pe, s, b, par, None, tokens_of(b)), heavy, nothing, straight=True)

        def claim_pool(pool, m):
            pool.wait_ge(me["in_tile"], m + 1)
            nc.gpsimd.tensor_tensor(claim[:, :, 0, :], pair_parts[:, :, 0:1].broadcast_to([P, PAIRS, SLOT_TILES]),
                                    in_tile[:, :, :], ALU.mult).then_inc(me["claim"], 1)

        def claim_scalar(act, m):
            act.wait_ge(me["in_tile"], m + 1)
            nc.scalar.activation(claim[:, :, 1, :], in_tile[:, :, :], ACT.Identity,
                                 scale=consts[:, C_PAIR + 1:C_PAIR + 2]).then_inc(me["claim_act"], 1)

        def dispatch_tensor(pe, s, m):
            pe.wait_ge(me["both"], m + 1)
            pe.wait_ge(s["xT"], B)
            taken = rt[:, 5].rearrange("p t e -> p (t e)")
            nc.tensor.matmul(ps[:, 0, 0:TILES * E], before_me, taken, start=True, stop=True)
            nc.tensor.matmul(ps[:, 1, 0:TILES * E], all_ones[:, :], taken, start=True, stop=True).then_inc(me["count"], 1)
            pe.wait_ge(me["claim"], m + 1)
            pe.wait_ge(me["claim_act"], m + 1)
            for n in range(PAIRS):
                if n % LANE_PIECE == 0:
                    pe.wait_ge(me["lanes"], (m * PAIRS + n) // LANE_PIECE + 1)
                last = nc.tensor.matmul(ps[:, 2, 0:2 * SLOT_TILES], lane_of[:, n, :],
                                        claim[:, n].rearrange("p k n -> p (k n)"), start=(n == 0), stop=(n == PAIRS - 1))
            last.then_inc(me["slots"], 1)

        def keep_tokens(sp, s, kept):
            for b in range(B):
                sp.wait_ge(s["xn"], (b + 1) * TPB)
                sp.dma_start(kept[b * S:(b + 1) * S, :].rearrange("(t p) d -> p t d", p=P),
                             tokens_of(b)).then_inc(kept_done, 16)

        def slot_tiles(eng, step, drain, peel=1, spare=0):
            end = (SLOT_TILES - spare) // 2
            for n in range(2 * peel):
                step(n, n % 2)
            with eng.Fori(peel, end) as i:
                step(i * 2, 0)
                step(i * 2 + 1, 1)
            for n in range(end * 2, SLOT_TILES):
                step(n, n % 2)
            drain()

        def there(n, back):
            return not isinstance(n, int) or n >= back

        def moved(n, par, m):
            return m * 16 * ((SLOT_TILES + 1 - par) // 2) + (n - par + 2) * 8

        def after_moved(eng, sem, n, par, m):
            if not isinstance(n, int) or n >= 0:
                eng.wait_ge(sem[par], moved(n, par, m))

        AHEAD = 3
        BEHIND = 5

        def moe_pool(pool, s, m, kept, back):
            pool.wait_ge(kept_done, (m + 1) * 16 * B)
            pool.wait_ge(me["source"], m + 1)

            def wait_taken(k, n):
                after(pool, turned[k], m * SLOT_TILES + n)
                nc.gpsimd.tensor_tensor(pool_turn[:, k:k + 1], ones[:, 0:1], ones[:, 0:1], ALU.add).then_inc(turned[k], 1)

            def gather(n, par):
                after(pool, me["xg_ps"], m * SLOT_TILES + n - 1)
                pool.wait_ge(me["source_now"], m * SLOT_TILES + n + 1)
                wait_taken(0, n)
                nc.gpsimd.indirect_dma_start(xg[:, par, :], None, kept,
                                             bass.IndirectOffsetOnAxis(ap=source_now[:, par, :], axis=0)).then_inc(gathered[par], 16)

            def scatter(n, par):
                pool.wait_ge(me["target_now"], m * SLOT_TILES + n + 1)
                pool.wait_ge(me["ys"], m * SLOT_TILES + n + 1)
                wait_taken(1, n)
                nc.gpsimd.indirect_dma_start(back, bass.IndirectOffsetOnAxis(ap=target_now[:, par, :], axis=0),
                                             ys[:, par, :], None).then_inc(scattered[par], 16)

            def step(n, par):
                gather(n, par)
                if there(n, BEHIND):
                    scatter(n - BEHIND, 1 - par)

            def drain():
                for n in range(SLOT_TILES - BEHIND, SLOT_TILES):
                    scatter(n, n % 2)
            slot_tiles(pool, step, drain, peel=3)

        def moe_tensor(pe, m):
            pe.wait_ge(me["expert"], m + 1)
            pe.wait_ge(me["source"], m + 1)

            def expert_of(n):
                return pe.value_load(expert[0:1, ds(n, 1)], min_val=0, max_val=E - 1)

            def turn_tokens(n, par):
                pe.wait_ge(gathered[par], moved(n, par, m))
                after(pe, me["xs"], m * SLOT_TILES + n)
                nc.tensor.transpose(ps[:, 7, 0:P], xg[:, par, :], ident).then_inc(me["xg_ps"], 1)

            def gate_up(n, par):
                e = expert_of(n)
                pe.wait_ge(me["xs"], m * SLOT_TILES + n + 1)
                after(pe, me["h"], m * SLOT_TILES + n - 1)
                nc.tensor.matmul(ps[:, 2 * par, 0:I], xs[:, par, :], W1[:, e, :], start=True, stop=True)
                nc.tensor.matmul(ps[:, 2 * par + 1, 0:I], xs[:, par, :], W3[:, e, :], start=True,
                                 stop=True).then_inc(me["gu"], 1)

            def turn_hidden(n, par):
                pe.wait_ge(me["h"], m * SLOT_TILES + n + 1)
                after(pe, me["hT"], m * SLOT_TILES + n - 1)
                for c in range(NCH):
                    last = nc.tensor.transpose(ps[0:IC, 4 + par, c * P:(c + 1) * P],
                                               hb[:, par, c * IC:(c + 1) * IC], ident)
                last.then_inc(me["hT_ps"], 1)

            def down(n, par):
                e = expert_of(n)
                pe.wait_ge(me["hT"], m * SLOT_TILES + n + 1)
                after(pe, me["ys"], m * SLOT_TILES + n)
                for c in range(NCH):
                    last = nc.tensor.matmul(ps[:, 6, 0:D], hT[:, par, c, :], W2[:, e, c, :],
                                            start=(c == 0), stop=(c == NCH - 1))
                last.then_inc(me["y"], 1)

            def step(n, par):
                if isinstance(n, int) and n == 0:
                    turn_tokens(0, 0)
                gate_up(n, par)
                if not isinstance(n, int) or n + 1 < SLOT_TILES:
                    turn_tokens(n + 1, 1 - par)
                if there(n, 1):
                    turn_hidden(n - 1, 1 - par)
                if there(n, 2):
                    down(n - 2, par)

            def drain():
                n = SLOT_TILES
                turn_hidden(n - 1, (n - 1) % 2)
                down(n - 2, n % 2)
                down(n - 1, (n - 1) % 2)
            slot_tiles(pe, step, drain, peel=2)

        def moe_scalar(act, m):
            def silu(n, par):
                act.wait_ge(me["gu"], m * SLOT_TILES + n + 1)
                after(act, me["h"], m * SLOT_TILES + n - 1)
                nc.scalar.activation(sg[:, par, :], ps[:, 2 * par, 0:I], ACT.Silu).then_inc(me["sg"], 1)

            def evict_hidden(n, par):
                act.wait_ge(me["hT_ps"], m * SLOT_TILES + n + 1)
                after(act, me["y"], m * SLOT_TILES + n - 1)
                nc.scalar.copy(hT[:, par].rearrange("p c t -> p (c t)"), ps[0:IC, 4 + par, :]).then_inc(me["hT"], 1)

            def evict_output(n, par):
                act.wait_ge(me["y"], m * SLOT_TILES + n + 1)
                after_moved(act, scattered, n - 2, par, m)
                nc.scalar.mul(ys[:, par, :], ps[:, 6, 0:D], 0.5).then_inc(me["ys"], 1)

            def step(n, par):
                silu(n, par)
                if there(n, 1):
                    evict_hidden(n - 1, 1 - par)
                if there(n, 2):
                    evict_output(n - 2, par)

            def drain():
                n = SLOT_TILES
                evict_hidden(n - 1, (n - 1) % 2)
                evict_output(n - 2, n % 2)
                evict_output(n - 1, (n - 1) % 2)
            slot_tiles(act, step, drain, peel=2)

        def index_source(dve, m, n, par):
            after_moved(dve, gathered, n - 2, par, m)
            nc.vector.tensor_copy(source_now[:, par, :], source[:, ds(n, 1)]).then_inc(me["source_now"], 1)

        def moe_vector(dve, s, m):
            def evict_tokens(n, par):
                dve.wait_ge(me["xg_ps"], m * SLOT_TILES + n + 1)
                nc.vector.tensor_copy(xs[:, par, :], ps[:, 7, 0:P]).then_inc(me["xs"], 1)

            def hidden(n, par):
                dve.wait_ge(me["sg"], m * SLOT_TILES + n + 1)
                after(dve, me["hT_ps"], m * SLOT_TILES + n - 1)
                nc.vector.tensor_tensor(hb[:, par, :], sg[:, par, :], ps[:, 2 * par + 1, 0:I], ALU.mult).then_inc(me["h"], 1)

            def index_target(n, par):
                after_moved(dve, scattered, n - 2, par, m)
                nc.vector.tensor_copy(target_now[:, par, :], target[:, ds(n, 1)]).then_inc(me["target_now"], 1)

            def step(n, par):
                if isinstance(n, int) and n == 0:
                    index_source(dve, m, 2, 0)
                    evict_tokens(0, 0)
                if not isinstance(n, int) or n + 1 < SLOT_TILES:
                    evict_tokens(n + 1, 1 - par)
                hidden(n, par)
                if not isinstance(n, int) or n + AHEAD < SLOT_TILES:
                    index_source(dve, m, n + AHEAD, 1 - par)
                if there(n, 2):
                    index_target(n - 2, par)

            def drain():
                for n in range(SLOT_TILES - 2, SLOT_TILES):
                    index_target(n, n % 2)
            slot_tiles(dve, step, drain, peel=2, spare=AHEAD)

            for n in range(0, TILES, KEEP):
                dve.wait_ge(fetched[n // KEEP], 16 * TOPK * (m + 1))
                for k in range(TOPK):
                    for t in range(n, n + KEEP):
                        if k:
                            dve.wait_ge(s["x_done"], n * TOPK + t - n + 1)
                        nc.vector.scalar_tensor_tensor(X[:, t, :], yback[:, k, t, :], rs[:, 6 + k, t:t + 1], X[:, t, :],
                                                       ALU.mult, ALU.add).then_inc(s["x_done"], 1)
                for t in range(n, n + KEEP):
                    tile_stats(dve, s, t, n * TOPK + KEEP + t - n + 1)

        def fetch_outputs(sp, s, m, back):
            for n in (SLOT_TILES - 2, SLOT_TILES - 1):
                sp.wait_ge(scattered[n % 2], moved(n, n % 2, m))
            by_token = back[0:PAIRS * P, :].rearrange("(k t p) d -> p k t d", k=TOPK, p=P)
            for n in range(0, TILES, KEEP):
                for k in range(TOPK):
                    sp.dma_start(yback[:, k, n:n + KEEP, :], by_token[:, k, n:n + KEEP, :]).then_inc(fetched[n // KEEP], 16)

        def rwkv_vector(dve, s, turn, before, stats):
            norm_vector(dve, turn, before)

            def heavy(b, par):
                two_before(dve, s["rk"], b)
                dve.wait_ge(s["shift"], b * 2 + 2)
                for k, mu in ((0, "L1_ffn_mu_r"), (1, "L1_ffn_mu_k")):
                    nc.vector.scalar_tensor_tensor(mixed[:, par, k, :], xT[:, par, 1:S + 1], vec(mu),
                                                   mixed[:, par, 2 + k, :], ALU.mult, ALU.add).then_inc(s["mix"], 1)

            def tail(b, par):
                dve.wait_ge(s["v"], b + 1)
                dve.wait_ge(s["rgate"], b + 1)
                nc.vector.scalar_tensor_tensor(rv[:, par, :], ps[:, 6 + par, 0:S], 0.5, rgate[:, par, :],
                                               ALU.mult, ALU.mult).then_inc(s["rv"], 1)
                dve.wait_ge(s["rv"], b + 1)
                update_batch(dve, s, b, rv[:, par, :], stats)
            batches(dve, lambda b, par: front_vector(dve, s, b, par), heavy, tail)

        def rwkv_scalar(act, s, turn):
            norm_scalar(act, turn)

            def front(b, par):
                two_before(act, s["mix"], b, 2)
                front_scalar(act, s, b, par)
                act.wait_ge(s["xT"], b + 1)
                for k in range(2):
                    nc.scalar.activation(mixed[:, par, 2 + k, :], xT[:, par, 0:S], ACT.Identity,
                                         scale=omu[:, k:k + 1]).then_inc(s["shift"], 1)

            def heavy(b, par):
                act.wait_ge(s["rk"], b + 1)
                two_before(act, s["rv"], b)
                nc.scalar.activation(rgate[:, par, :], ps[:, 2 + par, 0:S], ACT.Sigmoid).then_inc(s["rgate"], 1)
                two_before(act, s["v"], b)
                nc.scalar.activation(kact[:, par, 0, :], ps[:, 4 + par, 0:S], ACT.Relu).then_inc(s["krelu"], 1)
                act.wait_ge(s["krelu"], b + 1)
                nc.scalar.activation(kact[:, par, 1, :], kact[:, par, 0, :], ACT.Square).then_inc(s["kact"], 1)
            batches(act, front, heavy, nothing)

        def rwkv_tensor(pe, s, before):
            pe.wait_ge(*before)

            def heavy(b, par):
                pe.wait_ge(s["mix"], b * 2 + 2)
                two_before(pe, s["kact"], b)
                for j in range(TPB):
                    nc.tensor.matmul(ps[:, 2 + par, j * P:(j + 1) * P], mixed[:, par, 0, j * P:(j + 1) * P],
                                     w("L1_ffn_W_r"), start=True, stop=True)
                nc.tensor.matmul(ps[:, 4 + par, 0:S], w("L1_ffn_W_k"), mixed[:, par, 1, :], start=True,
                                 stop=True).then_inc(s["rk"], 1)

            def tail(b, par):
                pe.wait_ge(s["kact"], b + 1)
                for j in range(TPB):
                    last = nc.tensor.matmul(ps[:, 6 + par, j * P:(j + 1) * P], kact[:, par, 1, j * P:(j + 1) * P],
                                            w("L1_ffn_W_v"), start=True, stop=True)
                last.then_inc(s["v"], 1)
            batches(pe, lambda b, par: front_tensor(pe, s, b, par), heavy, tail, tail_first=True)

        UNITS = {"L0_attn_": TPB, "L1_attn_": TPB * TPB}
        NBUF = 4

        def overlapped(eng, prologue, body, epilogue):
            prologue()
            for b in range(3):
                body(b, b % 2, False)
            with eng.Fori(1, B // 2 - 1) as i:
                body(i * 2 + 1, 1, False)
                body(i * 2 + 2, 0, False)
            body(B - 1, 1, True)
            epilogue()

        def has(b, back):
            return not isinstance(b, int) or b >= back

        def attn_tokens_tensor(pe, s, l, b, par):
            after(pe, s["vm"], b * TPB)
            if l == L0:
                after(pe, s["vfull"], b)
                after(pe, s["kd"], b)
            front_tensor(pe, s, b, par, 2)

        def attn_qk_tensor(pe, s, l, b, par):
            pe.wait_ge(s["xT"], b + 1)
            after(pe, s["k4"], b * ROUNDS)
            x = xT[:, par, 1:S + 1]
            nc.tensor.matmul(ps[:, 1, 0:S], w(l + "Wq"), x, start=True, stop=True)
            nc.tensor.matmul(ps[:, 1, S:2 * S], w(l + "Wk"), x, start=True, stop=True).then_inc(s["qk_ps"], 1)

        def attn_v_tensor(pe, s, l, b, par):
            pe.wait_ge(s["xT"], b + 1)
            for j in range(TPB):
                last = nc.tensor.matmul(ps[:, 2, j * P:(j + 1) * P], xT[:, par, 1 + j * P:1 + (j + 1) * P], w(l + "Wv"),
                                        start=True, stop=True)
            if l == L0:
                last = nc.tensor.matmul(ps[:, 2, 2 * P:3 * P], xT[:, par, 1:1 + P], w(l + "Wk"), start=True, stop=True)
            last.then_inc(s["v_ps"], 1)

        def attn_tokens_scalar(act, s, b, par):
            two_before(act, s["v_ps"], b)
            front_scalar(act, s, b, par, 2)

        def attn_qk_scalar(act, s, l, b, par):
            act.wait_ge(s["qk_ps"], b + 1)
            two_before(act, s["lo"], b)
            if l == L0:
                two_before(act, s["qd"], b)
            two_before(act, s["copied"], b, ROUNDS)
            for dst in (qk[:, par], qk_part[:, par, 0]):
                for which, bias in ((0, "bq"), (1, "bk")):
                    nc.scalar.activation(dst[:, which, :], ps[:, 1, which * S:(which + 1) * S], ACT.Identity,
                                         bias=vec(l + bias)).then_inc(s["q"], 1)

        def attn_parts_vector(dve, s, b, par):
            dve.wait_ge(s["q"], b * 4 + 4)
            two_before(dve, s["copied"], b, ROUNDS)
            nc.vector.tensor_tensor(qk_part[:, par, 1], qk[:, par], qk_part[:, par, 0], ALU.subtract).then_inc(s["lo"], 1)

        ROUNDS = 4

        def copy_tensor(pe, s, b, par, n):
            which = n // 2
            pe.wait_ge(s["lo"], b + 1)
            if n:
                pe.wait_ge(s["k4"], b * ROUNDS + n)
            for j in range(2):
                for part in range(2):
                    last = nc.tensor.matmul(ps[:, 1, j * S:(j + 1) * S], copying[:, which, n % 2 * 2 + j, part, :],
                                            qk_part[:, par, part, which, :], start=(part == 0), stop=(part == 1))
            last.then_inc(s["copied"], 1)

        def copy_scalar(act, s, l, b, par, n):
            act.wait_ge(s["copied"], b * ROUNDS + n + 1)
            two_before(act, s["sc"], b, UNITS[l] * HR)
            two_before(act, s["qm"], b, HR)
            groups = slice(n % 2 * 2, n % 2 * 2 + 2)
            dst = q4 if n < 2 else K4
            nc.scalar.copy(dst[:, par, groups].rearrange("p g s -> p (g s)"), ps[:, 1, :]).then_inc(s["k4"], 1)

        def queries_by_head(eng, s, l, b, par, parts):
            eng.wait_ge(s["k4"], b * ROUNDS + 2)
            two_before(eng, s["sc"], b, UNITS[l] * HR)
            for r in parts:
                dst, all_heads = (x.rearrange("p g s -> p (g s)") for x in (Q4[:, par, r], q4[:, par]))
                if l == L0:
                    ins = nc.vector.tensor_scalar(dst, all_heads, head_of[:, r:r + 1], None, ALU.mult)
                else:
                    ins = nc.scalar.activation(dst, all_heads, ACT.Identity, scale=head_of[:, r:r + 1])
                ins.then_inc(s["qm"], 1)

        def attn_out_scalar(act, s, l, b, par):
            act.wait_ge(s["av"], b * UNITS[l] + UNITS[l])
            two_before(act, s["yps"], b)
            nc.scalar.copy(oT[:, par, :], ps[:, 7, 0:S]).then_inc(s["oT"], 1)

        def values_vector(dve, s, l, b, par):
            dve.wait_ge(s["v_ps"], b + 1)
            two_before(dve, s["av"], b, UNITS[l])
            bias = row(l + "bv")
            for j in range(TPB):
                dst = Vm[:, par, j].rearrange("p (g r) (q d) -> p g (r q) d", r=HR, q=HR)[:, :, 0:HR * HR:HR + 1, :]
                src = ps[:, 2, j * P:(j + 1) * P].rearrange("p (g r d) -> p g r d", g=HG, r=HR)
                nc.vector.tensor_tensor(dst, src, bias.rearrange("p (g r d) -> p g r d", g=HG, r=HR),
                                        ALU.add).then_inc(s["vm"], 1)
            if l == L0:
                nc.vector.tensor_tensor(Vfull[:, par, :], ps[:, 2, 0:P], bias, ALU.add).then_inc(s["vfull"], 1)
                nc.vector.scalar_tensor_tensor(Kd[:, par, :], ps[:, 2, 2 * P:3 * P], k_decay, bk_decay[:, :],
                                               ALU.mult, ALU.add).then_inc(s["kd"], 1)

        def weigh_values(pe, s, par, keys, queries, buf, first, ready):
            for r in range(HR):
                pe.wait_ge(ready[r][0], ready[r][1])
                for g in range(HG):
                    last = nc.tensor.matmul(ps[g * MW:(g + 1) * MW, 7, queries * P:(queries + 1) * P],
                                            Vm[:, par, keys, g * HR + r, :], att[:, buf, r, g, :],
                                            start=(first and r == 0), stop=(r == HR - 1),
                                            skip_group_check=True)
            last.then_inc(s["av"], 1)

        L0 = "L0_attn_"

        def attn0_tensor(pe, s, before):
            def state(b, par):
                after(pe, s["oT"], b)
                pe.wait_ge(s["kd"], b + 1)
                pe.wait_ge(s["vfull"], b + 1)
                nc.tensor.matmul(ps[:, 7, S:S + P], Kd[:, par, :], Vfull[:, par, :], start=True,
                                 stop=True).then_inc(s["st_ps"], 1)

            def values(b, par, u):
                n = b * TPB + u
                pe.wait_ge(s["vm"], b * TPB + TPB)
                pe.wait_ge(s["st"], b + 1)
                if u == 1:
                    pe.wait_ge(s["qd"], b + 1)
                    nc.tensor.matmul(ps[:, 7, P:2 * P], St[:, par, :], qD[:, par, :], start=True, stop=False,
                                     skip_group_check=True)
                weigh_values(pe, s, par, u, u, 2 * par + u, u == 0, [(s["at"], n * HR + r + 1) for r in range(HR)])

            def output(b, par):
                pe.wait_ge(s["oT"], b + 1)
                after(pe, s["x_done"], b)
                nc.tensor.matmul(ps[:, 0, 0:S], w(L0 + "Wo"), oT[:, par, :], start=True, stop=True).then_inc(s["yps"], 1)

            def head_mean(b):
                pe.wait_ge(s["ym"], b + 1)
                nc.tensor.matmul(ps[:, 0, S:S + 1], block_avg[:, :], gst[:, 2:3], start=True, stop=True).then_inc(s["gm_ps"], 1)

            def head_variance(b):
                pe.wait_ge(s["dev"], b + 1)
                nc.tensor.matmul(ps[:, 0, S:S + 1], block_avg[:, :], gst[:, 4:5], start=True, stop=True).then_inc(s["gv_ps"], 1)

            def turn_output(b):
                pe.wait_ge(s["yn"], b + 1)
                nc.tensor.transpose(ps[:, 0, 0:P], yT[:, 0:P], ident)
                nc.tensor.transpose(ps[:, 0, P:S], yT[:, P:S], ident).then_inc(s["ynT"], 1)

            def prologue():
                pe.wait_ge(*before)
                attn_tokens_tensor(pe, s, L0, 0, 0)
                attn_qk_tensor(pe, s, L0, 0, 0)
                attn_v_tensor(pe, s, L0, 0, 0)
                for n in range(ROUNDS):
                    copy_tensor(pe, s, 0, 0, n)

            def body(b, par, last):
                def scores(u, r):
                    pe.wait_ge(s["qm"], b * HR + r + 1)
                    pe.wait_ge(s["k4"], b * ROUNDS + ROUNDS)
                    after(pe, s["at"], (b * TPB + u - 1) * HR + r + 1)
                    for g in range(HG):
                        last = nc.tensor.matmul(ps[:, 3 + r, g * P:(g + 1) * P], K4[:, par, g, u * P:(u + 1) * P],
                                                Q4[:, par, r, g, u * P:(u + 1) * P], start=True, stop=True)
                    last.then_inc(s["sc"], 1)
                scores(0, 0)
                if has(b, 1):
                    values(b - 1, 1 - par, 1)
                scores(0, 1)
                if not last:
                    attn_tokens_tensor(pe, s, L0, b + 1, 1 - par)
                if has(b, 2):
                    turn_output(b - 2)
                scores(0, 2)
                state(b, par)
                scores(0, 3)
                if has(b, 1):
                    output(b - 1, 1 - par)
                if not last:
                    attn_qk_tensor(pe, s, L0, b + 1, 1 - par)
                scores(1, 0)
                if not last:
                    attn_v_tensor(pe, s, L0, b + 1, 1 - par)
                scores(1, 1)
                if has(b, 1):
                    head_mean(b - 1)
                if not last:
                    copy_tensor(pe, s, b + 1, 1 - par, 0)
                scores(1, 2)
                if not last:
                    copy_tensor(pe, s, b + 1, 1 - par, 1)
                scores(1, 3)
                if not last:
                    copy_tensor(pe, s, b + 1, 1 - par, 2)
                values(b, par, 0)
                if not last:
                    copy_tensor(pe, s, b + 1, 1 - par, 3)
                if has(b, 1):
                    head_variance(b - 1)

            def epilogue():
                values(B - 1, 1, 1)
                turn_output(B - 2)
                output(B - 1, 1)
                head_mean(B - 1)
                head_variance(B - 1)
                turn_output(B - 1)
            overlapped(pe, prologue, body, epilogue)

        def attn0_scalar(act, s, turn):
            norm_scalar(act, turn)

            def root(b):
                act.wait_ge(s["gv"], b + 1)
                nc.scalar.activation(gst[:, 6:7], gst[:, 5:6], ACT.Sqrt).then_inc(s["groot"], 1)

            def prologue():
                attn_tokens_scalar(act, s, 0, 0)
                attn_qk_scalar(act, s, L0, 0, 0)
                for n in range(ROUNDS):
                    copy_scalar(act, s, L0, 0, 0, n)

            def body(b, par, last):
                if has(b, 1):
                    attn_out_scalar(act, s, L0, b - 1, 1 - par)
                if not last:
                    attn_tokens_scalar(act, s, b + 1, 1 - par)
                    attn_qk_scalar(act, s, L0, b + 1, 1 - par)
                    for n in range(ROUNDS):
                        copy_scalar(act, s, L0, b + 1, 1 - par, n)
                if has(b, 1):
                    root(b - 1)

            def epilogue():
                attn_out_scalar(act, s, L0, B - 1, 1)
                root(B - 1)
            overlapped(act, prologue, body, epilogue)

        def attn0_vector(dve, s, turn, before):
            norm_vector(dve, turn, before)
            v = nc.vector
            col = [gst[:, n:n + 1] for n in range(10)]

            def weights(b, par, u, r):
                n = b * TPB + u
                dve.wait_ge(s["sc"], n * HR + r + 1)
                after(dve, s["av"], n - NBUF + 1)
                v.tensor_tensor(att[:, 2 * par + u, r], ps[:, 3 + r, :].rearrange("p (g q) -> p g q", g=HG),
                                decay_mask.unsqueeze(1).broadcast_to([P, HG, P]), ALU.mult).then_inc(s["at"], 1)

            def channel_stats(b):
                dve.wait_ge(s["yps"], b + 1)
                v.bn_stats(gbn[:, :], ps[:, 0, 0:S]).then_inc(s["ymv"], 1)
                dve.wait_ge(s["ymv"], b * 5 + 1)
                v.tensor_tensor(col[0], gbn[:, 1:2], gbn[:, 4:5], ALU.add).then_inc(s["ymv"], 1)
                dve.wait_ge(s["ymv"], b * 5 + 2)
                v.scalar_tensor_tensor(col[2], col[0], 0.5, vec(L0 + "bo"), ALU.mult, ALU.add).then_inc(s["ym"], 1)
                v.tensor_tensor(col[1], gbn[:, 1:2], gbn[:, 4:5], ALU.subtract).then_inc(s["ymv"], 1)
                v.tensor_tensor(col[7], gbn[:, 2:3], gbn[:, 5:6], ALU.add).then_inc(s["ymv"], 1)
                dve.wait_ge(s["ymv"], b * 5 + 4)
                v.scalar_tensor_tensor(col[8], col[1], 0.25, col[1], ALU.mult, ALU.mult).then_inc(s["ymv"], 1)
                dve.wait_ge(s["ymv"], b * 5 + 5)
                v.scalar_tensor_tensor(col[1], col[7], 1.0 / S, col[8], ALU.mult, ALU.add).then_inc(s["yvar"], 1)

            def deviation(b):
                dve.wait_ge(s["gm_ps"], b + 1)
                v.tensor_tensor(col[3], col[2], ps[:, 0, S:S + 1], ALU.subtract).then_inc(s["gm"], 1)
                dve.wait_ge(s["gm"], b + 1)
                dve.wait_ge(s["yvar"], b + 1)
                v.scalar_tensor_tensor(col[4], col[3], col[3], col[1], ALU.mult, ALU.add).then_inc(s["dev"], 1)

            def scale_output(b):
                dve.wait_ge(s["gv_ps"], b + 1)
                v.tensor_scalar(col[5], ps[:, 0, S:S + 1], EPS, None, ALU.add).then_inc(s["gv"], 1)
                v.scalar_tensor_tensor(col[9], col[0], -0.5, col[3], ALU.mult, ALU.add).then_inc(s["ab"], 1)
                dve.wait_ge(s["groot"], b + 1)
                v.reciprocal(col[7], col[6]).then_inc(s["grs"], 1)
                dve.wait_ge(s["grs"], b + 1)
                v.tensor_tensor(col[8], col[7], vec(L0 + "gamma"), ALU.mult).then_inc(s["ab"], 1)
                dve.wait_ge(s["ab"], b * 3 + 2)
                v.scalar_tensor_tensor(col[2], col[8], col[9], vec(L0 + "beta"), ALU.mult, ALU.add).then_inc(s["ab"], 1)
                dve.wait_ge(s["ab"], b * 3 + 3)
                v.tensor_scalar(yT[:, :], ps[:, 0, 0:S], col[8], col[2], ALU.mult, ALU.add).then_inc(s["yn"], 1)

            def update(b):
                dve.wait_ge(s["ynT"], b + 1)
                update_batch(dve, s, b, ps[:, 0, 0:S])

            def prologue():
                front_vector(dve, s, 0, 0)
                attn_parts_vector(dve, s, 0, 0)
                values_vector(dve, s, L0, 0, 0)
                queries_by_head(dve, s, L0, 0, 0, range(HR))

            def body(b, par, last):
                if not last:
                    front_vector(dve, s, b + 1, 1 - par)
                weights(b, par, 0, 0)
                dve.wait_ge(s["q"], b * 4 + 1)
                two_before(dve, s["av"], b, TPB)
                v.tensor_tensor(qD[:, par, :], qk[:, par, 0, P:S], q_decay, ALU.mult).then_inc(s["qd"], 1)
                weights(b, par, 0, 1)
                if has(b, 2):
                    update(b - 2)
                weights(b, par, 0, 2)
                dve.wait_ge(s["st_ps"], b + 1)
                v.tensor_tensor(St[:, par, :], ps[:, 7, S:S + P], block_diag, ALU.mult).then_inc(s["st"], 1)
                weights(b, par, 0, 3)
                weights(b, par, 1, 0)
                if has(b, 1):
                    channel_stats(b - 1)
                if not last:
                    attn_parts_vector(dve, s, b + 1, 1 - par)
                weights(b, par, 1, 1)
                if not last:
                    values_vector(dve, s, L0, b + 1, 1 - par)
                weights(b, par, 1, 2)
                if has(b, 1):
                    deviation(b - 1)
                weights(b, par, 1, 3)
                if not last:
                    queries_by_head(dve, s, L0, b + 1, 1 - par, range(HR))
                if has(b, 1):
                    scale_output(b - 1)

            def epilogue():
                update(B - 2)
                channel_stats(B - 1)
                deviation(B - 1)
                scale_output(B - 1)
                update(B - 1)
            overlapped(dve, prologue, body, epilogue)

        L1 = "L1_attn_"
        NU = UNITS[L1]
        LAG = 3

        def attn1_tensor(pe, s, before):
            def values(b, par, u):
                n = b * NU + u
                if u == 0:
                    after(pe, s["oT"], b)
                    pe.wait_ge(s["vm"], b * TPB + TPB)
                ready = [(s["at"], n * HR + r + 1) for r in range(HR)]
                weigh_values(pe, s, par, u % TPB, u // TPB, u, u % TPB == 0, ready)

            def output(b, par):
                pe.wait_ge(s["oT"], b + 1)
                after(pe, s["x_done"], b)
                for j in range(TPB):
                    nc.tensor.matmul(ps[:, 0, j * P:(j + 1) * P], oT[:, par, j * P:(j + 1) * P], w(L1 + "Wo"),
                                     start=True, stop=False)
                    last = nc.tensor.matmul(ps[:, 0, j * P:(j + 1) * P], ones[:, :], row(L1 + "bo")[0:1, :],
                                            start=False, stop=True)
                last.then_inc(s["yps"], 1)

            def prologue():
                pe.wait_ge(*before)
                attn_tokens_tensor(pe, s, L1, 0, 0)
                attn_qk_tensor(pe, s, L1, 0, 0)
                attn_v_tensor(pe, s, L1, 0, 0)
                for n in range(ROUNDS):
                    copy_tensor(pe, s, 0, 0, n)

            def scores(b, par, u, half):
                n = b * NU + u
                keys, q0 = u % TPB * P, u // TPB * P + half * QH
                for k in range(2):
                    pe.wait_ge(s["qm"], b * HR + 2 * k + 2)
                    pe.wait_ge(s["k4"], b * ROUNDS + ROUNDS)
                    after(pe, s["ex"], (n - 1) * HR + 2 * half + k + 1)
                    by_group = ps[:, 3 + 2 * half + k, :].rearrange("p (r g q) -> p g r q", r=2, g=HG)
                    for g in range(HG):
                        last = nc.tensor.matmul(by_group[:, g], K4[:, par, g, keys:keys + P],
                                                Q4[:, par, 2 * k:2 * k + 2, g, q0:q0 + QH],
                                                start=(g == 0), stop=True,
                                                skip_group_check=True)
                    last.then_inc(s["sc"], 1)

            def subtract(n, half):
                pe.wait_ge(s["mx"], n * 2 + half + 1)
                for k in range(2):
                    nc.tensor.matmul(ps[:, 3 + 2 * half + k, :], minus_i[:, :],
                                     amax[:, half, :].unsqueeze(1).broadcast_to([P, 2 * HG, QH]),
                                     start=False, stop=True, skip_group_check=True).then_inc(s["sub"], 1)

            def body(b, par, last):
                for u in range(NU):
                    n = b * NU + u
                    scores(b, par, u, 0)
                    if has(b, 1) or u:
                        subtract(n - 1, 1)
                    if u == 0 and not last:
                        attn_tokens_tensor(pe, s, L1, b + 1, 1 - par)
                    if u == 1 and not last:
                        attn_v_tensor(pe, s, L1, b + 1, 1 - par)
                    scores(b, par, u, 1)
                    if u in (1, 2) and not last:
                        copy_tensor(pe, s, b + 1, 1 - par, 2 * u - 2)
                        copy_tensor(pe, s, b + 1, 1 - par, 2 * u - 1)
                    subtract(n, 0)
                    if u == 0 and not last:
                        attn_qk_tensor(pe, s, L1, b + 1, 1 - par)
                    if u == 3 and has(b, 1):
                        output(b - 1, 1 - par)
                    if u >= LAG:
                        values(b, par, u - LAG)
                    elif has(b, 1):
                        values(b - 1, 1 - par, u + NU - LAG)

            def epilogue():
                subtract(B * NU - 1, 1)
                for u in range(NU - LAG, NU):
                    values(B - 1, 1, u)
                output(B - 1, 1)
            overlapped(pe, prologue, body, epilogue)

        def attn1_scalar(act, s, turn):
            norm_scalar(act, turn)

            def prologue():
                attn_tokens_scalar(act, s, 0, 0)
                attn_qk_scalar(act, s, L1, 0, 0)
                for n in range(ROUNDS):
                    copy_scalar(act, s, L1, 0, 0, n)
                queries_by_head(act, s, L1, 0, 0, range(HR))

            def exponentials(n, u, half):
                after(act, s["av"], n - NBUF + 1)
                for k in range(2):
                    act.wait_ge(s["sub"], n * HR + 2 * half + k + 1)
                    nc.scalar.activation(att[:, u, 2 * k:2 * k + 2, :, half * QH:(half + 1) * QH].rearrange("p r g q -> p (r g) q"),
                                         ps[:, 3 + 2 * half + k, :].rearrange("p (h q) -> p h q", q=QH), ACT.Exp,
                                         scale=SCALE).then_inc(s["ex"], 1)

            def body(b, par, last):
                for u in range(NU):
                    n = b * NU + u
                    if has(b, 1) or u:
                        exponentials(n - 1, (u - 1) % NBUF, 1)
                    if u >= 2 and not last:
                        queries_by_head(act, s, L1, b + 1, 1 - par, (2 * u - 3,))
                    if u == 0 and not last:
                        attn_tokens_scalar(act, s, b + 1, 1 - par)
                    if u == 3 and has(b, 1):
                        attn_out_scalar(act, s, L1, b - 1, 1 - par)
                    if u in (1, 2) and not last:
                        copy_scalar(act, s, L1, b + 1, 1 - par, 2 * u - 2)
                        copy_scalar(act, s, L1, b + 1, 1 - par, 2 * u - 1)
                    exponentials(n, u, 0)
                    if u in (1, 2) and not last:
                        queries_by_head(act, s, L1, b + 1, 1 - par, (2 * u - 2,))
                    if u == 0 and not last:
                        attn_qk_scalar(act, s, L1, b + 1, 1 - par)

            def epilogue():
                exponentials(B * NU - 1, NBUF - 1, 1)
                attn_out_scalar(act, s, L1, B - 1, 1)
            overlapped(act, prologue, body, epilogue)

        def attn1_pool(pool, s):
            def normalise(b, u):
                pool.wait_ge(s["rden"], b * NU + u + 1)
                for r in range(HR):
                    nc.gpsimd.tensor_tensor(att[:, u, r], att[:, u, r], rden[:, u % 2, :].unsqueeze(1).broadcast_to([P, HG, P]),
                                            ALU.mult).then_inc(s["at"], 1)

            def body(b, par, last):
                for u in range(NU):
                    if u:
                        normalise(b, u - 1)
                    elif has(b, 1):
                        normalise(b - 1, NU - 1)
            overlapped(pool, lambda: None, body, lambda: normalise(B - 1, NU - 1))

        def attn1_vector(dve, s, turn, before):
            norm_vector(dve, turn, before)
            v = nc.vector

            def largest(n, half):
                m = n * 2 + half
                dve.wait_ge(s["sc"], n * HR + 2 * half + 2)
                after(dve, s["sub"], (m - 1) * 2)
                v.tensor_reduce(amax[:, half, :], ps[:, 3 + 2 * half:5 + 2 * half, :].rearrange("p k (h q) -> p q (k h)", q=QH),
                                AX_X, ALU.max).then_inc(s["mx"], 1)

            def sum_heads(n, u, half):
                dve.wait_ge(s["ex"], n * HR + 2 * half + 2)
                v.tensor_reduce(den[:, u % 2, half * QH:(half + 1) * QH],
                                att[:, u, :, :, half * QH:(half + 1) * QH].rearrange("p r g q -> p q (r g)"), AX_X,
                                ALU.add).then_inc(s["den"], 1)

            def invert(n, u):
                dve.wait_ge(s["den"], n * 2 + 2)
                after(dve, s["at"], (n - 1) * HR)
                v.reciprocal(rden[:, u % 2, :], den[:, u % 2, :]).then_inc(s["rden"], 1)

            def update(b):
                dve.wait_ge(s["yps"], b + 1)
                update_batch(dve, s, b, ps[:, 0, 0:S])

            def prologue():
                front_vector(dve, s, 0, 0)
                attn_parts_vector(dve, s, 0, 0)
                values_vector(dve, s, L1, 0, 0)

            def body(b, par, last):
                if not last:
                    front_vector(dve, s, b + 1, 1 - par)
                for u in range(NU):
                    n = b * NU + u
                    largest(n, 0)
                    if has(b, 1) or u >= 1:
                        sum_heads(n - 1, (u - 1) % NU, 0)
                    if u == 3 and not last:
                        values_vector(dve, s, L1, b + 1, 1 - par)
                    largest(n, 1)
                    if has(b, 1) or u >= 1:
                        sum_heads(n - 1, (u - 1) % NU, 1)
                        invert(n - 1, (u - 1) % NU)
                    if u == 0 and not last:
                        attn_parts_vector(dve, s, b + 1, 1 - par)
                    if u == 3 and has(b, 1):
                        update(b - 1)

            def epilogue():
                n = B * NU - 1
                sum_heads(n, NU - 1, 0)
                sum_heads(n, NU - 1, 1)
                invert(n, NU - 1)
                update(B - 1)
            overlapped(dve, prologue, body, epilogue)

        moe1, moe2, rwkv1, rwkv2 = MO["moe1"], MO["moe2"], RW["rwkv1"], RW["rwkv2"]
        attn0, attn1 = AT["attn0"], AT["attn1"]

        kept = [nc.dram_tensor(f"kept{n}", (TILES * P, D), F32, kind="Internal").ap() for n in range(2)]
        back = [nc.dram_tensor(f"back{n}", ((PAIRS + SLOT_TILES) * P, D), F32, kind="Internal").ap() for n in range(2)]

        block = ctx.enter_context(nc.Block())

        @block.sync
        def _(sp):
            for n in range(4):
                sp.dma_start(X[:, n * 4:(n + 1) * 4, :],
                             io["x"][n * 4 * P:(n + 1) * 4 * P, :].rearrange("(t p) d -> p t d", p=P)).then_inc(x_piece[n], 16)
            sp.dma_start(gateT[:, :], io["gateT"]).then_inc(ld["small"], 16)
            sp.dma_start(rows[:, :, :], io["rows"].broadcast_to([P, len(R_NAMES), D])).then_inc(ld["small"], 16)
            for n, moe in enumerate((moe1, moe2)):
                keep_tokens(sp, moe, kept[n])
                if n == 0:
                    sp.dma_start(W1[:, :, :], io["w1"]).then_inc(ld["moe"], 16)
                    sp.dma_start(W3[:, :, :], io["w3"]).then_inc(ld["moe"], 16)
                    sp.dma_start(W2[:, :, :, :], io["w2"]).then_inc(ld["moe"], 16)
                    sp.dma_start(W[:, :, :], io["weights"]).then_inc(ld["w"], 16)
                fetch_outputs(sp, moe, n, back[n])
            for b in range(B):
                sp.wait_ge(rwkv2["x_done"], b + 1)
                sp.dma_start(out[b].rearrange("(t p) d -> p t d", p=P),
                             X[:, b * TPB:(b + 1) * TPB, :]).then_inc(final["stored"], 16)
            sp.wait_ge(final["stored"], 16 * B)

        @block.gpsimd
        def _(pool):
            nc.gpsimd.memset(ones[:, :], 1.0)
            nc.gpsimd.memset(all_ones[:, :], 1.0)
            nc.gpsimd.memset(run[:, :, 0:PAD, :], 0.0)
            nc.gpsimd.memset(xT[:, :, 0:1], 0.0)
            nc.gpsimd.memset(Vm[:, :, :, :, :], 0.0).then_inc(su["zeros"], 1)
            claim_pool(pool, 0)
            moe_pool(pool, moe1, 0, kept[0], back[0])
            claim_pool(pool, 1)
            moe_pool(pool, moe2, 1, kept[1], back[1])
            attn1_pool(pool, attn1)

        @block.vector
        def _(dve):
            dve.wait_ge(ld["const"], 32)
            dve.wait_ge(su["zeros"], 1)
            nc.vector.tensor_scalar(omu[:, :], vecs[:, len(V_NAMES) - 2:], -1.0, 1.0, ALU.mult, ALU.add)
            nc.vector.tensor_copy(lane16[:, :], lane)
            nc.vector.tensor_copy(pair_parts[:, :, :], consts[:, C_PAIR:C_PAIR + 2 * PAIRS].rearrange("p (n k) -> p n k", k=2))
            nc.vector.tensor_scalar(minus_i[:, :], ident, -1.0, None, ALU.mult)
            nc.vector.tensor_scalar(block_avg[:, :], block_diag, 1.0 / HD, None, ALU.mult).then_inc(su["consts"], 1)
            dve.wait_ge(su["consts"], 1)
            for t in range(TILES):
                dve.wait_ge(x_piece[t // KEEP], 16)
                tile_stats(dve, su, t, None)
            moe_front_vector(dve, moe1, 0, 0, (su["stats"], TILES))
            moe_vector(dve, moe1, 0)
            dve.wait_ge(ld["small"], 32)
            nc.vector.tensor_scalar(bk_decay[:, :], row(L0 + "bk"), k_decay, None, ALU.mult).then_inc(su["consts"], 1)
            dve.wait_ge(su["consts"], 2)
            attn0_vector(dve, attn0, 1, (moe1["stats"], TILES))
            moe_front_vector(dve, moe2, 1, 2, (attn0["stats"], TILES))
            moe_vector(dve, moe2, 1)
            rwkv_vector(dve, rwkv1, 3, (moe2["stats"], TILES), True)
            attn1_vector(dve, attn1, 4, (rwkv1["stats"], TILES))
            rwkv_vector(dve, rwkv2, 5, (attn1["stats"], TILES), False)

        @block.scalar
        def _(act):
            act.dma_start(consts[:, :], io["consts"]).then_inc(ld["const"], 16)
            act.dma_start(vecs[:, :], io["vecs"]).then_inc(ld["const"], 16)
            act.dma_start(copying[:, :, :, :, :], io["copying"]).then_inc(ld["copying"], 16)
            act.wait_ge(ld["const"], 32)
            moe_front_scalar(act, moe1, 0, 0)
            claim_scalar(act, 0)
            moe_scalar(act, 0)
            attn0_scalar(act, attn0, 1)
            moe_front_scalar(act, moe2, 1, 2)
            claim_scalar(act, 1)
            moe_scalar(act, 1)
            rwkv_scalar(act, rwkv1, 3)
            attn1_scalar(act, attn1, 4)
            rwkv_scalar(act, rwkv2, 5)

        @block.tensor
        def _(pe):
            pe.wait_ge(ld["const"], 32)
            pe.wait_ge(ld["small"], 32)
            pe.wait_ge(su["consts"], 1)
            moe_front_tensor(pe, moe1, (su["stats"], TILES))
            dispatch_tensor(pe, moe1, 0)
            pe.wait_ge(ld["moe"], 48)
            moe_tensor(pe, 0)
            pe.wait_ge(ld["w"], 16)
            pe.wait_ge(ld["copying"], 16)
            attn0_tensor(pe, attn0, (moe1["stats"], TILES))
            moe_front_tensor(pe, moe2, (attn0["stats"], TILES))
            dispatch_tensor(pe, moe2, 1)
            moe_tensor(pe, 1)
            rwkv_tensor(pe, rwkv1, (moe2["stats"], TILES))
            attn1_tensor(pe, attn1, (rwkv1["stats"], TILES))
            rwkv_tensor(pe, rwkv2, (attn1["stats"], TILES))


def kernel(**inputs):
    import concourse.bacc as bacc
    from concourse.bass_utils import run_bass_kernel_spmd as run

    a = {n: np.asarray(v) for n, v in inputs.items()}
    arrays = {
        "x": a["L0_attn_x"].reshape(B * S, D),
        "consts": shape_constants(),
        "copying": copying_matrices(),
        "vecs": np.stack([a[n] for n in V_NAMES], axis=1),
        "rows": np.stack([a[n] for n in R_NAMES])[None],
        "weights": np.stack([a[n] for n in W_NAMES] + [a[n].T for n in WT_NAMES], axis=1),
        "gateT": a["L0_ffn_gate_w"].T,
        "w1": a["L0_ffn_w1"].transpose(1, 0, 2),
        "w3": a["L0_ffn_w3"].transpose(1, 0, 2),
        "w2": a["L0_ffn_w2"].reshape(E, NCH, IC, D).transpose(2, 0, 1, 3),
    }
    arrays = {n: np.ascontiguousarray(v) for n, v in arrays.items()}
    nc = bacc.Bacc("TRN2", target_bir_lowering=False, num_devices=1)
    io = {n: nc.dram_tensor(f"in_{n}", v.shape, mybir.dt.from_np(v.dtype), kind="ExternalInput").ap()
          for n, v in arrays.items()}
    out = nc.dram_tensor("out_0", (B, S, D), F32, kind="ExternalOutput").ap()
    build(nc, io, out)
    r = run(nc, [{f"in_{n}": v for n, v in arrays.items()}], core_ids=[0])
    return r.results[0]["out_0"]
```
